# Optimizing a Trainium2 kernel written in Bass

```python
import numpy as np
import jax
import jax.numpy as jnp

def _softmax(x, axis=-1):
    return jax.nn.softmax(x, axis=axis)

def _gelu(x):
    return jax.nn.gelu(x, approximate=True)

def _silu(x):
    return jax.nn.silu(x)

def _sigmoid(x):
    return jax.nn.sigmoid(x)

def _layernorm(x, axis=-1, eps=1e-05):
    m = jnp.mean(x, axis=axis, keepdims=True)
    v = jnp.var(x, axis=axis, keepdims=True)
    return (x - m) / jnp.sqrt(v + eps)

def _scatter_add(tgt, idx, src, axis=0):
    return tgt.at[idx].add(src)

def _segment_sum(src, seg, n):
    return jax.ops.segment_sum(src, seg, n)
kernel_name = 'mk_flamingo_gated_d2_seqx_r4_9062c3'

def setup_inputs(seed: int=0):
    np.random.seed(seed)
    _w = jnp.asarray

    def _rec_inputs():
        import jax
        import jax.numpy as jnp
        _rk = jax.random.key(seed)
        x = 4.136e-05 + 0.9999 * jax.random.normal(jax.random.fold_in(_rk, 1), (4, 512, 512), jnp.float32)
        _lenS = 512 - jax.random.randint(jax.random.fold_in(_rk, 7), (4,), 0, max(1, 512 // 4) + 1, jnp.int32)
        _lenS2 = 512 - jax.random.randint(jax.random.fold_in(_rk, 8), (4,), 0, max(1, 512 // 4) + 1, jnp.int32)
        _ctx_1024P = jax.random.normal(jax.random.fold_in(_rk, 11), (4, 16, 256), jnp.float32)
        _ctx_1024c = jax.random.dirichlet(jax.random.fold_in(_rk, 511), 0.3 * jnp.ones((16,), jnp.float32), (4, 512))
        _ctx_1024t = jnp.einsum('bsk,bkd->bsd', _ctx_1024c, _ctx_1024P)
        _ctx_1024t = _ctx_1024t * jax.lax.rsqrt(jnp.mean(jnp.square(_ctx_1024t)) + 1e-12) * 0.953939
        ctx_1024 = -0.000292821 + 1.00034 * (_ctx_1024t + 0.3 * jax.random.normal(jax.random.fold_in(_rk, 611), (4, 512, 256), jnp.float32))
        _g = jax.random.normal(jax.random.fold_in(_rk, 9001), (2, 2), jnp.float32)
        _g = jnp.sign(_g) * jnp.maximum(jnp.abs(_g), 1.0) + (_g == 0) * 1.0
        g_xattn = _g[0]
        g_ffn = _g[1]
        return (x, ctx_1024, g_xattn, g_ffn)
    x, ctx_1024, g_xattn, g_ffn = _rec_inputs()

    def _L0_xattn_setup():
        import jax, jax.numpy as jnp
        import numpy as np
        import math
        B, L, DM = (2, 512, 256)
        DS, DC, EXP = (16, 4, 2)
        DI = EXP * DM
        DR = math.ceil(DM / 16)
        DT_MIN, DT_MAX, DT_FLOOR = (0.001, 0.1, 0.0001)

        def _ssm_forward(hidden_states, z, in_proj_w, conv_w, conv_b, x_proj_w, dt_proj_w, dt_proj_b, A_log, D):
            b = hidden_states.shape[0]
            x = jnp.einsum('ed,bld->bel', in_proj_w, hidden_states)
            xp = jnp.pad(x, ((0, 0), (0, 0), (DC - 1, 0)))
            xc = jax.lax.conv_general_dilated(xp, conv_w[:, None, :], window_strides=(1,), padding='VALID', dimension_numbers=('NCH', 'OIH', 'NCH'), feature_group_count=DI)
            u = jax.nn.silu(xc + conv_b[None, :, None])
            x_dbl = jnp.einsum('ke,bel->bkl', x_proj_w, u)
            dt_lo = x_dbl[:, :DR]
            Bm = x_dbl[:, DR:DR + DS]
            Cm = x_dbl[:, DR + DS:]
            delta = jax.nn.softplus(jnp.einsum('er,brl->bel', dt_proj_w, dt_lo) + dt_proj_b[None, :, None])
            A = -jnp.exp(A_log)

            def step(state, xs):
                d_t, B_t, C_t, u_t = xs
                dA = jnp.exp(d_t[..., None] * A)
                state = state * dA + (d_t * u_t)[..., None] * B_t[:, None, :]
                y_t = jnp.einsum('ben,bn->be', state, C_t)
                return (state, y_t)
            xs = (jnp.moveaxis(delta, -1, 0), jnp.moveaxis(Bm, -1, 0), jnp.moveaxis(Cm, -1, 0), jnp.moveaxis(u, -1, 0))
            state0 = jnp.zeros((b, DI, DS), delta.dtype)
            _, ys = jax.lax.scan(step, state0, xs)
            y = jnp.moveaxis(ys, 0, -1)
            y = y + D[None, :, None] * u
            y = y * jax.nn.silu(z)
            return jnp.swapaxes(y, 1, 2)
        key = jax.random.key(seed)
        ks = jax.random.split(key, 8)
        hidden_states = jax.random.normal(ks[0], (B, L, DM), jnp.float32)
        z = jax.random.normal(ks[1], (B, DI, L), jnp.float32)
        in_proj_w = jax.random.normal(ks[2], (DI, DM), jnp.float32) * DM ** (-0.5)
        conv_w = jax.random.normal(ks[3], (DI, DC), jnp.float32) * DC ** (-0.5)
        conv_b = jnp.zeros((DI,), jnp.float32)
        x_proj_w = jax.random.normal(ks[4], (DR + 2 * DS, DI), jnp.float32) * DI ** (-0.5)
        dt_std = DR ** (-0.5)
        dt_proj_w = jax.random.uniform(ks[5], (DI, DR), jnp.float32, -dt_std, dt_std)
        dt = jnp.exp(jax.random.uniform(ks[6], (DI,), jnp.float32) * (math.log(DT_MAX) - math.log(DT_MIN)) + math.log(DT_MIN))
        dt = jnp.clip(dt, DT_FLOOR)
        dt_proj_b = dt + jnp.log(-jnp.expm1(-dt))
        A_log = jnp.log(jnp.broadcast_to(jnp.arange(1, DS + 1, dtype=jnp.float32), (DI, DS)))
        D = jnp.ones((DI,), jnp.float32)
        return dict(hidden_states=hidden_states, z=z, in_proj_w=in_proj_w, conv_w=conv_w, conv_b=conv_b, x_proj_w=x_proj_w, dt_proj_w=dt_proj_w, dt_proj_b=dt_proj_b, A_log=A_log, D=D)
    _L0_xattn_all = _L0_xattn_setup()
    _L0_xattn_in = {k: v for k, v in _L0_xattn_all.items() if k in ('in_proj_w', 'conv_w', 'conv_b', 'x_proj_w', 'dt_proj_w', 'dt_proj_b', 'A_log', 'D')}
    del _L0_xattn_all

    def _L0_ffn_setup():
        import jax, jax.numpy as jnp
        import numpy as np
        B, S, D = (2, 1024, 512)
        E, DFF = (8, 2048)
        TOP_K = 2
        key = jax.random.key(seed)
        ks = jax.random.split(key, 4)
        scale_in = 1.0 / np.sqrt(D)
        scale_ff = 1.0 / np.sqrt(DFF)
        return {'hidden_states': jax.random.normal(ks[0], (B, S, D), dtype=jnp.float32), 'gate_w': jax.random.normal(ks[1], (E, D), dtype=jnp.float32) * scale_in, 'w1': jax.random.normal(ks[2], (E, D, DFF), dtype=jnp.float32) * scale_in, 'b1': jnp.zeros((E, DFF), dtype=jnp.float32), 'w2': jax.random.normal(ks[3], (E, DFF, D), dtype=jnp.float32) * scale_ff, 'b2': jnp.zeros((E, D), dtype=jnp.float32)}
    _L0_ffn_all = _L0_ffn_setup()
    _L0_ffn_in = {k: v for k, v in _L0_ffn_all.items() if k in ('gate_w', 'w1', 'b1', 'w2', 'b2')}
    del _L0_ffn_all

    def _L1_xattn_setup():
        import jax, jax.numpy as jnp
        import numpy as np
        B_, L_, D_MODEL = (4, 512, 256)
        D_STATE, D_CONV, EXPAND = (16, 4, 2)
        D_INNER = EXPAND * D_MODEL
        DT_RANK = (D_MODEL + 15) // 16

        def silu(x):
            return x * jax.nn.sigmoid(x)
        key = jax.random.key(seed)
        ks = jax.random.split(key, 10)
        f32 = jnp.float32
        hidden_states = jax.random.normal(ks[0], (B_, L_, D_MODEL), dtype=f32)
        z = jax.random.normal(ks[1], (B_, D_INNER, L_), dtype=f32)
        in_proj_w = jax.random.normal(ks[2], (D_INNER, D_MODEL), dtype=f32) * 0.02
        conv_w = jax.random.normal(ks[3], (D_INNER, 1, D_CONV), dtype=f32) * 0.1
        conv_b = jax.random.normal(ks[4], (D_INNER,), dtype=f32) * 0.02
        x_proj_w = jax.random.normal(ks[5], (DT_RANK + 2 * D_STATE, D_INNER), dtype=f32) * 0.02
        dt_proj_w = jax.random.uniform(ks[6], (D_INNER, DT_RANK), dtype=f32, minval=-DT_RANK ** (-0.5), maxval=DT_RANK ** (-0.5))
        dt = jnp.exp(jax.random.uniform(ks[7], (D_INNER,), dtype=f32, minval=np.log(0.001), maxval=np.log(0.1)))
        dt_proj_b = jnp.log(jnp.expm1(dt))
        A_log = jnp.log(jnp.broadcast_to(jnp.arange(1, D_STATE + 1, dtype=f32), (D_INNER, D_STATE)))
        D = jnp.ones((D_INNER,), f32)
        return {'hidden_states': hidden_states, 'z': z, 'in_proj_w': in_proj_w, 'conv_w': conv_w, 'conv_b': conv_b, 'x_proj_w': x_proj_w, 'dt_proj_w': dt_proj_w, 'dt_proj_b': dt_proj_b, 'A_log': A_log, 'D': D}
    _L1_xattn_all = _L1_xattn_setup()
    _L1_xattn_in = {k: v for k, v in _L1_xattn_all.items() if k in ('in_proj_w', 'conv_w', 'conv_b', 'x_proj_w', 'dt_proj_w', 'dt_proj_b', 'A_log', 'D')}
    del _L1_xattn_all

    def _L1_ffn_setup():
        import jax, jax.numpy as jnp
        import numpy as np
        B, S, D, H = (4, 512, 512, 2048)

        def fwht(x):
            orig_shape = x.shape
            n = orig_shape[-1]
            x = x.reshape(-1, n)
            h = 1
            while h < n:
                xb = x.reshape(-1, n // (2 * h), 2, h)
                a = xb[:, :, 0, :]
                b = xb[:, :, 1, :]
                x = jnp.stack([a + b, a - b], axis=2).reshape(-1, n)
                h *= 2
            scale = jnp.asarray(1.0 / np.sqrt(n), dtype=x.dtype)
            return (x * scale).reshape(orig_shape)
        key = jax.random.key(seed)
        kx, k1, k2, k3 = jax.random.split(key, 4)
        x = jax.random.normal(kx, (B, S, D), dtype=jnp.float32)
        W1 = jax.random.normal(k1, (H, D), dtype=jnp.float32) * (1.0 / np.sqrt(D))
        W2 = jax.random.normal(k2, (D, H), dtype=jnp.float32) * (1.0 / np.sqrt(H))
        W3 = jax.random.normal(k3, (H, D), dtype=jnp.float32) * (1.0 / np.sqrt(D))
        return {'x': x, 'W1': W1, 'W2': W2, 'W3': W3}
    _L1_ffn_all = _L1_ffn_setup()
    _L1_ffn_in = {k: v for k, v in _L1_ffn_all.items() if k in ('W1', 'W2', 'W3')}
    del _L1_ffn_all
    return {'x': x, 'ctx_1024': ctx_1024, 'g_xattn': g_xattn, 'g_ffn': g_ffn, 'L0_xattn_in_proj_w': _L0_xattn_in['in_proj_w'], 'L0_xattn_conv_w': _L0_xattn_in['conv_w'], 'L0_xattn_conv_b': _L0_xattn_in['conv_b'], 'L0_xattn_x_proj_w': _L0_xattn_in['x_proj_w'], 'L0_xattn_dt_proj_w': _L0_xattn_in['dt_proj_w'], 'L0_xattn_dt_proj_b': _L0_xattn_in['dt_proj_b'], 'L0_xattn_A_log': _L0_xattn_in['A_log'], 'L0_xattn_D': _L0_xattn_in['D'], 'L0_ffn_gate_w': _L0_ffn_in['gate_w'], 'L0_ffn_w1': _L0_ffn_in['w1'], 'L0_ffn_b1': _L0_ffn_in['b1'], 'L0_ffn_w2': _L0_ffn_in['w2'], 'L0_ffn_b2': _L0_ffn_in['b2'], 'L1_xattn_in_proj_w': _L1_xattn_in['in_proj_w'], 'L1_xattn_conv_w': _L1_xattn_in['conv_w'], 'L1_xattn_conv_b': _L1_xattn_in['conv_b'], 'L1_xattn_x_proj_w': _L1_xattn_in['x_proj_w'], 'L1_xattn_dt_proj_w': _L1_xattn_in['dt_proj_w'], 'L1_xattn_dt_proj_b': _L1_xattn_in['dt_proj_b'], 'L1_xattn_A_log': _L1_xattn_in['A_log'], 'L1_xattn_D': _L1_xattn_in['D'], 'L1_ffn_W1': _L1_ffn_in['W1'], 'L1_ffn_W2': _L1_ffn_in['W2'], 'L1_ffn_W3': _L1_ffn_in['W3']}

def reference(x, ctx_1024, g_xattn, g_ffn, L0_xattn_in_proj_w, L0_xattn_conv_w, L0_xattn_conv_b, L0_xattn_x_proj_w, L0_xattn_dt_proj_w, L0_xattn_dt_proj_b, L0_xattn_A_log, L0_xattn_D, L0_ffn_gate_w, L0_ffn_w1, L0_ffn_b1, L0_ffn_w2, L0_ffn_b2, L1_xattn_in_proj_w, L1_xattn_conv_w, L1_xattn_conv_b, L1_xattn_x_proj_w, L1_xattn_dt_proj_w, L1_xattn_dt_proj_b, L1_xattn_A_log, L1_xattn_D, L1_ffn_W1, L1_ffn_W2, L1_ffn_W3):
    import jax
    import jax.numpy as jnp

    def _L0_xattn_ref(hidden_states, z, in_proj_w, conv_w, conv_b, x_proj_w, dt_proj_w, dt_proj_b, A_log, D):
        import jax, jax.numpy as jnp
        import numpy as np
        import math
        B, L, DM = (2, 512, 256)
        DS, DC, EXP = (16, 4, 2)
        DI = EXP * DM
        DR = math.ceil(DM / 16)
        DT_MIN, DT_MAX, DT_FLOOR = (0.001, 0.1, 0.0001)

        def _ssm_forward(hidden_states, z, in_proj_w, conv_w, conv_b, x_proj_w, dt_proj_w, dt_proj_b, A_log, D):
            b = hidden_states.shape[0]
            x = jnp.einsum('ed,bld->bel', in_proj_w, hidden_states)
            xp = jnp.pad(x, ((0, 0), (0, 0), (DC - 1, 0)))
            xc = jax.lax.conv_general_dilated(xp, conv_w[:, None, :], window_strides=(1,), padding='VALID', dimension_numbers=('NCH', 'OIH', 'NCH'), feature_group_count=DI)
            u = jax.nn.silu(xc + conv_b[None, :, None])
            x_dbl = jnp.einsum('ke,bel->bkl', x_proj_w, u)
            dt_lo = x_dbl[:, :DR]
            Bm = x_dbl[:, DR:DR + DS]
            Cm = x_dbl[:, DR + DS:]
            delta = jax.nn.softplus(jnp.einsum('er,brl->bel', dt_proj_w, dt_lo) + dt_proj_b[None, :, None])
            A = -jnp.exp(A_log)

            def step(state, xs):
                d_t, B_t, C_t, u_t = xs
                dA = jnp.exp(d_t[..., None] * A)
                state = state * dA + (d_t * u_t)[..., None] * B_t[:, None, :]
                y_t = jnp.einsum('ben,bn->be', state, C_t)
                return (state, y_t)
            xs = (jnp.moveaxis(delta, -1, 0), jnp.moveaxis(Bm, -1, 0), jnp.moveaxis(Cm, -1, 0), jnp.moveaxis(u, -1, 0))
            state0 = jnp.zeros((b, DI, DS), delta.dtype)
            _, ys = jax.lax.scan(step, state0, xs)
            y = jnp.moveaxis(ys, 0, -1)
            y = y + D[None, :, None] * u
            y = y * jax.nn.silu(z)
            return jnp.swapaxes(y, 1, 2)
        return _ssm_forward(hidden_states, z, in_proj_w, conv_w, conv_b, x_proj_w, dt_proj_w, dt_proj_b, A_log, D)

    def _L0_ffn_ref(hidden_states, gate_w, w1, b1, w2, b2):
        import jax, jax.numpy as jnp
        import numpy as np
        B, S, D = (2, 1024, 512)
        E, DFF = (8, 2048)
        TOP_K = 2
        b, s, d = hidden_states.shape
        x = hidden_states.reshape(-1, d)
        router_logits = x @ gate_w.T
        _, sel = jax.lax.top_k(router_logits.sum(axis=0), TOP_K)
        rw = jax.nn.softmax(router_logits[:, sel].astype(jnp.float32), axis=1)
        rw = rw.astype(x.dtype)
        w1s, b1s = (w1[sel], b1[sel])
        w2s, b2s = (w2[sel], b2[sel])
        h = jax.nn.gelu(jnp.einsum('nd,kdf->knf', x, w1s) + b1s[:, None, :])
        y = jnp.einsum('knf,kfd->knd', h, w2s) + b2s[:, None, :]
        out = jnp.einsum('nk,knd->nd', rw, y)
        return out.reshape(b, s, -1)

    def _L1_xattn_ref(hidden_states, z, in_proj_w, conv_w, conv_b, x_proj_w, dt_proj_w, dt_proj_b, A_log, D):
        import jax, jax.numpy as jnp
        import numpy as np
        B_, L_, D_MODEL = (4, 512, 256)
        D_STATE, D_CONV, EXPAND = (16, 4, 2)
        D_INNER = EXPAND * D_MODEL
        DT_RANK = (D_MODEL + 15) // 16

        def silu(x):
            return x * jax.nn.sigmoid(x)
        Bsz, L, _ = hidden_states.shape
        d_inner, _, d_conv = conv_w.shape
        dt_rank = dt_proj_w.shape[1]
        d_state = A_log.shape[1]
        x = jnp.einsum('bld,ed->bel', hidden_states, in_proj_w)
        xc = jax.lax.conv_general_dilated(x, conv_w, window_strides=(1,), padding=[(d_conv - 1, 0)], feature_group_count=d_inner, dimension_numbers=('NCH', 'OIH', 'NCH'))
        x = silu(xc + conv_b[None, :, None])
        x_dbl = jnp.einsum('bdl,ed->bel', x, x_proj_w)
        dt_low, Bm, Cm = jnp.split(x_dbl, [dt_rank, dt_rank + d_state], axis=1)
        dt = jnp.einsum('brl,dr->bdl', dt_low, dt_proj_w)
        dt = jax.nn.softplus(dt + dt_proj_b[None, :, None])
        A = -jnp.exp(A_log)
        dt_t = jnp.moveaxis(dt, -1, 0)
        B_t = jnp.moveaxis(Bm, -1, 0)
        C_t = jnp.moveaxis(Cm, -1, 0)
        u_t = jnp.moveaxis(x, -1, 0)

        def step(state, inp):
            d, b, c, u = inp
            dA = jnp.exp(d[..., None] * A)
            state = state * dA + (d * u)[..., None] * b[:, None, :]
            y = jnp.einsum('bdn,bn->bd', state, c)
            return (state, y)
        state0 = jnp.zeros((Bsz, d_inner, d_state), x.dtype)
        _, ys = jax.lax.scan(step, state0, (dt_t, B_t, C_t, u_t))
        y = jnp.moveaxis(ys, 0, 2)
        y = y + D[None, :, None] * x
        y = y * silu(z)
        return jnp.swapaxes(y, 1, 2)

    def _L1_ffn_ref(x, W1, W2, W3):
        import jax, jax.numpy as jnp
        import numpy as np
        B, S, D, H = (4, 512, 512, 2048)

        def fwht(x):
            orig_shape = x.shape
            n = orig_shape[-1]
            x = x.reshape(-1, n)
            h = 1
            while h < n:
                xb = x.reshape(-1, n // (2 * h), 2, h)
                a = xb[:, :, 0, :]
                b = xb[:, :, 1, :]
                x = jnp.stack([a + b, a - b], axis=2).reshape(-1, n)
                h *= 2
            scale = jnp.asarray(1.0 / np.sqrt(n), dtype=x.dtype)
            return (x * scale).reshape(orig_shape)
        up_gate = jnp.einsum('bsd,hd->bsh', x, W1)
        up_lin = jnp.einsum('bsd,hd->bsh', x, W3)
        hidden = jax.nn.silu(up_gate) * up_lin
        hidden = fwht(hidden)
        out = jnp.einsum('bsh,dh->bsd', hidden, W2)
        return out
    x = x + jnp.tanh(g_xattn[0]) * _L0_xattn_ref(ctx_1024, _layernorm(x, axis=-1), L0_xattn_in_proj_w, L0_xattn_conv_w, L0_xattn_conv_b, L0_xattn_x_proj_w, L0_xattn_dt_proj_w, L0_xattn_dt_proj_b, L0_xattn_A_log, L0_xattn_D)
    x = x + jnp.tanh(g_ffn[0]) * _L0_ffn_ref(_layernorm(x, axis=-1), L0_ffn_gate_w, L0_ffn_w1, L0_ffn_b1, L0_ffn_w2, L0_ffn_b2)
    x = x + jnp.tanh(g_xattn[1]) * _L1_xattn_ref(ctx_1024, _layernorm(x, axis=-1), L1_xattn_in_proj_w, L1_xattn_conv_w, L1_xattn_conv_b, L1_xattn_x_proj_w, L1_xattn_dt_proj_w, L1_xattn_dt_proj_b, L1_xattn_A_log, L1_xattn_D)
    x = x + jnp.tanh(g_ffn[1]) * _L1_ffn_ref(_layernorm(x, axis=-1), L1_ffn_W1, L1_ffn_W2, L1_ffn_W3)
    return x

_drawn_inputs = setup_inputs


def setup_inputs(seed=0):
    import zlib

    import numpy as np

    out = dict(_drawn_inputs(seed))
    spreads = {'g_ffn': (-1.0, 0.2),
     'L0_xattn_conv_b': (0.0, 0.1),
     'L0_xattn_D': (1.0, 0.2),
     'L0_ffn_b1': (0.0, 0.1),
     'L0_ffn_b2': (0.0, 0.1),
     'L1_xattn_D': (1.0, 0.6)}
    factors = {'L0_xattn_dt_proj_w': 6.153,
     'L0_xattn_dt_proj_b': 2.678,
     'L1_xattn_in_proj_w': 3.168,
     'L1_xattn_conv_w': 3.248,
     'L1_xattn_conv_b': 8.0,
     'L1_xattn_x_proj_w': 8.0,
     'L1_xattn_dt_proj_w': 8.0,
     'L1_xattn_dt_proj_b': 8.0,
     'L1_xattn_A_log': 8.0}
    for name, (base, spread) in spreads.items():
        noise = np.random.default_rng([zlib.crc32(name.encode()), seed]).standard_normal(out[name].shape)
        drawn = base * np.exp(spread * noise) if base else spread * noise
        out[name] = jnp.asarray(drawn.astype(out[name].dtype))
    for name, factor in factors.items():
        out[name] = (out[name] * factor).astype(out[name].dtype)
    return out
```

```python
from contextlib import ExitStack

import numpy as np
import concourse.bass as bass
from concourse import mybir

P = 128
NB, L, DM = 4, 512, 512
DC, DI, DS, DR, TAPS = 256, 512, 16, 16, 4
E, F = 8, 2048
ET = DI // P
TT = L // P
TILES = NB * TT
NC = 4
CH = DS // NC
KC = DC // P
KD = DM // P
FG = 512
FT = FG // P
NG = F // FG
HB = NB // 2
HTOK = HB * L
HTILES = HTOK // P
P_W, P_CB, P_DB, P_D, P_AL = 0, TAPS, TAPS + 1, TAPS + 2, TAPS + 3
NPAR = TAPS + 3 + DS
EPS = 1e-5
N_SCALE = float(1.0 / np.sqrt(F))

F32 = mybir.dt.float32
U32 = mybir.dt.uint32
ALU = mybir.AluOpType
ACT = mybir.ActivationFunctionType
AX = mybir.AxisListType


class Chain:

    def __init__(self, eng, sem):
        self.eng, self.sem, self.base, self.n, self.outer = eng, sem, 0, 0, []

    def step(self, ins):
        ins.then_inc(self.sem, 1)
        self.n += 1

    def join(self):
        self.eng.wait_ge(self.sem, self.base + self.n)

    def link(self, ins):
        self.step(ins)
        self.join()

    def enter(self, i, per):
        self.outer.append((self.base, self.n))
        self.base, self.n = self.base + self.n + i * per, 0

    def leave(self, per, count):
        assert self.n == per, f"the body marks {self.n}, not {per}"
        self.base, self.n = self.outer.pop()
        self.n += per * count


def build(nc, d):
    ctx = ExitStack()
    sb = lambda name, shape, dt=F32: ctx.enter_context(nc.sbuf_tensor(name, shape, dt))
    sem = lambda name: ctx.enter_context(nc.semaphore(name))
    bank = [ctx.enter_context(nc.psum_tensor(f"bank{i}", [P, 512], F32)) for i in range(8)]

    x_sb = sb("x_sb", [P, TILES, DM])
    bc = sb("bc", [P, 2, DS, L])
    dA = sb("dA", [P, 2, CH, L])
    st = sb("st", [P, 2, CH, L])
    pt = sb("pt", [P, 2, 3, L])
    yt = sb("yt", [P, 2, L])
    pool = sb("pool", [P, 12 * 1024])
    ident = sb("ident", [P, P])
    ones = sb("ones", [P, P])
    par = [sb(f"par{l}", [P, ET, NPAR]) for l in range(2)]
    negA = [sb(f"negA{l}", [P, ET, DS]) for l in range(2)]
    gates = sb("gates", [P, 4])
    mv = sb("mv", [P, TT, 2])
    bnst = sb("bnst", [P, TT, 6])
    rstd = sb("rstd", [P, TT])
    gwT = sb("gwT", [P, KD, E])
    logit = sb("logit", [P, TILES, E])
    lsum = sb("lsum", [P, E])
    top = sb("top", [P, 8])
    topi = sb("topi", [P, 8], U32)
    topf = sb("topf", [P, 8])
    iota = sb("iota", [P, E])
    hot = sb("hot", [P, 2, E])
    lsel = sb("lsel", [P, 2, TILES])
    lwork = sb("lwork", [P, TILES, E])
    lmax = sb("lmax", [P, TILES])
    lexp = sb("lexp", [P, 2, TILES])
    coef = sb("coef", [P, 2, 2, HTILES])
    b1s = sb("b1s", [P, F // P])
    b2b = sb("b2b", [P, DM])
    epsc = sb("epsc", [P, 1])
    onec = sb("onec", [P, 1])
    v = lambda src, o, n, pat, **k: src[:, o:o + n].rearrange(pat, **k)
    ctxT = v(pool, 0, KC * NB * L, "p (k t) -> p k t", k=KC)
    inw = v(pool, 4096, KC * DI, "p (k e) -> p k e", k=KC)
    u4 = v(pool, 5120, 2 * ET * L, "p (s e t) -> p s e t", s=2, e=ET)
    xpw = v(pool, 9216, ET * 48, "p (k m) -> p k m", k=ET)
    dtw = pool[:, 9408:9408 + DI]
    xd = pool[:, 9920:9920 + L]
    e4, r4 = st[:, 0], st[:, 1]
    l4, q4 = dA[:, 0], dA[:, 1]
    hd = pool[:, 10432:10432 + P]
    bcf = bc[:, :, :, :].rearrange("p a n t -> p (a n t)")
    wv = v(bcf, 0, 16 * DM, "p (h d) -> p h d", h=16)
    wz = v(bcf, 16 * DM, 16 * DM, "p (h d) -> p h d", h=16)
    zs = v(pool, 0, TILES * L, "p (t d) -> p t d", t=TILES)
    xT = v(pool, 0, KD * HTOK, "p (k t) -> p k t", k=KD)
    w1g = v(pool, 4096, KD * FG, "p (k f) -> p k f", k=KD)
    w2g = v(pool, 6144, FT * DM, "p (k f) -> p k f", k=FT)
    hT = v(pool, 8192, 2 * FT * L, "p (s f t) -> p s f t", s=2, f=FT)
    xT1 = v(bcf, 0, KD * NB * L, "p (k t) -> p k t", k=KD)
    w3g = v(bcf, 8192, KD * FG, "p (k f) -> p k f", k=KD)
    sg = v(bcf, 10240, 2 * L, "p (s t) -> p s t", s=2)
    xn = st[:, 0]

    dma_par, dma_had, dma_x, dma_ctx = sem("dma_par"), sem("dma_had"), sem("dma_x"), sem("dma_ctx")
    held = sem("held")
    phase = sem("phase")
    act_own, dve_own, pool_own = sem("act_own"), sem("dve_own"), sem("pool_own")
    gates_ready, consts_ready = sem("gates_ready"), sem("consts_ready")
    two = lambda name: [sem(f"{name}{l}") for l in range(2)]
    dma_w = two("dma_w")
    xin = two("xin")
    tap_last = two("tap_last")
    conv = two("conv")
    u_ready = two("u_ready")
    xdbl = two("xdbl")
    xd_ready = two("xd_ready")
    dtraw = two("dtraw")
    soft = two("soft")
    prep_ready = two("prep_ready")
    xd_out = two("xd_out")
    u_out = two("u_out")
    dd_out = two("dd_out")
    butterfly, had_mm, had_ev, had_out = sem("butterfly"), sem("had_mm"), sem("had_ev"), sem("had_out")
    slots = lambda name: [[sem(f"{name}{l}{s}") for s in range(2)] for l in range(2)]
    pt_in = slots("pt_in")
    bc_in = [[sem(f"bc_in{l}{c}") for c in range(NC)] for l in range(2)]
    dA_ready = slots("dA_ready")
    dA_free = slots("dA_free")
    bx_ready = slots("bx_ready")
    p_ready = slots("p_ready")
    st_free = slots("st_free")
    unit_done = sem("unit_done")
    dA_zero = sem("dA_zero")
    y_gated, y_turned, y_added = sem("y_gated"), sem("y_turned"), sem("y_added")
    y1_out = two("y1_out")
    ln_stats, ln_std, ln_done, z_ready = sem("ln_stats"), sem("ln_std"), sem("ln_done"), sem("z_ready")
    xn_turned, xT_ready, xT_out, logit_mm = sem("xn_turned"), sem("xT_ready"), sem("xT_out"), sem("logit_mm")
    lsum_in, lsum_mm, sel_ready, sel_out = sem("lsum_in"), sem("lsum_mm"), sem("sel_ready"), sem("sel_out")
    rt_in, rt_exp = sem("rt_in"), sem("rt_exp")
    xT_in, w1_in, w2_in, b1_in, b2_in = sem("xT_in"), sem("w1_in"), sem("w2_in"), sem("b1_in"), sem("b2_in")
    b2_used = sem("b2_used")
    up_done, hid_ready, down_done, evac_done = sem("up_done"), sem("hid_ready"), sem("down_done"), sem("evac_done")
    g_stats, g_std, g_norm, g_z = sem("g_stats"), sem("g_std"), sem("g_norm"), sem("g_z")
    y1_in, g_gated, g_turned, g_added = sem("y1_in"), sem("g_gated"), sem("g_turned"), sem("g_added")
    g_xturned, g_xT = sem("g_xturned"), sem("g_xT")
    cw_in, cw2_in = sem("cw_in"), sem("cw2_in")
    c_up, c_sg, c_hid, c_down, c_evac = sem("c_up"), sem("c_sg"), sem("c_hid"), sem("c_down"), sem("c_evac")
    out_sem = sem("out_sem")

    CR_BANK, CR_ONE, CR_TWO, CR_ST, CR_UP, CR_HID, CR_DOWN, CR_EV = ET, 1, 2, 3, 2 * FT, FT, 2 * TT, 3 * TT
    opening = [(s, CR_BANK) for s in conv] + [(y_added, CR_TWO), (up_done, CR_UP), (hid_ready, CR_HID),
               (down_done, CR_DOWN), (evac_done, CR_EV), (b2_used, CR_ONE), (g_added, CR_BANK), (g_xT, CR_BANK),
               (c_up, CR_UP), (c_hid, CR_TWO), (c_down, CR_DOWN), (c_evac, CR_EV)]
    opening += [(s, CR_ONE) for g in (soft, xd_out, u_out, dd_out, prep_ready, y1_out) for s in g]
    opening += [(unit_done, CR_TWO)]
    opening += [(s, n) for g, n in ((dA_free, CR_ONE), (p_ready, CR_TWO), (st_free, CR_ST)) for l in g for s in l]
    block = ctx.enter_context(nc.Block())
    ENGINES = 5

    def end_phase(eng, k):
        eng.drain().then_inc(phase, 1)
        eng.wait_ge(phase, ENGINES * k)

    def hold(eng):
        eng.sem_inc(held, 1)

    flat = lambda ap: ap.rearrange("p n t -> p (n t)")
    one = lambda ap: ap.rearrange("p o t -> p (o t)")
    tile_of = lambda i: x_sb[:, bass.ds(i, 1), :].rearrange("p o t -> p (o t)")
    u_of = lambda b, et: one(u4[:, bass.ds(b % 2, 1), et])

    @block.sync
    def _(sp):
        for s, n in opening:
            sp.sem_inc(s, n)
        sp.dma_start(ctxT, d["ctxT"].rearrange("(k p) t -> p k t", p=P)).then_inc(dma_ctx, 16)

        def weights(l):
            sp.dma_start(inw, d[f"inw{l}"].rearrange("(k p) e -> p k e", p=P)).then_inc(dma_w[l], 16)
            sp.dma_start(xpw, d[f"xpw{l}"].rearrange("(k p) m -> p k m", p=P)).then_inc(dma_w[l], 16)
            sp.dma_start(dtw[32:48, :], d[f"dtw{l}"]).then_inc(dma_w[l], 16)
        weights(0)
        for l in range(2):
            sp.dma_start(par[l][:, :, :], d[f"par{l}"].rearrange("p (e n) -> p e n", e=ET)).then_inc(dma_par, 16)
        sp.dma_start(gates[:, :], d["gates"].to_broadcast([P, 4])).then_inc(dma_par, 16)
        sp.dma_start(iota[:, :], d["iota"].to_broadcast([P, E])).then_inc(dma_par, 16)
        sp.dma_start(ident[:, :], d["ident"]).then_inc(dma_par, 16)
        sp.dma_start(gwT[:, :, :], d["gwT"].rearrange("(k p) e -> p k e", p=P)).then_inc(dma_par, 16)
        sp.dma_start(wv, d["W2T"].rearrange("(h p) d -> p h d", p=P)).then_inc(dma_had, 16)
        sp.dma_start(hd, d["had"]).then_inc(dma_had, 16)
        sp.dma_start(x_sb[:, :, :], d["x"].rearrange("(t p) d -> p t d", p=P)).then_inc(dma_x, 16)

        for l in range(2):
            if l:
                sp.wait_ge(dtraw[0], ET * NB)
                weights(1)
            with sp.Fori(0, NB) as b:
                sp.wait_ge(xd_ready[l], b + 1)
                sp.dma_start(d[f"bc{l}"][bass.ds(b, 1)].rearrange("o n t -> (o n) t"), xd[0:32, :]).then_inc(xd_out[l], 16)
                sp.wait_ge(u_ready[l], ET * b + ET)
                sp.dma_start(d[f"prep{l}"][bass.ds(b, 1), 0].rearrange("o e p t -> p (o e) t"),
                             u4[:, bass.ds(b % 2, 1)].rearrange("p o e t -> p (o e) t")).then_inc(u_out[l], 16)
                sp.wait_ge(prep_ready[l], b + 1 + CR_ONE)
                sp.dma_start(d[f"prep{l}"][bass.ds(b, 1), 1].rearrange("o e p t -> p (o e) t"), l4).then_inc(dd_out[l], 16)
                sp.dma_start(d[f"prep{l}"][bass.ds(b, 1), 2].rearrange("o e p t -> p (o e) t"), q4).then_inc(dd_out[l], 16)
        sp.wait_ge(had_ev, 16)
        sp.dma_start(d["w2h"].rearrange("(h p) d -> p h d", p=P), wv).then_inc(had_out, 16)
        for l in range(2):
            sp.wait_ge(xd_out[l], 16 * NB + CR_ONE)
            sp.wait_ge(u_out[l], 16 * NB + CR_ONE)
            sp.wait_ge(dd_out[l], 32 * NB + CR_ONE)
        sp.wait_ge(had_out, 16)
        sp.wait_ge(dma_x, 16)
        end_phase(sp, 1)

        def unit_load(l, b, et):
            if l == 0:
                sp.wait_ge(unit_done, ET * b + et - 2 + 1 + CR_TWO)
            else:
                sp.wait_ge(st_free[1][1], 8 * b + 2 * (et - 2) + 2 + CR_ST)
            sp.dma_start(pt[:, et % 2], d[f"prep{l}"][bass.ds(b, 1), :, et].rearrange("o a p t -> p (o a) t")).then_inc(pt_in[l][et % 2], 16)

        def bc_load(l, b, c):
            sp.wait_ge(p_ready[l][c % 2], 8 * (b - 1) + 2 * (ET - 1) + c // 2 + 1 + CR_TWO)
            for a in range(2):
                src = d[f"bc{l}"][bass.ds(b, 1), DS * a + CH * c:DS * a + CH * c + CH, :].rearrange("o n t -> o (n t)")
                sp.dma_start(flat(bc[:, a, CH * c:CH * c + CH, :]), src.to_broadcast([P, CH * L])).then_inc(bc_in[l][c], 16)

        with sp.Fori(0, NB) as b:
            for et in range(ET):
                unit_load(0, b, et)
                if et == 0:
                    for c in range(NC):
                        bc_load(0, b, c)
        end_phase(sp, 2)

        for hf in range(2):
            sp.wait_ge(xT_ready, HTILES * hf + HTILES)
            sp.dma_start(d["xT"][hf].rearrange("(k p) t -> p k t", p=P), xT).then_inc(xT_out, 16)
        sp.wait_ge(sel_ready, 1)
        sp.dma_start(d["sel"], topi[0:1, :]).then_inc(sel_out, 16)
        sp.wait_ge(xT_out, 32)
        sp.wait_ge(sel_out, 16)
        end_phase(sp, 3)

        with sp.Fori(0, 2) as hf:
            sp.wait_ge(up_done, 64 * hf + CR_UP)
            sp.dma_start(xT, d["xT"][bass.ds(hf, 1)].rearrange("o (k p) t -> p (o k) t", p=P)).then_inc(xT_in, 16)
            with sp.Fori(0, 2) as i:
                e = sp.value_load(d["sel"][0:1, bass.ds(i, 1)], min_val=0, max_val=E - 1)
                j = 2 * hf + i
                sp.wait_ge(hid_ready, 32 * j + CR_HID)
                sp.dma_start(b1s[:, :], d["b1"][bass.ds(e, 1)].rearrange("o p f -> p (o f)")).then_inc(b1_in, 16)
                sp.wait_ge(b2_used, j + CR_ONE)
                sp.dma_start(b2b[:, :], d["b2"][bass.ds(e, 1)].to_broadcast([P, DM])).then_inc(b2_in, 16)
                for k in range(NG):
                    w = 4 * j + k
                    unit_load(1, j, k)
                    sp.wait_ge(up_done, 8 * w + CR_UP)
                    sp.dma_start(w1g, d["w1"][bass.ds(e, 1), :, k * FG:k * FG + FG].rearrange("o (k p) f -> p (o k) f", p=P)).then_inc(w1_in, 16)
                    if k == 0:
                        bc_load(1, j, 0)
                        bc_load(1, j, 1)
                    sp.wait_ge(down_done, 8 * w + CR_DOWN)
                    sp.dma_start(w2g, d["w2"][bass.ds(e, 1), k * FG:k * FG + FG].rearrange("o (k p) f -> p (o k) f", p=P)).then_inc(w2_in, 16)
                    if k == 0:
                        bc_load(1, j, 2)
                        bc_load(1, j, 3)
                    sp.wait_ge(st_free[1][1], 2 * w + CR_ST)
                    sp.dma_start(one(d["y1"][bass.ds(w, 1)].rearrange("o p t -> p o t")), yt[:, (k - 1) % 2, :]).then_inc(y1_out[(k - 1) % 2], 16)
        sp.wait_ge(st_free[1][1], 2 * NB * ET + CR_ST)
        sp.dma_start(d["y1"][NB * ET], yt[:, 1, :]).then_inc(y1_out[1], 16)
        sp.wait_ge(y1_out[0], 16 * 8 + CR_ONE)
        sp.wait_ge(y1_out[1], 16 * 9 + CR_ONE)
        end_phase(sp, 4)

        with sp.Fori(0, NB) as b:
            sp.wait_ge(g_added, ET * b + CR_BANK)
            sp.dma_start(hT[:, 0], d["y1"][bass.ds(ET * b + 1, ET)].rearrange("e p t -> p e t")).then_inc(y1_in, 16)
        end_phase(sp, 5)

        with sp.Fori(0, 2) as hf:
            for g in range(NG):
                w = NG * hf + g
                sp.wait_ge(c_up, 8 * w + CR_UP)
                sp.dma_start(w1g, d["W1T"][:, g * FG:g * FG + FG].rearrange("(k p) f -> p k f", p=P)).then_inc(cw_in, 16)
                sp.dma_start(w3g, d["W3T"][:, g * FG:g * FG + FG].rearrange("(k p) f -> p k f", p=P)).then_inc(cw_in, 16)
                sp.wait_ge(c_down, 8 * w + CR_DOWN)
                sp.dma_start(w2g, d["w2h"][g * FG:g * FG + FG].rearrange("(k p) f -> p k f", p=P)).then_inc(cw2_in, 16)
        sp.wait_ge(c_evac, 64 + CR_EV)
        sp.dma_start(d["out"].rearrange("(t p) d -> p t d", p=P), x_sb[:, :, :]).then_inc(out_sem, 16)
        sp.wait_ge(out_sem, 16)

    @block.tensor
    def _(pe):
        mm = nc.tensor.matmul
        pe.wait_ge(dma_ctx, 16)

        def in_proj(l, b):
            for et in range(ET):
                pe.wait_ge(conv[l], ET * b + et + 1)
                for k in range(KC):
                    last = mm(bank[et][:, :], inw[:, k, et * P:et * P + P], ctxT[:, k, bass.ds(b * L, L)],
                              start=(k == 0), stop=(k == KC - 1))
                last.then_inc(xin[l], 1)

        def x_proj(l, b):
            pe.wait_ge(soft[l], b + CR_ONE)
            for k in range(ET):
                pe.wait_ge(u_ready[l], ET * b + k + 1)
                last = mm(bank[4][0:48, :], xpw[:, k, :], u_of(b, k), start=(k == 0), stop=(k == ET - 1))
            last.then_inc(xdbl[l], 1)
            pe.wait_ge(xd_ready[l], b + 1)
            for et in range(ET):
                mm(bank[4 + et][:, :], dtw[32:48, et * P:et * P + P], xd[32:48, :], start=True, stop=True).then_inc(dtraw[l], 1)

        for l in range(2):
            pe.wait_ge(dma_w[l], 48)
            if l:
                pe.wait_ge(conv[0], ET * NB + CR_BANK)
                pe.wait_ge(soft[0], NB + CR_ONE)
            in_proj(l, 0)
            with pe.Fori(0, NB - 1) as b:
                in_proj(l, b + 1)
                x_proj(l, b)
            x_proj(l, NB - 1)
        pe.wait_ge(dma_had, 32)
        pe.wait_ge(butterfly, 1)
        pe.wait_ge(conv[1], ET * NB + CR_BANK)
        for h in range(16):
            if h >= 4:
                pe.wait_ge(had_ev, h - 3)
            mm(bank[h % 4][:, :], hd, wv[:, h, :], start=True, stop=True).then_inc(had_mm, 1)
        end_phase(pe, 1)

        def turn(bk, src, done):
            for k in range(4):
                last = nc.tensor.transpose(bk[:, k * P:k * P + P], src[:, k * P:k * P + P], ident[:, :])
            last.then_inc(done, 1)

        def reduce_chunk(b, et, c):
            s = c % 2
            pe.wait_ge(p_ready[0][s], 8 * b + 2 * et + c // 2 + 1 + CR_TWO)
            for n in range(CH):
                last = mm(bank[et % 2][:, :], ident[:, :], st[:, s, n, :], start=(c == 0 and n == 0), stop=(c == NC - 1 and n == CH - 1))
            last.then_inc(st_free[0][s], 1)

        def turn_unit(b, et):
            pe.wait_ge(y_gated, ET * b + et + 1)
            pe.wait_ge(y_added, ET * b + et - 2 + 1 + CR_TWO)
            turn(bank[2 + et % 2], yt[:, et % 2, :], y_turned)

        with pe.Fori(0, NB) as b:
            for et in range(ET):
                pe.wait_ge(unit_done, ET * b + et - 2 + 1 + CR_TWO)
                reduce_chunk(b, et, 0)
                reduce_chunk(b, et, 1)
                if et:
                    turn_unit(b, et - 1)
                reduce_chunk(b, et, 2)
                reduce_chunk(b, et, 3)
            turn_unit(b, ET - 1)
        end_phase(pe, 2)

        for t in range(TILES):
            pe.wait_ge(ln_done, 4 + t // TT + 1)
            if t >= 2:
                pe.wait_ge(xT_ready, t - 1)
            turn(bank[4 + t % 2], st[:, (t // TT) % 2, t % TT, :], xn_turned)
            pe.wait_ge(xT_ready, t + 1)
            for k in range(KD):
                last = mm(bank[6][:, t * E:t * E + E], xT[:, k, (t % HTILES) * P:(t % HTILES) * P + P], gwT[:, k, :],
                          start=(k == 0), stop=(k == KD - 1))
            last.then_inc(logit_mm, 1)
        pe.wait_ge(lsum_in, 1)
        mm(bank[7][:, 0:E], ones[:, :], lsum[:, :], start=True, stop=True).then_inc(lsum_mm, 1)
        end_phase(pe, 3)

        with pe.Fori(0, 2) as hf:
            pe.wait_ge(xT_in, 16 * hf + 16)
            hold(pe)
            with pe.Fori(0, 2) as i:
                for k in range(NG):
                    w = 4 * (2 * hf + i) + k
                    pe.wait_ge(w1_in, 16 * w + 16)
                    for g in range(2):
                        for f in range(FT):
                            pe.wait_ge(hid_ready, 8 * w + 4 * g + f - 4 + 1 + CR_HID)
                            for kd in range(KD):
                                last = mm(bank[f][:, :], w1g[:, kd, f * P:f * P + P], xT[:, kd, g * L:g * L + L],
                                          start=(kd == 0), stop=(kd == KD - 1))
                            last.then_inc(up_done, 1)
                    pe.wait_ge(w2_in, 16 * w + 16)
                    for g in range(2):
                        pe.wait_ge(hid_ready, 8 * w + 4 * g + FT + CR_HID)
                        for t in range(TT):
                            pe.wait_ge(evac_done, 8 * w + 4 * g + t - 4 + 1 + CR_EV)
                            for f in range(FT):
                                last = mm(bank[4 + t][:, :], hT[:, g, f, t * P:t * P + P], w2g[:, f, :],
                                          start=(f == 0), stop=(f == FT - 1))
                            last.then_inc(down_done, 1)
        end_phase(pe, 4)

        with pe.Fori(0, NB) as b:
            pe.wait_ge(g_gated, b + 1)
            for et in range(ET):
                pe.wait_ge(g_added, ET * b + et - 4 + 1 + CR_BANK)
                turn(bank[et], st[:, 1, et, :], g_turned)
            pe.wait_ge(g_norm, 2 * b + 2)
            for t in range(TT):
                pe.wait_ge(g_xT, TT * b + t - 4 + 1 + CR_BANK)
                turn(bank[4 + t], st[:, 0, t, :], g_xturned)
        end_phase(pe, 5)

        with pe.Fori(0, 2) as hf:
            for gi in range(NG):
                w = NG * hf + gi
                pe.wait_ge(cw_in, 32 * w + 32)
                for g in range(2):
                    for f in range(FT):
                        pe.wait_ge(c_hid, 8 * w + 4 * g + f - 2 + 1 + CR_TWO)
                        for m, wt in enumerate((w1g, w3g)):
                            for kd in range(KD):
                                last = mm(bank[2 * m + f % 2][:, :], wt[:, kd, f * P:f * P + P],
                                          xT1[:, kd, bass.ds(hf * HTOK + g * L, L)], start=(kd == 0), stop=(kd == KD - 1))
                        last.then_inc(c_up, 1)
                pe.wait_ge(cw2_in, 16 * w + 16)
                for g in range(2):
                    pe.wait_ge(c_hid, 8 * w + 4 * g + FT + CR_TWO)
                    for t in range(TT):
                        pe.wait_ge(c_evac, 8 * w + 4 * g + t - 4 + 1 + CR_EV)
                        for f in range(FT):
                            last = mm(bank[4 + t][:, :], hT[:, g, f, t * P:t * P + P], w2g[:, f, :],
                                      start=(f == 0), stop=(f == FT - 1))
                        last.then_inc(c_down, 1)

    @block.scalar
    def _(act):
        A = nc.scalar.activation
        own = Chain(act, act_own)
        act.wait_ge(dma_par, 16 * 6)
        A(gates[:, :], gates[:, :], ACT.Tanh).then_inc(gates_ready, 1)
        for l in range(2):
            own.link(A(negA[l][:, :, :], par[l][:, :, P_AL:], ACT.Exp))
            own.step(A(negA[l][:, :, :], negA[l][:, :, :], ACT.Copy, scale=-1.0))
        act.wait_ge(consts_ready, 1)

        def conv_start(l, b):
            for et in range(ET):
                act.wait_ge(xin[l], ET * b + et + 1)
                A(u_of(b, et), bank[et][:, :], ACT.Identity, bias=par[l][:, et, P_CB:P_CB + 1],
                  scale=par[l][:, et, P_W + TAPS - 1:P_W + TAPS]).then_inc(tap_last[l], 1)
            for et in range(ET):
                act.wait_ge(conv[l], ET * b + et + 1 + CR_BANK)
                hold(act)
                A(u_of(b, et), u_of(b, et), ACT.Silu).then_inc(u_ready[l], 1)

        def softplus(l, b):
            act.wait_ge(xdbl[l], b + 1)
            act.wait_ge(xd_out[l], 16 * b + CR_ONE)
            A(xd[0:48, :], bank[4][0:48, :], ACT.Copy).then_inc(xd_ready[l], 1)
            act.wait_ge(dd_out[l], 32 * b + CR_ONE)
            for et in range(ET):
                act.wait_ge(dtraw[l], ET * b + et + 1)
                A(r4[:, et, :], bank[4 + et][:, :], ACT.Relu, bias=par[l][:, et, P_DB:P_DB + 1])
                ab = A(e4[:, et, :], bank[4 + et][:, :], ACT.Abs, bias=par[l][:, et, P_DB:P_DB + 1])
            own.link(ab)
            own.link(A(e4, e4, ACT.Exp, scale=-1.0))
            A(l4, e4, ACT.Ln, bias=onec[:, 0:1]).then_inc(soft[l], 1)

        for l in range(2):
            if l:
                act.wait_ge(u_out[0], 16 * NB + CR_ONE)
                act.wait_ge(dd_out[0], 32 * NB + CR_ONE)
                act.wait_ge(xd_out[0], 16 * NB + CR_ONE)
            conv_start(l, 0)
            with act.Fori(0, NB - 1) as b:
                own.enter(b, 2)
                act.wait_ge(u_out[l], 16 * b + CR_ONE)
                act.wait_ge(prep_ready[l], b + CR_ONE)
                conv_start(l, b + 1)
                softplus(l, b)
                own.leave(2, NB - 1)
            softplus(l, NB - 1)
        for h in range(16):
            act.wait_ge(had_mm, h + 1)
            A(wv[:, h, :], bank[h % 4][:, :], ACT.Copy, scale=N_SCALE).then_inc(had_ev, 1)
        end_phase(act, 1)

        def std(stats, done, n):
            act.wait_ge(stats, n)
            A(rstd[:, :], mv[:, :, 1], ACT.Sqrt, bias=epsc[:, 0:1]).then_inc(done, 1)

        def exps(l, b, et, c):
            s, m = c % 2, 8 * b + 2 * et + c // 2
            if c == 0:
                act.wait_ge(pt_in[l][et % 2], 16 * (2 * b + et // 2) + 16)
            act.wait_ge(dA_free[l][s], m + CR_ONE)
            for n in range(CH):
                last = A(dA[:, s, n, 1:], pt[:, et % 2, 1, 1:], ACT.Exp, scale=negA[l][:, et, CH * c + n:CH * c + n + 1])
            last.then_inc(dA_ready[l][s], 1)

        for g in range(NB):
            std(ln_stats, ln_std, g + 1)
        for g in range(NB):
            act.wait_ge(ln_done, g + 1)
            zg = flat(zs[:, TT * g:TT * g + TT, :])
            A(zg, zg, ACT.Silu).then_inc(z_ready, 1)
        act.wait_ge(dA_zero, 1)
        with act.Fori(0, NB) as b:
            for et in range(ET):
                for c in range(NC):
                    exps(0, b, et, c)
        end_phase(act, 2)

        for g in range(NB):
            std(ln_stats, ln_std, NB + g + 1)
            for t in range(TT * g, TT * g + TT):
                if t == HTILES:
                    act.wait_ge(xT_out, 16)
                    act.wait_ge(logit_mm, HTILES)
                act.wait_ge(xn_turned, t + 1)
                o = (t % HTILES) * P
                A(xT[:, :, o:o + P], bank[4 + t % 2][:, :].rearrange("p (k t) -> p k t", k=KD), ACT.Copy).then_inc(xT_ready, 1)
        act.wait_ge(rt_in, 1)
        A(lexp[:, :, :], lsel[:, :, :], ACT.Exp).then_inc(rt_exp, 1)
        end_phase(act, 3)

        def gelu(w, k, g, f):
            act.wait_ge(up_done, 8 * w + 4 * g + f + 1 + CR_UP)
            if f == 0:
                act.wait_ge(down_done, 8 * w + 4 * g + 4 - 8 + CR_DOWN)
            A(hT[:, g, f, :], bank[f][:, :], ACT.Gelu_apprx_tanh, bias=b1s[:, k * FT + f:k * FT + f + 1]).then_inc(hid_ready, 1)

        with act.Fori(0, 2) as hf:
            with act.Fori(0, 2) as i:
                j = 2 * hf + i
                act.wait_ge(b1_in, 16 * j + 16)
                for k in range(NG):
                    w = 4 * j + k
                    exps(1, j, k, 0)
                    gelu(w, k, 0, 0)
                    gelu(w, k, 0, 1)
                    exps(1, j, k, 1)
                    gelu(w, k, 0, 2)
                    gelu(w, k, 0, 3)
                    gelu(w, k, 1, 0)
                    exps(1, j, k, 2)
                    gelu(w, k, 1, 1)
                    gelu(w, k, 1, 2)
                    gelu(w, k, 1, 3)
                    exps(1, j, k, 3)
        end_phase(act, 4)

        with act.Fori(0, NB) as b:
            std(g_stats, g_std, 2 * b + 1)
            act.wait_ge(g_norm, 2 * b + 1)
            A(flat(st[:, 1]), flat(st[:, 1]), ACT.Silu).then_inc(g_z, 1)
            std(g_stats, g_std, 2 * b + 2)
            for t in range(TT):
                act.wait_ge(g_xturned, TT * b + t + 1)
                A(xT1[:, :, bass.ds(b * L + t * P, P)], bank[4 + t][:, :].rearrange("p (k t) -> p k t", k=KD), ACT.Copy).then_inc(g_xT, 1)
        end_phase(act, 5)

        with act.Fori(0, 2) as hf:
            for gi in range(NG):
                w = NG * hf + gi
                for g in range(2):
                    for f in range(FT):
                        n = 8 * w + 4 * g + f
                        act.wait_ge(c_up, n + 1 + CR_UP)
                        act.wait_ge(c_hid, n - 2 + 1 + CR_TWO)
                        A(sg[:, f % 2, :], bank[f % 2][:, :], ACT.Silu).then_inc(c_sg, 1)

    @block.vector
    def _(dve):
        V = nc.vector
        own = Chain(dve, dve_own)
        V.memset(ones[:, :], 1.0)
        V.memset(yt[:, :, :], 0.0)
        V.memset(onec[:, :], 1.0)
        V.memset(epsc[:, :], EPS).then_inc(consts_ready, 1)
        dve.wait_ge(dma_par, 16 * 6)

        def convolve(l, b):
            for tap in range(1, TAPS):
                for et in range(ET):
                    if tap == 1:
                        dve.wait_ge(tap_last[l], ET * b + et + 1)
                    o = u4[:, bass.ds(b % 2, 1), et, tap:].rearrange("p o t -> p (o t)")
                    ins = V.scalar_tensor_tensor(out=o, in0=bank[et][:, 0:L - tap], scalar=par[l][:, et, P_W + TAPS - 1 - tap:P_W + TAPS - tap],
                                                 in1=o, op0=ALU.mult, op1=ALU.add)
                    if tap == TAPS - 1:
                        ins.then_inc(conv[l], 1)
                if tap < TAPS - 1:
                    own.link(ins)

        def delta(l, b):
            dve.wait_ge(soft[l], b + 1 + CR_ONE)
            ef, rf, lf, qf = flat(e4), flat(r4), flat(l4), flat(q4)
            own.link(V.tensor_scalar(qf, ef, 1.0, 1.0, ALU.add, ALU.subtract))
            own.link(V.tensor_tensor(qf, ef, qf, ALU.subtract))
            own.link(V.tensor_tensor(lf, lf, qf, ALU.add))
            own.link(V.tensor_tensor(lf, lf, rf, ALU.add))
            V.tensor_tensor(qf, lf, u4[:, bass.ds(b % 2, 1)].rearrange("p o e t -> p (o e t)"), ALU.mult).then_inc(prep_ready[l], 1)

        for l in range(2):
            convolve(l, 0)
            with dve.Fori(0, NB - 1) as b:
                own.enter(b, 6)
                convolve(l, b + 1)
                delta(l, b)
                own.leave(6, NB - 1)
            delta(l, NB - 1)
        end_phase(dve, 1)

        def norm(tile_ap, dst, stats, std_done, done, n):
            for t in range(TT):
                ins = V.bn_stats(bnst[:, t, :], tile_ap(t))
            own.link(ins)
            hold(dve)
            for t in range(TT):
                ins = V.bn_aggr(mv[:, t, :], bnst[:, t, :])
            ins.then_inc(stats, 1)
            dve.wait_ge(std_done, n)
            own.link(V.reciprocal(rstd[:, :], rstd[:, :]))
            for t in range(TT):
                ins = V.tensor_scalar(dst(t), tile_ap(t), mv[:, t, 0:1], rstd[:, t:t + 1], ALU.subtract, ALU.mult)
            ins.then_inc(done, 1)

        def scan(l, b, et, c):
            s, m = c % 2, 8 * b + 2 * et + c // 2
            dve.wait_ge(dA_ready[l][s], m + 1)
            dve.wait_ge(bx_ready[l][s], m + 1)
            V.tensor_tensor_scan(flat(st[:, s]), flat(dA[:, s]), flat(st[:, s]), 0.0, ALU.mult, ALU.add).then_inc(dA_free[l][s], 1)

        def times_c(l, b, et, c):
            s, m = c % 2, 8 * b + 2 * et + c // 2
            dve.wait_ge(dA_free[l][s], m + 1 + CR_ONE)
            V.tensor_tensor(st[:, s], st[:, s], bc[:, 1, CH * c:CH * c + CH, :], ALU.mult).then_inc(p_ready[l][s], 1)

        dve.wait_ge(dma_x, 16)
        for g in range(NB):
            norm(lambda t: x_sb[:, TT * g + t, :], lambda t: zs[:, TT * g + t, :], ln_stats, ln_std, ln_done, g + 1)
        dve.wait_ge(gates_ready, 1)
        dve.wait_ge(z_ready, NB)

        def gate_unit(b, et):
            s, u = et % 2, ET * b + et
            dve.wait_ge(st_free[0][1], 8 * b + 2 * et + 2 + CR_ST)
            V.scalar_tensor_tensor(out=yt[:, s, :], in0=pt[:, s, 0, :], scalar=par[0][:, et, P_D:P_D + 1], in1=bank[s][:, :],
                                   op0=ALU.mult, op1=ALU.add).then_inc(unit_done, 1)
            dve.wait_ge(unit_done, u + 1 + CR_TWO)
            V.tensor_tensor(yt[:, s, :], yt[:, s, :], one(zs[:, bass.ds(u, 1), :]), ALU.mult).then_inc(y_gated, 1)

        def add_unit(b, et):
            dve.wait_ge(y_turned, ET * b + et + 1)
            xs = x_sb[:, bass.ds(TT * b, TT), et * P:et * P + P]
            V.scalar_tensor_tensor(out=xs, in0=bank[2 + et % 2][:, :].rearrange("p (t e) -> p t e", t=TT), scalar=gates[:, 0:1],
                                   in1=xs, op0=ALU.mult, op1=ALU.add).then_inc(y_added, 1)

        with dve.Fori(0, NB) as b:
            for et in range(ET):
                scan(0, b, et, 0)
                times_c(0, b, et, 0)
                if et:
                    gate_unit(b, et - 1)
                scan(0, b, et, 1)
                times_c(0, b, et, 1)
                if et:
                    add_unit(b, et - 1)
                scan(0, b, et, 2)
                times_c(0, b, et, 2)
                scan(0, b, et, 3)
                times_c(0, b, et, 3)
            gate_unit(b, ET - 1)
            add_unit(b, ET - 1)
        end_phase(dve, 2)

        for g in range(NB):
            if g >= 2:
                dve.wait_ge(xn_turned, TT * (g - 1))
            norm(lambda t: x_sb[:, TT * g + t, :], lambda t: st[:, g % 2, t, :], ln_stats, ln_std, ln_done, NB + g + 1)
        dve.wait_ge(logit_mm, TILES)
        own.link(V.tensor_copy(logit[:, :, :], bank[6][:, 0:TILES * E].rearrange("p (t e) -> p t e", e=E)))
        V.tensor_reduce(out=lsum[:, :], in_=logit[:, :, :].rearrange("p t e -> p e t"), axis=AX.X, op=ALU.add).then_inc(lsum_in, 1)
        dve.wait_ge(lsum_mm, 1)
        own.link(V.tensor_copy(lsum[:, :], bank[7][:, 0:E]))
        own.link(V.max(top[:, :], lsum[:, :]))
        V.max_index(topi[:, :], top[:, :], lsum[:, :]).then_inc(sel_ready, 1)
        dve.wait_ge(sel_ready, 1)
        own.link(V.tensor_copy(topf[:, :], topi[:, :]))
        for k in range(2):
            ins = V.tensor_scalar(hot[:, k, :], iota[:, :], topf[:, k:k + 1], None, ALU.is_equal)
        own.link(ins)
        for k in range(2):
            own.link(V.tensor_tensor(lwork[:, :, :], logit[:, :, :], hot[:, k:k + 1, :].to_broadcast([P, TILES, E]), ALU.mult))
            own.link(V.tensor_reduce(out=lsel[:, k, :], in_=lwork[:, :, :], axis=AX.X, op=ALU.add))
        own.link(V.tensor_tensor(lmax[:, :], lsel[:, 0, :], lsel[:, 1, :], ALU.max))
        for k in range(2):
            ins = V.tensor_tensor(lsel[:, k, :], lsel[:, k, :], lmax[:, :], ALU.subtract)
        ins.then_inc(rt_in, 1)
        dve.wait_ge(rt_exp, 1)
        own.link(V.tensor_tensor(lmax[:, :], lexp[:, 0, :], lexp[:, 1, :], ALU.add))
        own.link(V.reciprocal(lmax[:, :], lmax[:, :]))
        for k in range(2):
            ins = V.tensor_tensor(lexp[:, k, :], lexp[:, k, :], lmax[:, :], ALU.mult)
        own.link(ins)
        for k in range(2):
            ins = V.tensor_scalar(coef[:, :, k, :], lexp[:, k, :].rearrange("p (h t) -> p h t", h=2), gates[:, 2:3], None, ALU.mult)
        end_phase(dve, 3)

        def b_times(b, et, c):
            s, m = c % 2, 8 * b + 2 * et + c // 2
            if c == 0:
                dve.wait_ge(pt_in[1][et % 2], 16 * (2 * b + et // 2) + 16)
            if et == 0:
                dve.wait_ge(bc_in[1][c], 32 * b + 32)
            dve.wait_ge(st_free[1][s], m + CR_ST)
            V.tensor_tensor(st[:, s], pt[:, et % 2, 2:3, :].to_broadcast([P, CH, L]), bc[:, 0, CH * c:CH * c + CH, :],
                            ALU.mult).then_inc(bx_ready[1][s], 1)

        with dve.Fori(0, 2) as hf:
            with dve.Fori(0, 2) as i:
                j = 2 * hf + i

                def cf(t):
                    return coef[:, bass.ds(hf, 1), bass.ds(i, 1), t].rearrange("p a b -> p (a b)")

                def evac(w, t):
                    dve.wait_ge(down_done, 8 * w + t + 1 + CR_DOWN)
                    dve.wait_ge(evac_done, 8 * w + t + 1 - 8 + CR_EV)
                    xt = tile_of(HTILES * hf + t)
                    V.scalar_tensor_tensor(out=xt, in0=bank[4 + t % 4][:, :], scalar=cf(t), in1=xt, op0=ALU.mult, op1=ALU.add).then_inc(evac_done, 1)

                dve.wait_ge(b2_in, 16 * j + 16)
                dve.wait_ge(evac_done, 32 * j + CR_EV)
                for t in range(HTILES):
                    xt = tile_of(HTILES * hf + t)
                    ins = V.scalar_tensor_tensor(out=xt, in0=b2b[:, :], scalar=cf(t), in1=xt, op0=ALU.mult, op1=ALU.add)
                ins.then_inc(b2_used, 1)
                dve.wait_ge(b2_used, j + 1 + CR_ONE)
                for k in range(NG):
                    w = 4 * j + k
                    for c in range(2):
                        b_times(j, k, c)
                        scan(1, j, k, c)
                        times_c(1, j, k, c)
                    b_times(j, k, 2)
                    evac(w, 0)
                    scan(1, j, k, 2)
                    evac(w, 1)
                    times_c(1, j, k, 2)
                    evac(w, 2)
                    b_times(j, k, 3)
                    evac(w, 3)
                    scan(1, j, k, 3)
                    evac(w, 4)
                    times_c(1, j, k, 3)
                    for t in range(5, 8):
                        evac(w, t)
        end_phase(dve, 4)

        with dve.Fori(0, NB) as b:
            own.enter(b, 5)
            mine = lambda t: tile_of(TT * b + t)
            norm(mine, lambda t: st[:, 1, t, :], g_stats, g_std, g_norm, 2 * b + 1)
            dve.wait_ge(g_z, b + 1)
            dve.wait_ge(y1_in, 16 * b + 16)
            V.tensor_tensor(flat(st[:, 1]), flat(st[:, 1]), flat(hT[:, 0]), ALU.mult).then_inc(g_gated, 1)
            for et in range(ET):
                dve.wait_ge(g_turned, ET * b + et + 1)
                xs = x_sb[:, bass.ds(TT * b, TT), et * P:et * P + P]
                ins = V.scalar_tensor_tensor(out=xs, in0=bank[et][:, :].rearrange("p (t e) -> p t e", t=TT), scalar=gates[:, 1:2],
                                             in1=xs, op0=ALU.mult, op1=ALU.add).then_inc(g_added, 1)
            dve.wait_ge(g_added, ET * b + ET + CR_BANK)
            dve.wait_ge(g_xT, TT * b + CR_BANK)
            hold(dve)
            norm(mine, lambda t: st[:, 0, t, :], g_stats, g_std, g_norm, 2 * b + 2)
            own.step(V.memset(topf[:, 0:1], 0.0))
            own.leave(5, NB)
        end_phase(dve, 5)

        with dve.Fori(0, 2) as hf:
            for gi in range(NG):
                w = NG * hf + gi
                for g in range(2):
                    dve.wait_ge(c_down, 8 * w + 4 * g + 4 - 8 + CR_DOWN)
                    for f in range(FT):
                        dve.wait_ge(c_sg, 8 * w + 4 * g + f + 1)
                        V.tensor_tensor(hT[:, g, f, :], sg[:, f % 2, :], bank[2 + f % 2][:, :], ALU.mult).then_inc(c_hid, 1)
                for t in range(HTILES):
                    n = 8 * w + t
                    dve.wait_ge(c_down, n + 1 + CR_DOWN)
                    dve.wait_ge(c_evac, n + 1 - 8 + CR_EV)
                    xt = tile_of(HTILES * hf + t)
                    V.scalar_tensor_tensor(out=xt, in0=bank[4 + t % 4][:, :], scalar=gates[:, 3:4], in1=xt, op0=ALU.mult, op1=ALU.add).then_inc(c_evac, 1)

    @block.gpsimd
    def _(gp):
        G = nc.gpsimd
        own = Chain(gp, pool_own)
        gp.wait_ge(dma_had, 32)
        src, dst = wv, wz
        for s in range(4):
            a = src.rearrange("p (h two l) d -> p two h (l d)", two=2, l=2 ** s)
            o = dst.rearrange("p (h two l) d -> p two h (l d)", two=2, l=2 ** s)
            G.tensor_tensor(o[:, 0], a[:, 0], a[:, 1], ALU.add)
            last = G.tensor_tensor(o[:, 1], a[:, 0], a[:, 1], ALU.subtract)
            if s < 3:
                own.link(last)
            src, dst = dst, src
        last.then_inc(butterfly, 1)
        end_phase(gp, 1)

        G.memset(dA[:, :, :, 0:1], 0.0).then_inc(dA_zero, 1)
        with gp.Fori(0, NB) as b:
            for et in range(ET):
                gp.wait_ge(pt_in[0][et % 2], 16 * (2 * b + et // 2) + 16)
                for c in range(NC):
                    s, m = c % 2, 8 * b + 2 * et + c // 2
                    if et == 0:
                        gp.wait_ge(bc_in[0][c], 32 * b + 32)
                    gp.wait_ge(st_free[0][s], m + CR_ST)
                    G.tensor_tensor(st[:, s], pt[:, et % 2, 2:3, :].to_broadcast([P, CH, L]), bc[:, 0, CH * c:CH * c + CH, :],
                                    ALU.mult).then_inc(bx_ready[0][s], 1)
        end_phase(gp, 2)
        end_phase(gp, 3)

        with gp.Fori(0, 2) as hf:
            with gp.Fori(0, 2) as i:
                j = 2 * hf + i
                own.enter(j, ET * (1 + 2 * NC))
                for et in range(ET):
                    s2 = et % 2
                    gp.wait_ge(pt_in[1][s2], 16 * (2 * j + et // 2) + 16)
                    gp.wait_ge(y1_out[s2], 16 * (2 * j + et // 2 + s2) + CR_ONE)
                    hold(gp)
                    own.link(G.tensor_scalar(yt[:, s2, :], pt[:, s2, 0, :], par[1][:, et, P_D:P_D + 1], None, ALU.mult))
                    for c in range(NC):
                        s, m = c % 2, 8 * j + 2 * et + c // 2
                        gp.wait_ge(p_ready[1][s], m + 1 + CR_TWO)
                        own.link(G.tensor_tensor(st[:, s, 0:2], st[:, s, 0:2], st[:, s, 2:4], ALU.add))
                        own.link(G.tensor_tensor(st[:, s, 0], st[:, s, 0], st[:, s, 1], ALU.add))
                        G.tensor_tensor(yt[:, s2, :], yt[:, s2, :], st[:, s, 0], ALU.add).then_inc(st_free[1][s], 1)
                        gp.wait_ge(st_free[1][s], m + 1 + CR_ST)
                own.leave(ET * (1 + 2 * NC), 4)
        end_phase(gp, 4)
        end_phase(gp, 5)

    ctx.close()


def kernel(**a):
    import concourse.bacc as bacc
    from concourse.bass_utils import run_bass_kernel_spmd

    n = lambda name: np.asarray(a[name])
    had = np.array([[1.0]], np.float32)
    while had.shape[0] < P:
        had = np.block([[had, had], [had, -had]]).astype(np.float32)
    host = {
        "x": n("x").reshape(NB * L, DM),
        "ctxT": n("ctx_1024").reshape(NB * L, DC).T,
        "gates": np.concatenate([n("g_xattn"), n("g_ffn")])[None, :],
        "ident": np.eye(P, dtype=np.float32),
        "had": had,
        "iota": np.arange(E, dtype=np.float32)[None, :],
        "gwT": n("L0_ffn_gate_w").T,
        "w1": n("L0_ffn_w1"),
        "b1": n("L0_ffn_b1").reshape(E, F // P, P).transpose(0, 2, 1),
        "w2": n("L0_ffn_w2"),
        "b2": n("L0_ffn_b2"),
        "W1T": n("L1_ffn_W1").T,
        "W2T": n("L1_ffn_W2").T,
        "W3T": n("L1_ffn_W3").T,
    }
    for l in range(2):
        g = lambda name: n(f"L{l}_xattn_{name}")
        host[f"inw{l}"] = g("in_proj_w").T
        host[f"xpw{l}"] = np.concatenate([g("x_proj_w")[DR:], g("x_proj_w")[:DR]]).T
        host[f"dtw{l}"] = g("dt_proj_w").T
        cols = [g("conv_w").reshape(DI, TAPS), g("conv_b")[:, None], g("dt_proj_b")[:, None], g("D")[:, None], g("A_log")]
        host[f"par{l}"] = np.concatenate(cols, axis=1).reshape(ET, P, NPAR).transpose(1, 0, 2).reshape(P, ET * NPAR)
    nc = bacc.Bacc("TRN2", target_bir_lowering=False, num_devices=1)
    arrays = {f"in_{k}": np.ascontiguousarray(v) for k, v in host.items()}
    d = {k: nc.dram_tensor(f"in_{k}", v.shape, mybir.dt.from_np(v.dtype), kind="ExternalInput").ap() for k, v in host.items()}
    scratch = {"bc0": [NB, 2 * DS, L], "bc1": [NB, 2 * DS, L], "prep0": [NB, 3, ET, P, L], "prep1": [NB, 3, ET, P, L],
               "y1": [1 + NB * ET, P, L], "xT": [2, DM, HTOK], "w2h": [F, DM]}
    for k, shape in scratch.items():
        d[k] = nc.dram_tensor(k, shape, F32, kind="Internal").ap()
    d["sel"] = nc.dram_tensor("sel", [1, 8], U32, kind="Internal").ap()
    d["out"] = nc.dram_tensor("out_0", [NB * L, DM], F32, kind="ExternalOutput").ap()
    build(nc, d)
    r = run_bass_kernel_spmd(nc, [arrays], core_ids=[0])
    return r.results[0]["out_0"].reshape(NB, L, DM)
```

```python
from contextlib import ExitStack

import numpy as np
import concourse.bass as bass
from concourse import mybir

P = 128
NB, L, DM = 4, 512, 512
DC, DI, DS, DR, TAPS = 256, 512, 16, 16, 4
E, F = 8, 2048
ET = DI // P
TT = L // P
TILES = NB * TT
NC = 4
CH = DS // NC
KC = DC // P
KD = DM // P
FG = 512
FT = FG // P
NG = F // FG
HB = NB // 2
HTOK = HB * L
HTILES = HTOK // P
P_W, P_CB, P_DB, P_D, P_AL = 0, TAPS, TAPS + 1, TAPS + 2, TAPS + 3
NPAR = TAPS + 3 + DS
EPS = 1e-5
S_X, S_W, S_H = 256.0, 256.0, 64.0
N_SCALE = float(S_W / np.sqrt(F))

F32 = mybir.dt.float32
F16 = mybir.dt.float16
U32 = mybir.dt.uint32
ALU = mybir.AluOpType
ACT = mybir.ActivationFunctionType
AX = mybir.AxisListType


class Chain:

    def __init__(self, eng, sem):
        self.eng, self.sem, self.base, self.n, self.outer = eng, sem, 0, 0, []

    def step(self, ins):
        ins.then_inc(self.sem, 1)
        self.n += 1

    def join(self):
        self.eng.wait_ge(self.sem, self.base + self.n)

    def link(self, ins):
        self.step(ins)
        self.join()

    def enter(self, i, per):
        self.outer.append((self.base, self.n))
        self.base, self.n = self.base + self.n + i * per, 0

    def leave(self, per, count):
        assert self.n == per, f"the body marks {self.n}, not {per}"
        self.base, self.n = self.outer.pop()
        self.n += per * count


def build(nc, d):
    ctx = ExitStack()
    sb = lambda name, shape, dt=F32: ctx.enter_context(nc.sbuf_tensor(name, shape, dt))
    sem = lambda name: ctx.enter_context(nc.semaphore(name))
    bank = [ctx.enter_context(nc.psum_tensor(f"bank{i}", [P, 512], F32)) for i in range(8)]

    x_sb = sb("x_sb", [P, TILES, DM])
    bc = sb("bc", [P, 2, DS, L])
    dA = sb("dA", [P, 2, CH, L])
    st = sb("st", [P, 2, CH, L])
    pt = sb("pt", [P, 2, 3, L])
    yt = sb("yt", [P, 2, L])
    pool = sb("pool", [P, 15 * 1024])
    ident = sb("ident", [P, P])
    par = [sb(f"par{l}", [P, ET, NPAR]) for l in range(2)]
    negA = [sb(f"negA{l}", [P, ET, DS]) for l in range(2)]
    gates = sb("gates", [P, 4])
    mv = sb("mv", [P, TT, 2])
    down1 = sb("down1", [P, 1])
    bnst = sb("bnst", [P, TT, 6])
    rstd = sb("rstd", [P, TT])
    gwT = sb("gwT", [P, KD, E])
    lsum = sb("lsum", [P, E])
    top = sb("top", [P, 8])
    topi = sb("topi", [P, 8], U32)
    topf = sb("topf", [P, 8])
    iota = sb("iota", [P, E])
    hot = sb("hot", [P, 2, E])
    lsel = sb("lsel", [P, 2, TILES])
    lmax = sb("lmax", [P, TILES])
    lexp = sb("lexp", [P, 2, TILES])
    cbias = sb("cbias", [P, 2, 2, HTILES])
    coef = sb("coef", [P, 2, 2, HTILES])
    b1s = sb("b1s", [P, F // P])
    epsc = sb("epsc", [P, 1])
    onec = sb("onec", [P, 1])
    v = lambda src, o, size, pat, /, **k: src[:, o:o + size].rearrange(pat, **k)
    ctxT = v(pool, 0, KC * NB * L, "p (k t) -> p k t", k=KC)
    inw = v(pool, 4096, KC * DI, "p (k e) -> p k e", k=KC)
    u4 = v(pool, 5120, 2 * ET * L, "p (s e t) -> p s e t", s=2, e=ET)
    xpw = v(pool, 9216, ET * 48, "p (k m) -> p k m", k=ET)
    dtw = pool[:, 9408:9408 + DI]
    xd = pool[:, 9920:9920 + L]
    e4, r4 = st[:, 0], st[:, 1]
    l4, q4 = dA[:, 0], dA[:, 1]
    hd = pool[:, 10432:10432 + P]
    bcf = bc[:, :, :, :].rearrange("p a n t -> p (a n t)")
    wv = v(bcf, 0, 16 * DM, "p (h d) -> p h d", h=16)
    wz = v(bcf, 16 * DM, 16 * DM, "p (h d) -> p h d", h=16)
    zg = v(pt[:, :, :, :].rearrange("p s a t -> p (s a t)"), 0, TT * L, "p (t d) -> p t d", t=TT)
    stx = v(pool, 11264, 2 * CH * L, "p (s n t) -> p s n t", s=2, n=CH)
    stA = lambda c: st[:, c] if c < 2 else stx[:, c - 2]
    zt = v(pool, 1024, 2 * L, "p (s t) -> p s t", s=2)
    ctxb = v(pool, 0, KC * L, "p (k t) -> p k t", k=KC)
    u1 = v(pool, 5120, ET * L, "p (e t) -> p e t", e=ET)
    l1, e1 = (v(pool, o, 4 * L, "p (h s t) -> p h s t", h=2, s=2) for o in (2048, 7168))
    r1 = v(pool, 0, 2 * L, "p (s t) -> p s t", s=2)
    xTf = v(pool, 12288, 2 * KD * P, "p (s k t) -> p s k t", s=2, k=KD)
    logit = v(pool, 13312, TILES * E, "p (t e) -> p t e", t=TILES)
    lwork = v(pool, 13440, TILES * E, "p (t e) -> p t e", t=TILES)
    ones = pool[:, 13568:13568 + P]
    half = lambda o, n: pool[:, o:o + n // 2].bitcast(F16)
    xT = half(0, 2 * KD * HTOK).rearrange("p (a k t) -> p a k t", a=2, k=KD)
    w1g = half(4096, 2 * KD * FG).rearrange("p (a k f) -> p a k f", a=2, k=KD)
    w2g = half(6144, 2 * FT * DM).rearrange("p (a k f) -> p a k f", a=2, k=FT)
    hT = half(8192, 4 * FT * L).rearrange("p (a s f t) -> p a s f t", a=2, s=2, f=FT)
    stage = v(pool, 12288, KD * FG, "p (k f) -> p k f", k=KD)
    h32 = v(pool, 14336, 2 * L, "p (s t) -> p s t", s=2)
    b2b = h32[:, 0]
    bch = bcf.bitcast(F16)
    xT1 = bch[:, 0:2 * KD * NB * L].rearrange("p (a k t) -> p a k t", a=2, k=KD)
    w3g = bch[:, 16384:16384 + 2 * KD * FG].rearrange("p (a k f) -> p a k f", a=2, k=KD)
    stage3 = v(bcf, 10240, KD * FG, "p (k f) -> p k f", k=KD)
    sg = v(bcf, 12288, 2 * L, "p (s t) -> p s t", s=2)
    y1b = v(bcf, 13312, ET * L, "p (e t) -> p e t", e=ET)
    w2s = pool[:, 10624:10624 + 8 * DM].bitcast(F16).rearrange("p (s h a d) -> p s h a d", s=2, h=4, a=2)
    xn = st[:, 0]

    dma_par, dma_had, dma_x, dma_ctx = sem("dma_par"), sem("dma_had"), sem("dma_x"), sem("dma_ctx")
    held = sem("held")
    phase = sem("phase")
    act_own, dve_own, pool_own = sem("act_own"), sem("dve_own"), sem("pool_own")
    gates_ready, consts_ready = sem("gates_ready"), sem("consts_ready")
    two = lambda name: [sem(f"{name}{l}") for l in range(2)]
    dma_w = two("dma_w")
    xin = two("xin")
    tap_last = two("tap_last")
    conv = two("conv")
    u_ready = two("u_ready")
    xdbl = two("xdbl")
    xd_ready = two("xd_ready")
    dtraw = two("dtraw")
    soft = two("soft")
    prep_ready = two("prep_ready")
    xd_out = two("xd_out")
    u_out = two("u_out")
    dd_out = sem("dd_out")
    dd1_out = two("dd1_out")
    butterfly, had_mm, had_hi, had_lo = sem("butterfly"), sem("had_mm"), sem("had_hi"), sem("had_lo")
    had_out = two("had_out")
    slots = lambda name: [[sem(f"{name}{l}{s}") for s in range(2)] if l or name == "pt_in" else [] for l in range(2)]
    pt_in = slots("pt_in")
    uz_in = two("uz_in")
    bc_in = [sem(f"bc_in{c}") for c in range(NC)]
    dA_ready = slots("dA_ready")
    dA_free = slots("dA_free")
    bx_ready = slots("bx_ready")
    p_ready = slots("p_ready")
    st_free = slots("st_free")
    a_exp, a_bx, a_scan, a_p = sem("a_exp"), sem("a_bx"), sem("a_scan"), sem("a_p")
    a_summed = sem("a_summed")
    a_b_in, a_c_in = ([sem(f"{n}{c}") for c in range(NC)] for n in ("a_b_in", "a_c_in"))
    unit_done = sem("unit_done")
    dA_zero = sem("dA_zero")
    y_gated, y_turned, y_added = sem("y_gated"), sem("y_turned"), sem("y_added")
    y1_out = two("y1_out")
    ln_stats, ln_std, ln_done, z_ready = sem("ln_stats"), sem("ln_std"), sem("ln_done"), sem("z_ready")
    z_out, ctx_in = sem("z_out"), sem("ctx_in")
    xn_turned, xT_ready, xT_out, logit_mm = sem("xn_turned"), sem("xT_ready"), sem("xT_out"), sem("logit_mm")
    xT_f32, xT_hi = sem("xT_f32"), sem("xT_hi")
    lsum_in, lsum_mm, sel_ready, sel_out = sem("lsum_in"), sem("lsum_mm"), sem("sel_ready"), sem("sel_out")
    rt_in, rt_exp = sem("rt_in"), sem("rt_exp")
    xT_in, w1_in, w2_in, b1_in, b2_in = sem("xT_in"), sem("w1_in"), sem("w2_in"), sem("b1_in"), sem("b2_in")
    b2_used = sem("b2_used")
    w1_hi, w1_lo, w2_hi, w2_lo = sem("w1_hi"), sem("w1_lo"), sem("w2_hi"), sem("w2_lo")
    h_full, hid_hi, hid_lo = sem("h_full"), sem("hid_hi"), sem("hid_lo")
    up_done, down_done, evac_done = sem("up_done"), sem("down_done"), sem("evac_done")
    g_stats, g_std, g_norm, g_z = sem("g_stats"), sem("g_std"), sem("g_norm"), sem("g_z")
    y1_in, g_gated, g_turned, g_added = sem("y1_in"), sem("g_gated"), sem("g_turned"), sem("g_added")
    g_xturned, g_xhi, g_xT = sem("g_xturned"), sem("g_xhi"), sem("g_xT")
    cw_in, cw2_in = sem("cw_in"), sem("cw2_in")
    cw_hi, cw_lo = sem("cw_hi"), sem("cw_lo")
    c_up, c_sg, c_full, c_hi, c_lo, c_down, c_evac = (sem(x) for x in ("c_up", "c_sg", "c_full", "c_hi", "c_lo", "c_down", "c_evac"))
    out_sem = sem("out_sem")

    CR_BANK, CR_ONE, CR_TWO, CR_ST, CR_UP, CR_HID, CR_DOWN, CR_EV, CR_RING = ET, 1, 2, 3, 2 * FT, FT, 2 * TT, 3 * TT, NC
    opening = [(s, CR_BANK) for s in conv] + [(s, CR_RING) for s in (a_bx, a_p, a_summed)] + [(a_scan, CR_TWO), (a_exp, CR_RING), (soft[1], CR_TWO), (prep_ready[1], CR_TWO), 
               (y_gated, CR_TWO), (z_out, CR_ONE), (y_added, CR_TWO), (up_done, CR_UP), (h_full, CR_HID), (hid_lo, CR_TWO),
               (w1_lo, CR_ONE), (w2_lo, CR_ONE), (cw_lo, CR_ONE),
               (down_done, CR_DOWN), (evac_done, CR_EV), (b2_used, CR_ONE), (g_added, CR_BANK), (g_xT, CR_BANK),
               (c_up, CR_UP), (c_full, CR_TWO), (c_lo, CR_TWO), (c_down, CR_DOWN), (c_evac, CR_EV)]
    opening += [(s, CR_ONE) for g in (soft[:1], xd_out, u_out, [dd_out], dd1_out, prep_ready[:1], y1_out, had_out) for s in g]
    opening += [(unit_done, CR_TWO)]
    opening += [(s, n) for g, n in ((dA_free, CR_ONE), (p_ready, CR_TWO), (st_free, CR_ST)) for l in g for s in l]
    block = ctx.enter_context(nc.Block())
    ENGINES = 5

    def end_phase(eng, k):
        eng.drain().then_inc(phase, 1)
        eng.wait_ge(phase, ENGINES * k)

    def hold(eng):
        eng.sem_inc(held, 1)

    flat = lambda ap: ap.rearrange("p n t -> p (n t)")
    one = lambda ap: ap.rearrange("p o t -> p (o t)")
    tile_of = lambda i: x_sb[:, bass.ds(i, 1), :].rearrange("p o t -> p (o t)")
    u_of = lambda b, et: one(u4[:, bass.ds(b % 2, 1), et])

    @block.sync
    def _(sp):
        for s, n in opening:
            sp.sem_inc(s, n)
        sp.dma_start(ctxT, d["ctxT"].rearrange("(k p) t -> p k t", p=P)).then_inc(dma_ctx, 16)

        def weights(l):
            sp.dma_start(inw, d[f"inw{l}"].rearrange("(k p) e -> p k e", p=P)).then_inc(dma_w[l], 16)
            sp.dma_start(xpw, d[f"xpw{l}"].rearrange("(k p) m -> p k m", p=P)).then_inc(dma_w[l], 16)
            sp.dma_start(dtw[32:48, :], d[f"dtw{l}"]).then_inc(dma_w[l], 16)
        weights(0)
        for l in range(2):
            sp.dma_start(par[l][:, :, :], d[f"par{l}"].rearrange("p (e n) -> p e n", e=ET)).then_inc(dma_par, 16)
        sp.dma_start(gates[:, :], d["gates"].to_broadcast([P, 4])).then_inc(dma_par, 16)
        sp.dma_start(iota[:, :], d["iota"].to_broadcast([P, E])).then_inc(dma_par, 16)
        sp.dma_start(ident[:, :], d["ident"]).then_inc(dma_par, 16)
        sp.dma_start(gwT[:, :, :], d["gwT"].rearrange("(k p) e -> p k e", p=P)).then_inc(dma_par, 16)
        sp.dma_start(x_sb[:, :, :], d["x"].rearrange("(t p) d -> p t d", p=P)).then_inc(dma_x, 16)
        sp.dma_start(wv, d["W2T"].rearrange("(h p) d -> p h d", p=P)).then_inc(dma_had, 16)
        sp.dma_start(hd, d["had"]).then_inc(dma_had, 16)

        with sp.Fori(0, NB) as b:
            sp.wait_ge(z_ready, b + 1)
            sp.dma_start(d["z"][bass.ds(b, 1)].rearrange("o t p d -> p (o t) d"), zg).then_inc(z_out, 16)
            sp.wait_ge(xd_ready[0], b + 1)
            sp.dma_start(d["bc0"][bass.ds(b, 1)].rearrange("o n t -> (o n) t"), xd[0:32, :]).then_inc(xd_out[0], 16)
            sp.wait_ge(u_ready[0], ET * b + ET)
            sp.dma_start(d["prep0"][bass.ds(b, 1), 0].rearrange("o e p t -> p (o e) t"),
                         u4[:, bass.ds(b % 2, 1)].rearrange("p o e t -> p (o e) t")).then_inc(u_out[0], 16)
            sp.wait_ge(prep_ready[0], b + 1 + CR_ONE)
            sp.dma_start(d["prep0"][bass.ds(b, 1), 1].rearrange("o e p t -> p (o e) t"), l4).then_inc(dd_out, 16)
            sp.dma_start(d["prep0"][bass.ds(b, 1), 2].rearrange("o e p t -> p (o e) t"), q4).then_inc(dd_out, 16)
        sp.wait_ge(dtraw[0], ET * NB)
        weights(1)
        for h in range(4):
            sp.wait_ge(had_lo, 4 * h + 4)
            for a in range(2):
                sp.dma_start(d["w2h"][a, 4 * h * P:4 * h * P + 4 * P].rearrange("(h p) d -> p h d", p=P), w2s[:, h % 2, :, a]).then_inc(had_out[h % 2], 16)
        sp.wait_ge(xd_out[0], 16 * NB + CR_ONE)
        sp.wait_ge(u_out[0], 16 * NB + CR_ONE)
        sp.wait_ge(dd_out, 32 * NB + CR_ONE)
        sp.wait_ge(z_out, 16 * NB + CR_ONE)
        for s in range(2):
            sp.wait_ge(had_out[s], 32 * 2 + CR_ONE)
        sp.wait_ge(dma_x, 16)
        end_phase(sp, 1)

        def load_deltas(b, et):
            n = NC * (ET * b + et - 2) + NC
            sp.wait_ge(a_exp, n + CR_RING)
            sp.wait_ge(a_bx, n + CR_RING)
            sp.dma_start(pt[:, et % 2, 1:3], d["prep0"][bass.ds(b, 1), 1:3, et].rearrange("o a p t -> p (o a) t")).then_inc(pt_in[0][et % 2], 16)

        def load_gate(b, et):
            sp.wait_ge(y_gated, ET * b + et - 2 + 1 + CR_TWO)
            hold(sp)
            sp.dma_start(pt[:, et % 2, 0], d["prep0"][bass.ds(b, 1), 0, et].rearrange("o p t -> p (o t)")).then_inc(uz_in[et % 2], 16)
            sp.dma_start(zt[:, et % 2, :], d["z"][bass.ds(b, 1), et].rearrange("o p t -> p (o t)")).then_inc(uz_in[et % 2], 16)

        def spread(b, a, c, done):
            src = d["bc0"][bass.ds(b, 1), DS * a + CH * c:DS * a + CH * c + CH, :].rearrange("o n t -> o (n t)")
            sp.dma_start(flat(bc[:, a, CH * c:CH * c + CH, :]), src.to_broadcast([P, CH * L])).then_inc(done[c], 16)

        with sp.Fori(0, NB) as b:
            for c in range(NC):
                if c == 0:
                    load_deltas(b, 0)
                n = NC * ET * (b - 1) + NC * (ET - 1) + c + 1
                sp.wait_ge(a_bx, n + CR_RING)
                spread(b, 0, c, a_b_in)
                if c == 0:
                    load_gate(b, 0)
                if c == 1:
                    sp.wait_ge(prep_ready[1], 2 * b + CR_TWO)
                    sp.dma_start(ctxb, d["ctxT"].rearrange("(k p) t -> p k t", p=P)[:, :, bass.ds(b * L, L)]).then_inc(ctx_in, 16)
                sp.wait_ge(a_p, n + CR_RING)
                spread(b, 1, c, a_c_in)
            load_deltas(b, 1)
            load_gate(b, 1)
            load_deltas(b, 2)
            load_gate(b, 2)
            sp.wait_ge(u_ready[1], ET * b + ET)
            sp.dma_start(d["prep1"][bass.ds(b, 1), 0].rearrange("o e p t -> p (o e) t"), u1).then_inc(u_out[1], 16)
            load_deltas(b, 3)
            sp.wait_ge(xd_ready[1], b + 1)
            sp.dma_start(d["bc1"][bass.ds(b, 1)].rearrange("o n t -> (o n) t"), xd[0:32, :]).then_inc(xd_out[1], 16)
            load_gate(b, 3)
            sp.wait_ge(prep_ready[1], 2 * b + 1 + CR_TWO)
            for a, part in enumerate((l1[:, 0], e1[:, 0])):
                sp.dma_start(d["prep1"][bass.ds(b, 1), 1 + a, 0:2].rearrange("o e p t -> p (o e) t"), part).then_inc(dd1_out[0], 16)
        sp.wait_ge(xd_out[1], 16 * NB + CR_ONE)
        sp.wait_ge(u_out[1], 16 * NB + CR_ONE)
        for h in range(2):
            sp.wait_ge(dd1_out[h], 32 * NB + CR_ONE)
        end_phase(sp, 2)

        def unit_load(b, et):
            sp.wait_ge(st_free[1][1], 8 * b + 2 * (et - 2) + 2 + CR_ST)
            sp.dma_start(pt[:, et % 2], d["prep1"][bass.ds(b, 1), :, et].rearrange("o a p t -> p (o a) t")).then_inc(pt_in[1][et % 2], 16)

        def bc_load(b, c):
            sp.wait_ge(p_ready[1][c % 2], 8 * (b - 1) + 2 * (ET - 1) + c // 2 + 1 + CR_TWO)
            for a in range(2):
                src = d["bc1"][bass.ds(b, 1), DS * a + CH * c:DS * a + CH * c + CH, :].rearrange("o n t -> o (n t)")
                sp.dma_start(flat(bc[:, a, CH * c:CH * c + CH, :]), src.to_broadcast([P, CH * L])).then_inc(bc_in[c], 16)

        for hf in range(2):
            sp.wait_ge(xT_ready, HTILES * hf + HTILES)
            for a in range(2):
                sp.dma_start(d["xT"][hf, a].rearrange("(k p) t -> p k t", p=P), xT[:, a]).then_inc(xT_out, 16)
        sp.wait_ge(sel_ready, 1)
        sp.dma_start(d["sel"], topi[0:1, :]).then_inc(sel_out, 16)
        sp.wait_ge(xT_out, 64)
        sp.wait_ge(sel_out, 16)
        end_phase(sp, 3)

        with sp.Fori(0, 2) as hf:
            sp.wait_ge(up_done, 64 * hf + CR_UP)
            for a in range(2):
                sp.dma_start(xT[:, a], d["xT"][bass.ds(hf, 1), a].rearrange("o (k p) t -> p (o k) t", p=P)).then_inc(xT_in, 16)
            with sp.Fori(0, 2) as i:
                e = sp.value_load(d["sel"][0:1, bass.ds(i, 1)], min_val=0, max_val=E - 1)
                j = 2 * hf + i
                sp.wait_ge(hid_lo, 32 * j + CR_TWO)
                sp.dma_start(b1s[:, :], d["b1"][bass.ds(e, 1)].rearrange("o p f -> p (o f)")).then_inc(b1_in, 16)
                sp.dma_start(b2b, d["b2"][bass.ds(e, 1)].to_broadcast([P, DM])).then_inc(b2_in, 16)
                for k in range(NG):
                    w = 4 * j + k
                    unit_load(j, k)
                    sp.wait_ge(w2_lo, w + CR_ONE)
                    sp.dma_start(stage, d["w1"][bass.ds(e, 1), :, k * FG:k * FG + FG].rearrange("o (k p) f -> p (o k) f", p=P)).then_inc(w1_in, 16)
                    if k == 0:
                        bc_load(j, 0)
                        bc_load(j, 1)
                    sp.wait_ge(w1_lo, w + 1 + CR_ONE)
                    sp.dma_start(stage, d["w2"][bass.ds(e, 1), k * FG:k * FG + FG].rearrange("o (k p) f -> p (o k) f", p=P)).then_inc(w2_in, 16)
                    if k == 0:
                        bc_load(j, 2)
                        bc_load(j, 3)
                    sp.wait_ge(st_free[1][1], 2 * w + CR_ST)
                    sp.dma_start(one(d["y1"][bass.ds(w, 1)].rearrange("o p t -> p o t")), yt[:, (k - 1) % 2, :]).then_inc(y1_out[(k - 1) % 2], 16)
        sp.wait_ge(st_free[1][1], 2 * NB * ET + CR_ST)
        sp.dma_start(d["y1"][NB * ET], yt[:, 1, :]).then_inc(y1_out[1], 16)
        sp.wait_ge(y1_out[0], 16 * 8 + CR_ONE)
        sp.wait_ge(y1_out[1], 16 * 9 + CR_ONE)
        end_phase(sp, 4)

        with sp.Fori(0, NB) as b:
            sp.wait_ge(g_added, ET * b + CR_BANK)
            sp.dma_start(y1b, d["y1"][bass.ds(ET * b + 1, ET)].rearrange("e p t -> p e t")).then_inc(y1_in, 16)
        end_phase(sp, 5)

        with sp.Fori(0, 2) as hf:
            for g in range(NG):
                w = NG * hf + g
                sp.wait_ge(cw_lo, w + CR_ONE)
                sp.dma_start(stage, d["W1T"][:, g * FG:g * FG + FG].rearrange("(k p) f -> p k f", p=P)).then_inc(cw_in, 16)
                sp.dma_start(stage3, d["W3T"][:, g * FG:g * FG + FG].rearrange("(k p) f -> p k f", p=P)).then_inc(cw_in, 16)
                sp.wait_ge(c_down, 8 * w + CR_DOWN)
                for a in range(2):
                    sp.dma_start(w2g[:, a], d["w2h"][a, g * FG:g * FG + FG].rearrange("(k p) f -> p k f", p=P)).then_inc(cw2_in, 16)
        sp.wait_ge(c_evac, 64 + CR_EV)
        sp.dma_start(d["out"].rearrange("(t p) d -> p t d", p=P), x_sb[:, :, :]).then_inc(out_sem, 16)
        sp.wait_ge(out_sem, 16)

    @block.tensor
    def _(pe):
        mm = nc.tensor.matmul
        pe.wait_ge(dma_ctx, 16)

        def in_proj(b):
            for et in range(ET):
                pe.wait_ge(conv[0], ET * b + et + 1)
                for k in range(KC):
                    last = mm(bank[et][:, :], inw[:, k, et * P:et * P + P], ctxT[:, k, bass.ds(b * L, L)],
                              start=(k == 0), stop=(k == KC - 1))
                last.then_inc(xin[0], 1)

        def x_proj(b):
            pe.wait_ge(soft[0], b + CR_ONE)
            for k in range(ET):
                pe.wait_ge(u_ready[0], ET * b + k + 1)
                last = mm(bank[4][0:48, :], xpw[:, k, :], u_of(b, k), start=(k == 0), stop=(k == ET - 1))
            last.then_inc(xdbl[0], 1)

        def dt_proj(b):
            pe.wait_ge(xd_ready[0], b + 1)
            for et in range(ET):
                mm(bank[4 + et][:, :], dtw[32:48, et * P:et * P + P], xd[32:48, :], start=True, stop=True).then_inc(dtraw[0], 1)

        pe.wait_ge(dma_w[0], 48)
        in_proj(0)
        with pe.Fori(0, NB - 1) as b:
            x_proj(b)
            in_proj(b + 1)
            dt_proj(b)
        x_proj(NB - 1)
        dt_proj(NB - 1)
        pe.wait_ge(dma_had, 32)
        pe.wait_ge(butterfly, 1)
        pe.wait_ge(conv[0], ET * NB + CR_BANK)
        for h in range(16):
            if h >= 4:
                pe.wait_ge(had_lo, h - 3)
            mm(bank[h % 4][:, :], hd, wv[:, h, :], start=True, stop=True).then_inc(had_mm, 1)
        end_phase(pe, 1)

        def turn(bk, src, done):
            for k in range(4):
                last = nc.tensor.transpose(bk[:, k * P:k * P + P], src[:, k * P:k * P + P], ident[:, :])
            last.then_inc(done, 1)

        def reduce_chunk(b, et, c):
            pe.wait_ge(a_p, NC * (ET * b + et) + c + 1 + CR_RING)
            for n in range(CH):
                last = mm(bank[et % 2][:, :], ident[:, :], stA(c)[:, n, :], start=(c == 0 and n == 0), stop=(c == NC - 1 and n == CH - 1))
            last.then_inc(a_summed, 1)

        def turn_unit(b, et):
            pe.wait_ge(y_gated, ET * b + et + 1 + CR_TWO)
            pe.wait_ge(y_added, ET * b + et - 2 + 1 + CR_TWO)
            turn(bank[2 + et % 2], yt[:, et % 2, :], y_turned)

        def in_proj1(b):
            pe.wait_ge(ctx_in, 16 * b + 16)
            for et in range(ET):
                pe.wait_ge(soft[1], 2 * (b - 1) + et // 2 + 1 + CR_TWO)
                for k in range(KC):
                    last = mm(bank[4 + et][:, :], inw[:, k, et * P:et * P + P], ctxb[:, k, :], start=(k == 0), stop=(k == KC - 1))
                last.then_inc(xin[1], 1)

        def x_proj1(b):
            pe.wait_ge(conv[1], ET * b + 1 + CR_BANK)
            for k in range(ET):
                pe.wait_ge(u_ready[1], ET * b + k + 1)
                last = mm(bank[4][0:48, :], xpw[:, k, :], u1[:, k, :], start=(k == 0), stop=(k == ET - 1))
            last.then_inc(xdbl[1], 1)

        def dt_proj1(b):
            pe.wait_ge(xd_ready[1], b + 1)
            for et in range(ET):
                mm(bank[4 + et][:, :], dtw[32:48, et * P:et * P + P], xd[32:48, :], start=True, stop=True).then_inc(dtraw[1], 1)

        def scan_sums(b, first):
            for et in range(ET):
                pe.wait_ge(unit_done, ET * b + et - 2 + 1 + CR_TWO)
                if et == 0:
                    in_proj1(b)
                reduce_chunk(b, et, 0)
                reduce_chunk(b, et, 1)
                if et:
                    turn_unit(b, et - 1)
                elif not first:
                    turn_unit(b - 1, ET - 1)
                if et == 1:
                    x_proj1(b)
                reduce_chunk(b, et, 2)
                reduce_chunk(b, et, 3)
                if et == 1:
                    dt_proj1(b)

        pe.wait_ge(dma_w[1], 48)
        scan_sums(0, True)
        with pe.Fori(0, NB - 1) as b:
            scan_sums(b + 1, False)
        turn_unit(NB - 1, ET - 1)
        end_phase(pe, 2)

        for t in range(TILES):
            pe.wait_ge(ln_done, 4 + t // TT + 1)
            if t >= 2:
                pe.wait_ge(xT_ready, t - 1)
            turn(bank[4 + t % 2], st[:, (t // TT) % 2, t % TT, :], xn_turned)
            pe.wait_ge(xT_f32, t + 1)
            for k in range(KD):
                last = mm(bank[6][:, t * E:t * E + E], xTf[:, t % 2, k, :], gwT[:, k, :],
                          start=(k == 0), stop=(k == KD - 1))
            last.then_inc(logit_mm, 1)
        pe.wait_ge(lsum_in, 1)
        mm(bank[7][:, 0:E], ones, lsum[:, :], start=True, stop=True).then_inc(lsum_mm, 1)
        end_phase(pe, 3)

        def mm3(out, wt, tok, first, last_k):
            for m, (a, b) in enumerate(((0, 0), (0, 1), (1, 0))):
                ins = mm(out, wt[a], tok[b], start=(first and m == 0), stop=(last_k and m == 2))
            return ins

        with pe.Fori(0, 2) as hf:
            pe.wait_ge(xT_in, 32 * hf + 32)
            hold(pe)
            with pe.Fori(0, 2) as i:
                for k in range(NG):
                    w = 4 * (2 * hf + i) + k
                    pe.wait_ge(w1_lo, w + 1 + CR_ONE)
                    for g in range(2):
                        for f in range(FT):
                            pe.wait_ge(h_full, 8 * w + 4 * g + f - 4 + 1 + CR_HID)
                            for kd in range(KD):
                                last = mm3(bank[f][:, :], [w1g[:, a, kd, f * P:f * P + P] for a in range(2)],
                                           [xT[:, a, kd, g * L:g * L + L] for a in range(2)], kd == 0, kd == KD - 1)
                            last.then_inc(up_done, 1)
                    pe.wait_ge(w2_lo, w + 1 + CR_ONE)
                    for g in range(2):
                        pe.wait_ge(hid_lo, 8 * w + 4 * g + FT + CR_TWO)
                        for t in range(TT):
                            pe.wait_ge(evac_done, 8 * w + 4 * g + t - 4 + 1 + CR_EV)
                            for f in range(FT):
                                last = mm3(bank[4 + t][:, :], [hT[:, a, g, f, t * P:t * P + P] for a in range(2)],
                                           [w2g[:, a, f, :] for a in range(2)], f == 0, f == FT - 1)
                            last.then_inc(down_done, 1)
        end_phase(pe, 4)

        with pe.Fori(0, NB) as b:
            pe.wait_ge(g_gated, b + 1)
            for et in range(ET):
                pe.wait_ge(g_added, ET * b + et - 4 + 1 + CR_BANK)
                turn(bank[et], st[:, 1, et, :], g_turned)
            pe.wait_ge(g_norm, 2 * b + 2)
            for t in range(TT):
                pe.wait_ge(g_xT, TT * b + t - 4 + 1 + CR_BANK)
                turn(bank[4 + t], st[:, 0, t, :], g_xturned)
        end_phase(pe, 5)

        with pe.Fori(0, 2) as hf:
            for gi in range(NG):
                w = NG * hf + gi
                pe.wait_ge(cw_lo, w + 1 + CR_ONE)
                for g in range(2):
                    for f in range(FT):
                        pe.wait_ge(c_full, 8 * w + 4 * g + f - 2 + 1 + CR_TWO)
                        for m, wt in enumerate((w1g, w3g)):
                            for kd in range(KD):
                                tok = [xT1[:, a, kd, bass.ds(hf * HTOK + g * L, L)] for a in range(2)]
                                last = mm3(bank[2 * m + f % 2][:, :], [wt[:, a, kd, f * P:f * P + P] for a in range(2)],
                                           tok, kd == 0, kd == KD - 1)
                        last.then_inc(c_up, 1)
                pe.wait_ge(cw2_in, 32 * w + 32)
                for g in range(2):
                    pe.wait_ge(c_lo, 8 * w + 4 * g + FT + CR_TWO)
                    for t in range(TT):
                        pe.wait_ge(c_evac, 8 * w + 4 * g + t - 4 + 1 + CR_EV)
                        for f in range(FT):
                            last = mm3(bank[4 + t][:, :], [hT[:, a, g, f, t * P:t * P + P] for a in range(2)],
                                       [w2g[:, a, f, :] for a in range(2)], f == 0, f == FT - 1)
                        last.then_inc(c_down, 1)

    @block.scalar
    def _(act):
        A = nc.scalar.activation
        own = Chain(act, act_own)
        act.wait_ge(dma_par, 16 * 6)
        A(gates[:, :], gates[:, :], ACT.Tanh).then_inc(gates_ready, 1)
        for l in range(2):
            own.link(A(negA[l][:, :, :], par[l][:, :, P_AL:], ACT.Exp))
            own.step(A(negA[l][:, :, :], negA[l][:, :, :], ACT.Copy, scale=-1.0))
        act.wait_ge(consts_ready, 1)

        def std(stats, done, n):
            act.wait_ge(stats, n)
            A(rstd[:, :], mv[:, :, 1], ACT.Sqrt, bias=epsc[:, 0:1]).then_inc(done, 1)

        def last_taps(b):
            for et in range(ET):
                act.wait_ge(xin[0], ET * b + et + 1)
                A(u_of(b, et), bank[et][:, :], ACT.Identity, bias=par[0][:, et, P_CB:P_CB + 1],
                  scale=par[0][:, et, P_W + TAPS - 1:P_W + TAPS]).then_inc(tap_last[0], 1)

        def silu_u(b):
            for et in range(ET):
                act.wait_ge(conv[0], ET * b + et + 1 + CR_BANK)
                hold(act)
                A(u_of(b, et), u_of(b, et), ACT.Silu).then_inc(u_ready[0], 1)

        def silu_z(b):
            act.wait_ge(ln_done, b + 1)
            A(flat(zg), flat(zg), ACT.Silu).then_inc(z_ready, 1)

        def copy_xd(b):
            act.wait_ge(xdbl[0], b + 1)
            act.wait_ge(xd_out[0], 16 * b + CR_ONE)
            A(xd[0:48, :], bank[4][0:48, :], ACT.Copy).then_inc(xd_ready[0], 1)

        def softplus(b):
            act.wait_ge(prep_ready[0], b + CR_ONE)
            for et in range(ET):
                act.wait_ge(dtraw[0], ET * b + et + 1)
                A(r4[:, et, :], bank[4 + et][:, :], ACT.Relu, bias=par[0][:, et, P_DB:P_DB + 1])
                ab = A(e4[:, et, :], bank[4 + et][:, :], ACT.Abs, bias=par[0][:, et, P_DB:P_DB + 1])
            own.link(ab)
            own.link(A(e4, e4, ACT.Exp, scale=-1.0))
            act.wait_ge(dd_out, 32 * b + CR_ONE)
            A(l4, e4, ACT.Ln, bias=onec[:, 0:1]).then_inc(soft[0], 1)

        last_taps(0)
        silu_u(0)
        with act.Fori(0, NB - 1) as b:
            own.enter(b, 2)
            copy_xd(b)
            std(ln_stats, ln_std, b + 1)
            act.wait_ge(u_out[0], 16 * b + CR_ONE)
            act.wait_ge(prep_ready[0], b + CR_ONE)
            last_taps(b + 1)
            softplus(b)
            silu_u(b + 1)
            silu_z(b)
            own.leave(2, NB - 1)
        copy_xd(NB - 1)
        std(ln_stats, ln_std, NB)
        softplus(NB - 1)
        silu_z(NB - 1)
        for h in range(16):
            act.wait_ge(had_mm, h + 1)
            if h >= 8 and h % 4 == 0:
                act.wait_ge(had_out[h // 4 % 2], 32 + CR_ONE)
            A(w2s[:, h // 4 % 2, h % 4, 0], bank[h % 4][:, :], ACT.Copy, scale=N_SCALE).then_inc(had_hi, 1)
        end_phase(act, 1)

        def exp_chunk(slot, delta, l, et, c):
            for n in range(CH):
                last = A(dA[:, slot, n, 1:], delta, ACT.Exp, scale=negA[l][:, et, CH * c + n:CH * c + n + 1])
            return last

        def exps0(b, et, c):
            if c == 0:
                act.wait_ge(pt_in[0][et % 2], 16 * (2 * b + et // 2) + 16)
            act.wait_ge(a_scan, NC * (ET * b + et) + c - 2 + 1 + CR_TWO)
            exp_chunk(c % 2, pt[:, et % 2, 1, 1:], 0, et, c).then_inc(a_exp, 1)

        def exps(b, et, c):
            s, m = c % 2, 8 * b + 2 * et + c // 2
            if c == 0:
                act.wait_ge(pt_in[1][et % 2], 16 * (2 * b + et // 2) + 16)
            act.wait_ge(dA_free[1][s], m + CR_ONE)
            exp_chunk(s, pt[:, et % 2, 1, 1:], 1, et, c).then_inc(dA_ready[1][s], 1)

        def last_taps1(b):
            act.wait_ge(u_out[1], 16 * b + CR_ONE)
            act.wait_ge(prep_ready[1], 2 * b + CR_TWO)
            for et in range(ET):
                act.wait_ge(xin[1], ET * b + et + 1)
                A(u1[:, et, :], bank[4 + et][:, :], ACT.Identity, bias=par[1][:, et, P_CB:P_CB + 1],
                  scale=par[1][:, et, P_W + TAPS - 1:P_W + TAPS]).then_inc(tap_last[1], 1)

        def silu1(b):
            for et in range(ET):
                act.wait_ge(conv[1], ET * b + et + 1 + CR_BANK)
                A(u1[:, et, :], u1[:, et, :], ACT.Silu).then_inc(u_ready[1], 1)

        def soft1(b, h):
            act.wait_ge(prep_ready[1], 2 * b + h + CR_TWO)
            act.wait_ge(dd1_out[h], 32 * b + CR_ONE)
            for s in range(2):
                et = 2 * h + s
                act.wait_ge(dtraw[1], ET * b + et + 1)
                A(r1[:, s, :], bank[4 + et][:, :], ACT.Relu, bias=par[1][:, et, P_DB:P_DB + 1])
                ab = A(e1[:, h, s, :], bank[4 + et][:, :], ACT.Abs, bias=par[1][:, et, P_DB:P_DB + 1])
            own.link(ab)
            own.link(A(flat(e1[:, h]), flat(e1[:, h]), ACT.Exp, scale=-1.0))
            A(flat(l1[:, h]), flat(e1[:, h]), ACT.Ln, bias=onec[:, 0:1]).then_inc(soft[1], 1)

        act.wait_ge(dA_zero, 1)
        with act.Fori(0, NB) as b:
            own.enter(b, 4)
            for et in range(ET):
                exps0(b, et, 0)
                if et == 1:
                    silu1(b)
                if et == 2:
                    act.wait_ge(xdbl[1], b + 1)
                    act.wait_ge(xd_out[1], 16 * b + CR_ONE)
                    A(xd[0:48, :], bank[4][0:48, :], ACT.Copy).then_inc(xd_ready[1], 1)
                if et == 3:
                    soft1(b, 1)
                exps0(b, et, 1)
                exps0(b, et, 2)
                if et == 0:
                    last_taps1(b)
                if et == 2:
                    soft1(b, 0)
                exps0(b, et, 3)
            act.wait_ge(prep_ready[1], 2 * b + 2 + CR_TWO)
            for a, part in enumerate((l1[:, 1], e1[:, 1])):
                act.dma_start(d["prep1"][bass.ds(b, 1), 1 + a, 2:4].rearrange("o e p t -> p (o e) t"), part).then_inc(dd1_out[1], 16)
            own.leave(4, NB)
        end_phase(act, 2)

        for g in range(NB):
            std(ln_stats, ln_std, NB + g + 1)
            for t in range(TT * g, TT * g + TT):
                if t == HTILES:
                    act.wait_ge(xT_out, 32)
                act.wait_ge(xn_turned, t + 1)
                o = (t % HTILES) * P
                turned = bank[4 + t % 2][:, :].rearrange("p (k t) -> p k t", k=KD)
                A(xT[:, 0, :, o:o + P], turned, ACT.Copy).then_inc(xT_hi, 1)
                if t >= 2:
                    act.wait_ge(logit_mm, t - 1)
                A(xTf[:, t % 2], turned, ACT.Copy).then_inc(xT_f32, 1)
        act.wait_ge(rt_in, 1)
        A(lexp[:, :, :], lsel[:, :, :], ACT.Exp).then_inc(rt_exp, 1)
        end_phase(act, 3)

        def gelu(w, k, g, f):
            n = 8 * w + 4 * g + f
            act.wait_ge(up_done, n + 1 + CR_UP)
            act.wait_ge(hid_lo, n - 2 + 1 + CR_TWO)
            A(h32[:, f % 2], bank[f][:, :], ACT.Gelu_apprx_tanh, bias=b1s[:, k * FT + f:k * FT + f + 1], scale=1 / (S_X * S_W)).then_inc(h_full, 1)
            if f == 0:
                act.wait_ge(down_done, 8 * w + 4 * g + 4 - 8 + CR_DOWN)
            act.wait_ge(h_full, n + 1 + CR_HID)
            A(hT[:, 0, g, f, :], h32[:, f % 2], ACT.Copy, scale=S_H).then_inc(hid_hi, 1)

        def split_hi(arrived, n, dst, src, used, n_used, done):
            act.wait_ge(arrived, n)
            act.wait_ge(used, n_used)
            A(dst.rearrange("p k f -> p (k f)"), src.rearrange("p k f -> p (k f)"), ACT.Copy, scale=S_W).then_inc(done, 1)

        with act.Fori(0, 2) as hf:
            with act.Fori(0, 2) as i:
                j = 2 * hf + i
                act.wait_ge(b1_in, 16 * j + 16)
                act.wait_ge(b2_used, j + 1 + CR_ONE)
                for k in range(NG):
                    w = 4 * j + k
                    if k == 0:
                        split_hi(w1_in, 16 * w + 16, w1g[:, 0], stage, up_done, 8 * w + CR_UP, w1_hi)
                    exps(j, k, 0)
                    exps(j, k, 1)
                    split_hi(w2_in, 16 * w + 16, w2g[:, 0], stage, down_done, 8 * w + CR_DOWN, w2_hi)
                    for g in range(2):
                        for f in range(FT):
                            gelu(w, k, g, f)
                    if k < NG - 1:
                        split_hi(w1_in, 16 * w + 32, w1g[:, 0], stage, up_done, 8 * w + 8 + CR_UP, w1_hi)
                    exps(j, k, 2)
                    exps(j, k, 3)
        end_phase(act, 4)

        with act.Fori(0, NB) as b:
            std(g_stats, g_std, 2 * b + 1)
            act.wait_ge(g_norm, 2 * b + 1)
            A(flat(st[:, 1]), flat(st[:, 1]), ACT.Silu).then_inc(g_z, 1)
            std(g_stats, g_std, 2 * b + 2)
            for t in range(TT):
                act.wait_ge(g_xturned, TT * b + t + 1)
                A(xT1[:, 0, :, bass.ds(b * L + t * P, P)], bank[4 + t][:, :].rearrange("p (k t) -> p k t", k=KD), ACT.Copy).then_inc(g_xhi, 1)
        end_phase(act, 5)

        with act.Fori(0, 2) as hf:
            for gi in range(NG):
                w = NG * hf + gi
                act.wait_ge(cw_in, 32 * w + 32)
                act.wait_ge(c_up, 8 * w + CR_UP)
                A(w1g[:, 0].rearrange("p k f -> p (k f)"), stage.rearrange("p k f -> p (k f)"), ACT.Copy, scale=S_W)
                A(w3g[:, 0].rearrange("p k f -> p (k f)"), stage3.rearrange("p k f -> p (k f)"), ACT.Copy, scale=S_W).then_inc(cw_hi, 1)

                def hi(n, g, f):
                    act.wait_ge(c_full, n + 1 + CR_TWO)
                    A(hT[:, 0, g, f, :], h32[:, f % 2], ACT.Copy).then_inc(c_hi, 1)

                for g in range(2):
                    for f in range(FT):
                        n = 8 * w + 4 * g + f
                        act.wait_ge(c_up, n + 1 + CR_UP)
                        act.wait_ge(c_full, n - 2 + 1 + CR_TWO)
                        A(sg[:, f % 2, :], bank[f % 2][:, :], ACT.Silu, scale=1 / (S_X * S_W)).then_inc(c_sg, 1)
                        if f == 0:
                            act.wait_ge(c_down, 8 * w + 4 * g + 4 - 8 + CR_DOWN)
                        hi(n, g, f)

    @block.vector
    def _(dve):
        V = nc.vector
        own = Chain(dve, dve_own)
        V.memset(yt[:, :, :], 0.0)
        V.memset(onec[:, :], 1.0)
        V.memset(epsc[:, :], EPS).then_inc(consts_ready, 1)
        dve.wait_ge(dma_par, 16 * 6)

        def norm(tile_ap, dst, stats, std_done, done, n, scale=1.0):
            for t in range(TT):
                ins = V.bn_stats(bnst[:, t, :], tile_ap(t))
            own.link(ins)
            hold(dve)
            for t in range(TT):
                ins = V.bn_aggr(mv[:, t, :], bnst[:, t, :])
            ins.then_inc(stats, 1)
            dve.wait_ge(std_done, n)
            own.link(V.reciprocal(rstd[:, :], rstd[:, :]))
            if scale != 1.0:
                own.link(V.tensor_scalar(rstd[:, :], rstd[:, :], scale, None, ALU.mult))
            for t in range(TT):
                ins = V.tensor_scalar(dst(t), tile_ap(t), mv[:, t, 0:1], rstd[:, t:t + 1], ALU.subtract, ALU.mult)
            ins.then_inc(done, 1)

        def taps(u, l, first, done):
            for tap in range(1, TAPS):
                for et in range(ET):
                    if tap == 1:
                        dve.wait_ge(tap_last[l], first + et + 1)
                    o = u(et, tap)
                    ins = V.scalar_tensor_tensor(out=o, in0=bank[4 * l + et][:, 0:L - tap], scalar=par[l][:, et, P_W + TAPS - 1 - tap:P_W + TAPS - tap],
                                                 in1=o, op0=ALU.mult, op1=ALU.add)
                    if tap == TAPS - 1:
                        ins.then_inc(done, 1)
                if tap < TAPS - 1:
                    own.link(ins)

        def convolve(b):
            taps(lambda et, tap: u4[:, bass.ds(b % 2, 1), et, tap:].rearrange("p o t -> p (o t)"), 0, ET * b, conv[0])

        def delta(ef, rf, lf, qf, u, done):
            own.link(V.tensor_tensor(lf, lf, rf, ALU.add))
            own.link(V.tensor_scalar(rf, ef, 1.0, 1.0, ALU.add, ALU.subtract))
            own.link(V.tensor_tensor(rf, ef, rf, ALU.subtract))
            own.link(V.tensor_tensor(lf, lf, rf, ALU.add))
            V.tensor_tensor(qf, lf, u, ALU.mult).then_inc(done, 1)

        def delta0(b):
            dve.wait_ge(soft[0], b + 1 + CR_ONE)
            delta(flat(e4), flat(r4), flat(l4), flat(q4), u4[:, bass.ds(b % 2, 1)].rearrange("p o e t -> p (o e t)"), prep_ready[0])

        def delta1(b, h):
            dve.wait_ge(soft[1], 2 * b + h + 1 + CR_TWO)
            delta(*(flat(x) for x in (e1[:, h], r1, l1[:, h], e1[:, h])), flat(u1[:, 2 * h:2 * h + 2, :]), prep_ready[1])

        def norm_z(b):
            dve.wait_ge(z_out, 16 * b + CR_ONE)
            hold(dve)
            norm(lambda t: tile_of(TT * b + t), lambda t: zg[:, t, :], ln_stats, ln_std, ln_done, b + 1)

        convolve(0)
        dve.wait_ge(dma_x, 16)
        with dve.Fori(0, NB - 1) as b:
            own.enter(b, 8)
            norm_z(b)
            convolve(b + 1)
            delta0(b)
            own.leave(8, NB - 1)
        norm_z(NB - 1)
        delta0(NB - 1)
        for h in range(16):
            dve.wait_ge(had_hi, h + 1)
            V.scalar_tensor_tensor(out=w2s[:, h // 4 % 2, h % 4, 1], in0=bank[h % 4][:, :], scalar=N_SCALE, in1=w2s[:, h // 4 % 2, h % 4, 0],
                                   op0=ALU.mult, op1=ALU.subtract).then_inc(had_lo, 1)
        end_phase(dve, 1)

        def scan0(b, et, c):
            n = NC * (ET * b + et) + c
            dve.wait_ge(a_exp, n + 1 + CR_RING)
            dve.wait_ge(a_bx, n + 1 + CR_RING)
            V.tensor_tensor_scan(flat(stA(c)), flat(dA[:, c % 2]), flat(stA(c)), 0.0, ALU.mult, ALU.add).then_inc(a_scan, 1)
            if et == 0:
                dve.wait_ge(a_c_in[c], 16 * b + 16)
            dve.wait_ge(a_scan, n + 1 + CR_TWO)
            V.tensor_tensor(stA(c), stA(c), bc[:, 1, CH * c:CH * c + CH, :], ALU.mult).then_inc(a_p, 1)

        def scan(b, et, c):
            s, m = c % 2, 8 * b + 2 * et + c // 2
            dve.wait_ge(dA_ready[1][s], m + 1)
            dve.wait_ge(bx_ready[1][s], m + 1)
            V.tensor_tensor_scan(flat(st[:, s]), flat(dA[:, s]), flat(st[:, s]), 0.0, ALU.mult, ALU.add).then_inc(dA_free[1][s], 1)

        def times_c(b, et, c):
            s, m = c % 2, 8 * b + 2 * et + c // 2
            dve.wait_ge(dA_free[1][s], m + 1 + CR_ONE)
            V.tensor_tensor(st[:, s], st[:, s], bc[:, 1, CH * c:CH * c + CH, :], ALU.mult).then_inc(p_ready[1][s], 1)

        dve.wait_ge(gates_ready, 1)

        def gate_unit(b, et):
            s, u = et % 2, ET * b + et
            dve.wait_ge(uz_in[s], 32 * (2 * b + et // 2) + 32)
            dve.wait_ge(a_summed, NC * u + NC + CR_RING)
            V.scalar_tensor_tensor(out=yt[:, s, :], in0=pt[:, s, 0, :], scalar=par[0][:, et, P_D:P_D + 1], in1=bank[s][:, :],
                                   op0=ALU.mult, op1=ALU.add).then_inc(unit_done, 1)
            dve.wait_ge(unit_done, u + 1 + CR_TWO)
            V.tensor_tensor(yt[:, s, :], yt[:, s, :], zt[:, s, :], ALU.mult).then_inc(y_gated, 1)

        def add_unit(b, et):
            dve.wait_ge(y_turned, ET * b + et + 1)
            xs = x_sb[:, bass.ds(TT * b, TT), et * P:et * P + P]
            V.scalar_tensor_tensor(out=xs, in0=bank[2 + et % 2][:, :].rearrange("p (t e) -> p t e", t=TT), scalar=gates[:, 0:1],
                                   in1=xs, op0=ALU.mult, op1=ALU.add).then_inc(y_added, 1)

        def scan_batch(b, first):
            for et in range(ET):
                before = (b, et - 1) if et else (b - 1, ET - 1)
                scan0(b, et, 0)
                scan0(b, et, 1)
                if et or not first:
                    gate_unit(*before)
                if et == 3:
                    delta1(b, 1)
                scan0(b, et, 2)
                if et or not first:
                    add_unit(*before)
                if et == 0:
                    taps(lambda et, tap: u1[:, et, tap:], 1, ET * b, conv[1])
                scan0(b, et, 3)
                if et == 2:
                    delta1(b, 0)

        own.enter(0, 2 + 2 * 4)
        scan_batch(0, True)
        own.leave(2 + 2 * 4, 1)
        with dve.Fori(0, NB - 1) as b:
            own.enter(b, 2 + 2 * 4)
            scan_batch(b + 1, False)
            own.leave(2 + 2 * 4, NB - 1)
        gate_unit(NB - 1, ET - 1)
        add_unit(NB - 1, ET - 1)
        end_phase(dve, 2)
        V.memset(ones, 1.0)

        for g in range(NB):
            if g >= 2:
                dve.wait_ge(xn_turned, TT * (g - 1))
            norm(lambda t: x_sb[:, TT * g + t, :], lambda t: st[:, g % 2, t, :], ln_stats, ln_std, ln_done, NB + g + 1, S_X)
            for t in range(TT * g, TT * g + TT):
                o = (t % HTILES) * P
                dve.wait_ge(xT_hi, t + 1)
                dve.wait_ge(xT_f32, t + 1)
                V.tensor_tensor(xT[:, 1, :, o:o + P], bank[4 + t % 2][:, :].rearrange("p (k t) -> p k t", k=KD), xT[:, 0, :, o:o + P],
                                ALU.subtract).then_inc(xT_ready, 1)
        dve.wait_ge(logit_mm, TILES)
        own.link(V.tensor_scalar(logit[:, :, :], bank[6][:, 0:TILES * E].rearrange("p (t e) -> p t e", e=E), 1 / S_X, None, ALU.mult))
        V.tensor_reduce(out=lsum[:, :], in_=logit[:, :, :].rearrange("p t e -> p e t"), axis=AX.X, op=ALU.add).then_inc(lsum_in, 1)
        dve.wait_ge(lsum_mm, 1)
        own.link(V.tensor_copy(lsum[:, :], bank[7][:, 0:E]))
        own.link(V.max(top[:, :], lsum[:, :]))
        V.max_index(topi[:, :], top[:, :], lsum[:, :]).then_inc(sel_ready, 1)
        dve.wait_ge(sel_ready, 1)
        own.link(V.tensor_copy(topf[:, :], topi[:, :]))
        for k in range(2):
            ins = V.tensor_scalar(hot[:, k, :], iota[:, :], topf[:, k:k + 1], None, ALU.is_equal)
        own.link(ins)
        for k in range(2):
            own.link(V.tensor_tensor(lwork[:, :, :], logit[:, :, :], hot[:, k:k + 1, :].to_broadcast([P, TILES, E]), ALU.mult))
            own.link(V.tensor_reduce(out=lsel[:, k, :], in_=lwork[:, :, :], axis=AX.X, op=ALU.add))
        own.link(V.tensor_tensor(lmax[:, :], lsel[:, 0, :], lsel[:, 1, :], ALU.max))
        for k in range(2):
            ins = V.tensor_tensor(lsel[:, k, :], lsel[:, k, :], lmax[:, :], ALU.subtract)
        ins.then_inc(rt_in, 1)
        dve.wait_ge(rt_exp, 1)
        own.link(V.tensor_tensor(lmax[:, :], lexp[:, 0, :], lexp[:, 1, :], ALU.add))
        own.link(V.reciprocal(lmax[:, :], lmax[:, :]))
        for k in range(2):
            ins = V.tensor_tensor(lexp[:, k, :], lexp[:, k, :], lmax[:, :], ALU.mult)
        own.link(ins)
        for k in range(2):
            own.link(V.tensor_scalar(cbias[:, :, k, :], lexp[:, k, :].rearrange("p (h t) -> p h t", h=2), gates[:, 2:3], None, ALU.mult))
            ins = V.tensor_scalar(coef[:, :, k, :], cbias[:, :, k, :], 1 / (S_H * S_W), None, ALU.mult)
        V.tensor_scalar(down1[:, :], gates[:, 3:4], 1 / (S_H * S_W), None, ALU.mult)
        end_phase(dve, 3)

        def b_times(b, et, c):
            s, m = c % 2, 8 * b + 2 * et + c // 2
            if c == 0:
                dve.wait_ge(pt_in[1][et % 2], 16 * (2 * b + et // 2) + 16)
            if et == 0:
                dve.wait_ge(bc_in[c], 32 * b + 32)
            dve.wait_ge(st_free[1][s], m + CR_ST)
            V.tensor_tensor(st[:, s], pt[:, et % 2, 2:3, :].to_broadcast([P, CH, L]), bc[:, 0, CH * c:CH * c + CH, :],
                            ALU.mult).then_inc(bx_ready[1][s], 1)

        with dve.Fori(0, 2) as hf:
            with dve.Fori(0, 2) as i:
                j = 2 * hf + i

                def cf(t, src=coef):
                    return src[:, bass.ds(hf, 1), bass.ds(i, 1), t].rearrange("p a b -> p (a b)")

                def lo_hidden(w, g, f):
                    dve.wait_ge(hid_hi, 8 * w + 4 * g + f + 1)
                    V.scalar_tensor_tensor(out=hT[:, 1, g, f, :], in0=h32[:, f % 2], scalar=S_H, in1=hT[:, 0, g, f, :],
                                           op0=ALU.mult, op1=ALU.subtract).then_inc(hid_lo, 1)

                def lo_weights(hi, n, dst, done):
                    dve.wait_ge(hi, n)
                    f2 = lambda ap: ap.rearrange("p k f -> p (k f)")
                    V.scalar_tensor_tensor(out=f2(dst[:, 1]), in0=f2(stage), scalar=S_W, in1=f2(dst[:, 0]),
                                           op0=ALU.mult, op1=ALU.subtract).then_inc(done, 1)

                def evac(w, t):
                    dve.wait_ge(down_done, 8 * w + t + 1 + CR_DOWN)
                    dve.wait_ge(evac_done, 8 * w + t + 1 - 8 + CR_EV)
                    xt = tile_of(HTILES * hf + t)
                    V.scalar_tensor_tensor(out=xt, in0=bank[4 + t % 4][:, :], scalar=cf(t), in1=xt, op0=ALU.mult, op1=ALU.add).then_inc(evac_done, 1)

                dve.wait_ge(b2_in, 16 * j + 16)
                dve.wait_ge(evac_done, 32 * j + CR_EV)
                for t in range(HTILES):
                    xt = tile_of(HTILES * hf + t)
                    ins = V.scalar_tensor_tensor(out=xt, in0=b2b, scalar=cf(t, cbias), in1=xt, op0=ALU.mult, op1=ALU.add)
                ins.then_inc(b2_used, 1)
                dve.wait_ge(b2_used, j + 1 + CR_ONE)
                for k in range(NG):
                    w = 4 * j + k
                    if k == 0:
                        lo_weights(w1_hi, w + 1, w1g, w1_lo)
                    b_times(j, k, 0)
                    scan(j, k, 0)
                    times_c(j, k, 0)
                    lo_weights(w2_hi, w + 1, w2g, w2_lo)
                    lo_hidden(w, 0, 0)
                    b_times(j, k, 1)
                    lo_hidden(w, 0, 1)
                    scan(j, k, 1)
                    lo_hidden(w, 0, 2)
                    times_c(j, k, 1)
                    lo_hidden(w, 0, 3)
                    lo_hidden(w, 1, 0)
                    lo_hidden(w, 1, 1)
                    lo_hidden(w, 1, 2)
                    lo_hidden(w, 1, 3)
                    if k < NG - 1:
                        lo_weights(w1_hi, w + 2, w1g, w1_lo)
                    b_times(j, k, 2)
                    evac(w, 0)
                    scan(j, k, 2)
                    evac(w, 1)
                    times_c(j, k, 2)
                    evac(w, 2)
                    b_times(j, k, 3)
                    evac(w, 3)
                    scan(j, k, 3)
                    evac(w, 4)
                    times_c(j, k, 3)
                    for t in range(5, 8):
                        evac(w, t)
        end_phase(dve, 4)

        with dve.Fori(0, NB) as b:
            own.enter(b, 5)
            mine = lambda t: tile_of(TT * b + t)
            norm(mine, lambda t: st[:, 1, t, :], g_stats, g_std, g_norm, 2 * b + 1)
            dve.wait_ge(g_z, b + 1)
            dve.wait_ge(y1_in, 16 * b + 16)
            V.tensor_tensor(flat(st[:, 1]), flat(st[:, 1]), y1b.rearrange("p e t -> p (e t)"), ALU.mult).then_inc(g_gated, 1)
            for et in range(ET):
                dve.wait_ge(g_turned, ET * b + et + 1)
                xs = x_sb[:, bass.ds(TT * b, TT), et * P:et * P + P]
                ins = V.scalar_tensor_tensor(out=xs, in0=bank[et][:, :].rearrange("p (t e) -> p t e", t=TT), scalar=gates[:, 1:2],
                                             in1=xs, op0=ALU.mult, op1=ALU.add).then_inc(g_added, 1)
            dve.wait_ge(g_added, ET * b + ET + CR_BANK)
            dve.wait_ge(g_xT, TT * b + CR_BANK)
            hold(dve)
            norm(mine, lambda t: st[:, 0, t, :], g_stats, g_std, g_norm, 2 * b + 2, S_X)
            for t in range(TT):
                dve.wait_ge(g_xhi, TT * b + t + 1)
                o = bass.ds(b * L + t * P, P)
                V.tensor_tensor(xT1[:, 1, :, o], bank[4 + t][:, :].rearrange("p (k t) -> p k t", k=KD), xT1[:, 0, :, o],
                                ALU.subtract).then_inc(g_xT, 1)
            own.leave(5, NB)
        end_phase(dve, 5)

        with dve.Fori(0, 2) as hf:
            for gi in range(NG):
                w = NG * hf + gi
                f2 = lambda ap: ap.rearrange("p k f -> p (k f)")
                dve.wait_ge(cw_hi, w + 1)
                for part, src in ((w1g, stage), (w3g, stage3)):
                    ins = V.scalar_tensor_tensor(out=f2(part[:, 1]), in0=f2(src), scalar=S_W, in1=f2(part[:, 0]),
                                                 op0=ALU.mult, op1=ALU.subtract)
                ins.then_inc(cw_lo, 1)
                for g in range(2):
                    for f in range(FT):
                        n = 8 * w + 4 * g + f
                        dve.wait_ge(c_sg, n + 1)
                        dve.wait_ge(c_lo, n - 2 + 1 + CR_TWO)
                        V.scalar_tensor_tensor(out=h32[:, f % 2], in0=bank[2 + f % 2][:, :], scalar=S_H / (S_X * S_W), in1=sg[:, f % 2, :],
                                               op0=ALU.mult, op1=ALU.mult).then_inc(c_full, 1)
                        dve.wait_ge(c_hi, n + 1)
                        V.tensor_tensor(hT[:, 1, g, f, :], h32[:, f % 2], hT[:, 0, g, f, :], ALU.subtract).then_inc(c_lo, 1)
                for t in range(HTILES):
                    n = 8 * w + t
                    dve.wait_ge(c_down, n + 1 + CR_DOWN)
                    dve.wait_ge(c_evac, n + 1 - 8 + CR_EV)
                    xt = tile_of(HTILES * hf + t)
                    V.scalar_tensor_tensor(out=xt, in0=bank[4 + t % 4][:, :], scalar=down1[:, 0:1], in1=xt, op0=ALU.mult, op1=ALU.add).then_inc(c_evac, 1)

    @block.gpsimd
    def _(gp):
        G = nc.gpsimd
        own = Chain(gp, pool_own)
        gp.wait_ge(dma_had, 32)
        src, dst = wv, wz
        for s in range(4):
            a = src.rearrange("p (h two l) d -> p two h (l d)", two=2, l=2 ** s)
            o = dst.rearrange("p (h two l) d -> p two h (l d)", two=2, l=2 ** s)
            G.tensor_tensor(o[:, 0], a[:, 0], a[:, 1], ALU.add)
            last = G.tensor_tensor(o[:, 1], a[:, 0], a[:, 1], ALU.subtract)
            if s < 3:
                own.link(last)
            src, dst = dst, src
        last.then_inc(butterfly, 1)
        end_phase(gp, 1)

        G.memset(dA[:, :, :, 0:1], 0.0).then_inc(dA_zero, 1)
        with gp.Fori(0, NB) as b:
            for et in range(ET):
                gp.wait_ge(pt_in[0][et % 2], 16 * (2 * b + et // 2) + 16)
                for c in range(NC):
                    if et == 0:
                        gp.wait_ge(a_b_in[c], 16 * b + 16)
                    gp.wait_ge(a_summed, NC * (ET * b + et) + c - NC + 1 + CR_RING)
                    G.tensor_tensor(stA(c), pt[:, et % 2, 2:3, :].to_broadcast([P, CH, L]), bc[:, 0, CH * c:CH * c + CH, :],
                                    ALU.mult).then_inc(a_bx, 1)
        end_phase(gp, 2)
        end_phase(gp, 3)

        with gp.Fori(0, 2) as hf:
            with gp.Fori(0, 2) as i:
                j = 2 * hf + i
                own.enter(j, ET * (1 + 2 * NC))
                for et in range(ET):
                    s2 = et % 2
                    gp.wait_ge(pt_in[1][s2], 16 * (2 * j + et // 2) + 16)
                    gp.wait_ge(y1_out[s2], 16 * (2 * j + et // 2 + s2) + CR_ONE)
                    hold(gp)
                    own.link(G.tensor_scalar(yt[:, s2, :], pt[:, s2, 0, :], par[1][:, et, P_D:P_D + 1], None, ALU.mult))
                    for c in range(NC):
                        s, m = c % 2, 8 * j + 2 * et + c // 2
                        gp.wait_ge(p_ready[1][s], m + 1 + CR_TWO)
                        own.link(G.tensor_tensor(st[:, s, 0:2], st[:, s, 0:2], st[:, s, 2:4], ALU.add))
                        own.link(G.tensor_tensor(st[:, s, 0], st[:, s, 0], st[:, s, 1], ALU.add))
                        G.tensor_tensor(yt[:, s2, :], yt[:, s2, :], st[:, s, 0], ALU.add).then_inc(st_free[1][s], 1)
                        gp.wait_ge(st_free[1][s], m + 1 + CR_ST)
                own.leave(ET * (1 + 2 * NC), 4)
        end_phase(gp, 4)
        end_phase(gp, 5)

    ctx.close()


def kernel(**a):
    import concourse.bacc as bacc
    from concourse.bass_utils import run_bass_kernel_spmd

    n = lambda name: np.asarray(a[name])
    had = np.array([[1.0]], np.float32)
    while had.shape[0] < P:
        had = np.block([[had, had], [had, -had]]).astype(np.float32)
    host = {
        "x": n("x").reshape(NB * L, DM),
        "ctxT": n("ctx_1024").reshape(NB * L, DC).T,
        "gates": np.concatenate([n("g_xattn"), n("g_ffn")])[None, :],
        "ident": np.eye(P, dtype=np.float32),
        "had": had,
        "iota": np.arange(E, dtype=np.float32)[None, :],
        "gwT": n("L0_ffn_gate_w").T,
        "w1": n("L0_ffn_w1"),
        "b1": n("L0_ffn_b1").reshape(E, F // P, P).transpose(0, 2, 1),
        "w2": n("L0_ffn_w2"),
        "b2": n("L0_ffn_b2"),
        "W1T": n("L1_ffn_W1").T,
        "W2T": n("L1_ffn_W2").T,
        "W3T": n("L1_ffn_W3").T,
    }
    for l in range(2):
        g = lambda name: n(f"L{l}_xattn_{name}")
        host[f"inw{l}"] = g("in_proj_w").T
        host[f"xpw{l}"] = np.concatenate([g("x_proj_w")[DR:], g("x_proj_w")[:DR]]).T
        host[f"dtw{l}"] = g("dt_proj_w").T
        cols = [g("conv_w").reshape(DI, TAPS), g("conv_b")[:, None], g("dt_proj_b")[:, None], g("D")[:, None], g("A_log")]
        host[f"par{l}"] = np.concatenate(cols, axis=1).reshape(ET, P, NPAR).transpose(1, 0, 2).reshape(P, ET * NPAR)
    nc = bacc.Bacc("TRN2", target_bir_lowering=False, num_devices=1)
    arrays = {f"in_{k}": np.ascontiguousarray(v) for k, v in host.items()}
    d = {k: nc.dram_tensor(f"in_{k}", v.shape, mybir.dt.from_np(v.dtype), kind="ExternalInput").ap() for k, v in host.items()}
    scratch = {"bc0": [NB, 2 * DS, L], "bc1": [NB, 2 * DS, L], "prep0": [NB, 3, ET, P, L], "prep1": [NB, 3, ET, P, L],
               "z": [NB, TT, P, L], "y1": [1 + NB * ET, P, L], "xT": [2, 2, DM, HTOK], "w2h": [2, F, DM]}
    for k, shape in scratch.items():
        d[k] = nc.dram_tensor(k, shape, F16 if k in ("xT", "w2h") else F32, kind="Internal").ap()
    d["sel"] = nc.dram_tensor("sel", [1, 8], U32, kind="Internal").ap()
    d["out"] = nc.dram_tensor("out_0", [NB * L, DM], F32, kind="ExternalOutput").ap()
    build(nc, d)
    r = run_bass_kernel_spmd(nc, [arrays], core_ids=[0])
    return r.results[0]["out_0"].reshape(NB, L, DM)
```

```python
from contextlib import ExitStack

import numpy as np
import concourse.bass as bass
from concourse import mybir

P = 128
NB, L, DM = 4, 512, 512
DC, DI, DS, DR, TAPS = 256, 512, 16, 16, 4
E, F = 8, 2048
ET = DI // P
TT = L // P
TILES = NB * TT
NC = 4
CH = DS // NC
KC = DC // P
KD = DM // P
FG = 512
FT = FG // P
NG = F // FG
HB = NB // 2
HTOK = HB * L
HTILES = HTOK // P
HAD_TILES = F // P
HAD_FIRST = HAD_TILES // 2
P_W, P_CB, P_DB, P_D, P_AL = 0, TAPS, TAPS + 1, TAPS + 2, TAPS + 3
NPAR = TAPS + 3 + DS
EPS = 1e-5
S_X, S_W, S_H = 256.0, 256.0, 64.0
N_SCALE = float(S_W / np.sqrt(F))

F32 = mybir.dt.float32
F16 = mybir.dt.float16
U32 = mybir.dt.uint32
ALU = mybir.AluOpType
ACT = mybir.ActivationFunctionType
AX = mybir.AxisListType


class Chain:

    def __init__(self, eng, sem):
        self.eng, self.sem, self.base, self.n, self.outer = eng, sem, 0, 0, []

    def step(self, ins):
        ins.then_inc(self.sem, 1)
        self.n += 1

    def join(self):
        self.eng.wait_ge(self.sem, self.base + self.n)

    def link(self, ins):
        self.step(ins)
        self.join()

    def enter(self, i, per):
        self.outer.append((self.base, self.n))
        self.base, self.n = self.base + self.n + i * per, 0

    def leave(self, per, count):
        assert self.n == per, f"the body marks {self.n}, not {per}"
        self.base, self.n = self.outer.pop()
        self.n += per * count


def build(nc, d):
    ctx = ExitStack()
    sb = lambda name, shape, dt=F32: ctx.enter_context(nc.sbuf_tensor(name, shape, dt))
    sem = lambda name: ctx.enter_context(nc.semaphore(name))
    bank = [ctx.enter_context(nc.psum_tensor(f"bank{i}", [P, 512], F32)) for i in range(8)]

    x_sb = sb("x_sb", [P, TILES, DM])
    bc = sb("bc", [P, 2, DS, L])
    dA = sb("dA", [P, 2, CH, L])
    st = sb("st", [P, 2, CH, L])
    pt = sb("pt", [P, 2, 3, L])
    yt = sb("yt", [P, 2, L])
    pool = sb("pool", [P, 15 * 1024])
    ident = sb("ident", [P, P])
    par = [sb(f"par{l}", [P, ET, NPAR]) for l in range(2)]
    negA = [sb(f"negA{l}", [P, ET, DS]) for l in range(2)]
    gates = sb("gates", [P, 4])
    mv = sb("mv", [P, TT, 2])
    down1 = sb("down1", [P, 1])
    bnst = sb("bnst", [P, TT, 6])
    rstd = sb("rstd", [P, TT])
    gwT = sb("gwT", [P, KD, E])
    lsum = sb("lsum", [P, E])
    top = sb("top", [P, 8])
    topi = sb("topi", [P, 8], U32)
    topf = sb("topf", [P, 8])
    iota = sb("iota", [P, E])
    hot = sb("hot", [P, 2, E])
    lsel = sb("lsel", [P, 2, TILES])
    lmax = sb("lmax", [P, TILES])
    lexp = sb("lexp", [P, 2, TILES])
    cbias = sb("cbias", [P, 2, 2, HTILES])
    coef = sb("coef", [P, 2, 2, HTILES])
    b1s = sb("b1s", [P, F // P])
    epsc = sb("epsc", [P, 1])
    onec = sb("onec", [P, 1])
    v = lambda src, o, size, pat, /, **k: src[:, o:o + size].rearrange(pat, **k)
    ctxT = v(pool, 0, KC * NB * L, "p (k t) -> p k t", k=KC)
    inw = v(pool, 4096, KC * DI, "p (k e) -> p k e", k=KC)
    u4 = v(pool, 5120, 2 * ET * L, "p (s e t) -> p s e t", s=2, e=ET)
    xpw = v(pool, 9216, ET * 48, "p (k m) -> p k m", k=ET)
    dtw = pool[:, 9408:9408 + DI]
    xd = pool[:, 9920:9920 + L]
    e4, r4 = st[:, 0], st[:, 1]
    l4, q4 = dA[:, 0], dA[:, 1]
    hd = pool[:, 10432:10432 + P]
    bcf = bc[:, :, :, :].rearrange("p a n t -> p (a n t)")
    wv = v(bcf, 0, 16 * DM, "p (h d) -> p h d", h=16)
    wz = v(bcf, 16 * DM, 16 * DM, "p (h d) -> p h d", h=16)
    zg = v(pt[:, :, :, :].rearrange("p s a t -> p (s a t)"), 0, TT * L, "p (t d) -> p t d", t=TT)
    stx = v(pool, 11264, 2 * CH * L, "p (s n t) -> p s n t", s=2, n=CH)
    stA = lambda c: st[:, c] if c < 2 else stx[:, c - 2]
    zt = v(pool, 1024, 2 * L, "p (s t) -> p s t", s=2)
    ctxb = v(pool, 0, KC * L, "p (k t) -> p k t", k=KC)
    u1 = v(pool, 5120, ET * L, "p (e t) -> p e t", e=ET)
    l1, e1 = (v(pool, o, 4 * L, "p (h s t) -> p h s t", h=2, s=2) for o in (2048, 7168))
    r1 = v(pool, 0, 2 * L, "p (s t) -> p s t", s=2)
    xTf = v(pool, 8192, 4 * KD * P, "p (s k t) -> p s k t", s=4, k=KD)
    logit = v(pool, 10240, TILES * E, "p (t e) -> p t e", t=TILES)
    lwork = v(pool, 10368, TILES * E, "p (t e) -> p t e", t=TILES)
    ones = pool[:, 10496:10496 + P]
    half = lambda o, n: pool[:, o:o + n // 2].bitcast(F16)
    xT = half(0, 2 * KD * HTOK).rearrange("p (a k t) -> p a k t", a=2, k=KD)
    xTh = [xT, half(4096, 2 * KD * HTOK).rearrange("p (a k t) -> p a k t", a=2, k=KD)]
    w1g = half(4096, 2 * KD * FG).rearrange("p (a k f) -> p a k f", a=2, k=KD)
    w2g = half(6144, 2 * FT * DM).rearrange("p (a k f) -> p a k f", a=2, k=FT)
    hT = half(8192, 4 * FT * L).rearrange("p (a s f t) -> p a s f t", a=2, s=2, f=FT)
    stage = v(pool, 12288, KD * FG, "p (k f) -> p k f", k=KD)
    h32 = v(pool, 14336, 2 * L, "p (s t) -> p s t", s=2)
    b2b = h32[:, 0]
    bch = bcf.bitcast(F16)
    xT1 = bch[:, 0:2 * KD * NB * L].rearrange("p (a k t) -> p a k t", a=2, k=KD)
    w3g = bch[:, 16384:16384 + 2 * KD * FG].rearrange("p (a k f) -> p a k f", a=2, k=KD)
    stage3 = v(bcf, 10240, KD * FG, "p (k f) -> p k f", k=KD)
    sg = v(bcf, 12288, 2 * L, "p (s t) -> p s t", s=2)
    y1b = v(bcf, 13312, ET * L, "p (e t) -> p e t", e=ET)
    w2s = [pool[:, o:o + 4 * DM].bitcast(F16).rearrange("p (h a d) -> p h a d", h=4, a=2)
           for o in (10624, 10624 + 4 * DM, 0, 4 * DM)]

    dma_par, dma_had, dma_x = sem("dma_par"), sem("dma_had"), sem("dma_x")
    dma_ctx, dma_ctx_rest = sem("dma_ctx"), sem("dma_ctx_rest")
    held = sem("held")
    phase = sem("phase")
    act_own, dve_own, pool_own = sem("act_own"), sem("dve_own"), sem("pool_own")
    gates_ready, consts_ready = sem("gates_ready"), sem("consts_ready")
    two = lambda name: [sem(f"{name}{l}") for l in range(2)]
    dma_w = two("dma_w")
    xin = two("xin")
    tap_last = two("tap_last")
    conv = two("conv")
    u_ready = two("u_ready")
    xdbl = two("xdbl")
    xd_ready = two("xd_ready")
    dtraw = two("dtraw")
    soft = two("soft")
    prep_ready = two("prep_ready")
    xd_out = two("xd_out")
    u_out = two("u_out")
    dd_out = sem("dd_out")
    dd1_out = two("dd1_out")
    butterfly, had_mm, had_hi, had_lo = sem("butterfly"), sem("had_mm"), sem("had_hi"), sem("had_lo")
    had_out = sem("had_out")
    pt_in = [two(f"pt_in{l}_") for l in range(2)]
    uz_in = two("uz_in")
    bc_in = [sem(f"bc_in{c}") for c in range(NC)]
    dA_ready = two("dA_ready")
    dA_free = two("dA_free")
    bx_ready = two("bx_ready")
    p_ready = two("p_ready")
    st_free = two("st_free")
    a_exp, a_bx, a_scan, a_p = sem("a_exp"), sem("a_bx"), sem("a_scan"), sem("a_p")
    a_summed = sem("a_summed")
    a_b_in, a_c_in = ([sem(f"{n}{c}") for c in range(NC)] for n in ("a_b_in", "a_c_in"))
    unit_done = sem("unit_done")
    dA_zero = sem("dA_zero")
    y_gated, y_turned, y_added = sem("y_gated"), sem("y_turned"), sem("y_added")
    y1_out = two("y1_out")
    ln_stats, ln_std, ln_done, z_ready = sem("ln_stats"), sem("ln_std"), sem("ln_done"), sem("z_ready")
    z_out, ctx_in = sem("z_out"), sem("ctx_in")
    xn_turned, xT_ready, xT_out, logit_mm = sem("xn_turned"), sem("xT_ready"), sem("xT_out"), sem("logit_mm")
    xT_f32, xT_hi = sem("xT_f32"), sem("xT_hi")
    lsum_in, lsum_mm, sel_ready, sel_out = sem("lsum_in"), sem("lsum_mm"), sem("sel_ready"), sem("sel_out")
    rt_in, rt_exp = sem("rt_in"), sem("rt_exp")
    xT_in, w1_in, w2_in, b1_in, b2_in = sem("xT_in"), sem("w1_in"), sem("w2_in"), sem("b1_in"), sem("b2_in")
    b2_used = sem("b2_used")
    w1_hi, w1_lo, w2_hi, w2_lo = sem("w1_hi"), sem("w1_lo"), sem("w2_hi"), sem("w2_lo")
    h_full, hid_hi, hid_lo = sem("h_full"), sem("hid_hi"), sem("hid_lo")
    up_done, down_done, evac_done = sem("up_done"), sem("down_done"), sem("evac_done")
    g_stats, g_std, g_norm, g_z = sem("g_stats"), sem("g_std"), sem("g_norm"), sem("g_z")
    y1_in, g_gated, g_turned, g_added = sem("y1_in"), sem("g_gated"), sem("g_turned"), sem("g_added")
    g_xturned, g_xhi, g_xT = sem("g_xturned"), sem("g_xhi"), sem("g_xT")
    cw_in, cw2_in = sem("cw_in"), sem("cw2_in")
    cw_hi, cw_lo = sem("cw_hi"), sem("cw_lo")
    c_up, c_sg, c_full, c_hi, c_lo, c_down, c_evac = (sem(x) for x in ("c_up", "c_sg", "c_full", "c_hi", "c_lo", "c_down", "c_evac"))
    out_sem = sem("out_sem")

    CR_BANK, CR_ONE, CR_TWO, CR_ST, CR_UP, CR_HID, CR_DOWN, CR_EV, CR_RING = ET, 1, 2, 3, 2 * FT, FT, 2 * TT, 3 * TT, NC
    opening = [(s, CR_BANK) for s in conv] + [(s, CR_RING) for s in (a_exp, a_bx, a_p, a_summed)]
    opening += [(a_scan, CR_TWO), (soft[1], CR_TWO), (prep_ready[1], CR_TWO), (y_gated, CR_TWO), (z_out, CR_ONE), (y_added, CR_TWO), (up_done, CR_UP), (h_full, CR_HID), (hid_lo, CR_TWO),
               (w1_lo, CR_ONE), (w2_lo, CR_ONE), (cw_lo, CR_ONE),
               (down_done, CR_DOWN), (evac_done, CR_EV), (b2_used, CR_ONE), (g_gated, CR_ONE), (g_added, CR_BANK), (g_xT, CR_BANK),
               (c_up, CR_UP), (c_full, CR_TWO), (c_lo, CR_TWO), (c_down, CR_DOWN), (c_evac, CR_EV)]
    opening += [(s, CR_ONE) for g in (soft[:1], xd_out, u_out, [dd_out], dd1_out, prep_ready[:1], y1_out) for s in g]
    opening += [(unit_done, CR_TWO)]
    opening += [(s, n) for g, n in ((dA_free, CR_ONE), (p_ready, CR_TWO), (st_free, CR_ST)) for s in g]
    G_Y, G_X, G_BANK = FT, FT, 7
    block = ctx.enter_context(nc.Block())
    ENGINES = 5

    def end_phase(eng, k):
        eng.drain().then_inc(phase, 1)
        eng.wait_ge(phase, ENGINES * k)

    def hold(eng):
        eng.sem_inc(held, 1)

    flat = lambda ap: ap.rearrange("p n t -> p (n t)")
    one = lambda ap: ap.rearrange("p o t -> p (o t)")
    tile_of = lambda i: x_sb[:, bass.ds(i, 1), :].rearrange("p o t -> p (o t)")
    u_of = lambda b, et: one(u4[:, bass.ds(b % 2, 1), et])

    @block.sync
    def _(sp):
        for s, n in opening:
            sp.sem_inc(s, n)
        ctx_in_dram = d["ctxT"].rearrange("(k p) t -> p k t", p=P)
        sp.dma_start(ctxT[:, :, 0:L], ctx_in_dram[:, :, 0:L]).then_inc(dma_ctx, 16)

        def weights(l):
            sp.dma_start(inw, d[f"inw{l}"].rearrange("(k p) e -> p k e", p=P)).then_inc(dma_w[l], 16)
            sp.dma_start(xpw, d[f"xpw{l}"].rearrange("(k p) m -> p k m", p=P)).then_inc(dma_w[l], 16)
            sp.dma_start(dtw[32:48, :], d[f"dtw{l}"]).then_inc(dma_w[l], 16)
        weights(0)
        for l in range(2):
            sp.dma_start(par[l][:, :, :], d[f"par{l}"].rearrange("p (e n) -> p e n", e=ET)).then_inc(dma_par, 16)
        sp.dma_start(ctxT[:, :, L:], ctx_in_dram[:, :, L:]).then_inc(dma_ctx_rest, 16)
        sp.dma_start(gates[:, :], d["gates"].to_broadcast([P, 4])).then_inc(dma_par, 16)
        sp.dma_start(iota[:, :], d["iota"].to_broadcast([P, E])).then_inc(dma_par, 16)
        sp.dma_start(ident[:, :], d["ident"]).then_inc(dma_par, 16)
        sp.dma_start(gwT[:, :, :], d["gwT"].rearrange("(k p) e -> p k e", p=P)).then_inc(dma_par, 16)
        sp.dma_start(x_sb[:, :, :], d["x"].rearrange("(t p) d -> p t d", p=P)).then_inc(dma_x, 16)
        sp.dma_start(wv, d["W2T"].rearrange("(h p) d -> p h d", p=P)).then_inc(dma_had, 16)
        sp.dma_start(hd, d["had"]).then_inc(dma_had, 16)

        def store_inputs(b):
            sp.wait_ge(xd_ready[0], b + 1)
            sp.dma_start(d["bc0"][bass.ds(b, 1)].rearrange("o n t -> (o n) t"), xd[0:32, :]).then_inc(xd_out[0], 16)
            sp.wait_ge(u_ready[0], ET * b + ET)
            sp.dma_start(d["prep0"][bass.ds(b, 1), 0].rearrange("o e p t -> p (o e) t"),
                         u4[:, bass.ds(b % 2, 1)].rearrange("p o e t -> p (o e) t")).then_inc(u_out[0], 16)
            sp.wait_ge(z_ready, b + 1)
            sp.dma_start(d["z"][bass.ds(b, 1)].rearrange("o t p d -> p (o t) d"), zg).then_inc(z_out, 16)

        def store_deltas(b):
            sp.wait_ge(prep_ready[0], b + 1 + CR_ONE)
            for a, part in ((1, l4), (2, q4)):
                sp.dma_start(d["prep0"][bass.ds(b, 1), a].rearrange("o e p t -> p (o e) t"), part).then_inc(dd_out, 16)

        def store_hadamard(groups):
            for h in groups:
                sp.wait_ge(had_lo, 4 * h + 4)
                for a in range(2):
                    sp.dma_start(d["w2h"][a, 4 * h * P:4 * h * P + 4 * P].rearrange("(h p) d -> p h d", p=P), w2s[h][:, :, a]).then_inc(had_out, 16)

        with sp.Fori(0, NB - 1) as b:
            store_inputs(b)
            store_deltas(b)
        store_hadamard(range(2))
        store_inputs(NB - 1)
        sp.wait_ge(dtraw[0], ET * NB)
        weights(1)
        store_deltas(NB - 1)
        store_hadamard(range(2, 4))
        sp.wait_ge(xd_out[0], 16 * NB + CR_ONE)
        sp.wait_ge(u_out[0], 16 * NB + CR_ONE)
        sp.wait_ge(dd_out, 32 * NB + CR_ONE)
        sp.wait_ge(z_out, 16 * NB + CR_ONE)
        sp.wait_ge(had_out, 32 * 4)
        sp.wait_ge(dma_x, 16)
        end_phase(sp, 1)

        def load_deltas(b, et):
            n = NC * (ET * b + et - 2) + NC
            sp.wait_ge(a_exp, n + CR_RING)
            sp.wait_ge(a_bx, n + CR_RING)
            sp.dma_start(pt[:, et % 2, 1:3], d["prep0"][bass.ds(b, 1), 1:3, et].rearrange("o a p t -> p (o a) t")).then_inc(pt_in[0][et % 2], 16)

        def load_gate(b, et):
            sp.wait_ge(y_gated, ET * b + et - 2 + 1 + CR_TWO)
            hold(sp)
            sp.dma_start(pt[:, et % 2, 0], d["prep0"][bass.ds(b, 1), 0, et].rearrange("o p t -> p (o t)")).then_inc(uz_in[et % 2], 16)
            sp.dma_start(zt[:, et % 2, :], d["z"][bass.ds(b, 1), et].rearrange("o p t -> p (o t)")).then_inc(uz_in[et % 2], 16)

        def spread(b, a, c, done):
            src = d["bc0"][bass.ds(b, 1), DS * a + CH * c:DS * a + CH * c + CH, :].rearrange("o n t -> o (n t)")
            sp.dma_start(flat(bc[:, a, CH * c:CH * c + CH, :]), src.to_broadcast([P, CH * L])).then_inc(done[c], 16)

        with sp.Fori(0, NB) as b:
            for c in range(NC):
                if c == 0:
                    load_deltas(b, 0)
                n = NC * ET * (b - 1) + NC * (ET - 1) + c + 1
                sp.wait_ge(a_bx, n + CR_RING)
                spread(b, 0, c, a_b_in)
                if c == 0:
                    load_gate(b, 0)
                if c == 1:
                    sp.wait_ge(prep_ready[1], 2 * b + CR_TWO)
                    sp.dma_start(ctxb, d["ctxT"].rearrange("(k p) t -> p k t", p=P)[:, :, bass.ds(b * L, L)]).then_inc(ctx_in, 16)
                sp.wait_ge(a_p, n + CR_RING)
                spread(b, 1, c, a_c_in)
            load_deltas(b, 1)
            load_gate(b, 1)
            load_deltas(b, 2)
            load_gate(b, 2)
            sp.wait_ge(u_ready[1], ET * b + ET)
            sp.dma_start(d["prep1"][bass.ds(b, 1), 0].rearrange("o e p t -> p (o e) t"), u1).then_inc(u_out[1], 16)
            load_deltas(b, 3)
            sp.wait_ge(xd_ready[1], b + 1)
            sp.dma_start(d["bc1"][bass.ds(b, 1)].rearrange("o n t -> (o n) t"), xd[0:32, :]).then_inc(xd_out[1], 16)
            load_gate(b, 3)
            sp.wait_ge(prep_ready[1], 2 * b + 1 + CR_TWO)
            for a, part in enumerate((l1[:, 0], e1[:, 0])):
                sp.dma_start(d["prep1"][bass.ds(b, 1), 1 + a, 0:2].rearrange("o e p t -> p (o e) t"), part).then_inc(dd1_out[0], 16)
        sp.wait_ge(xd_out[1], 16 * NB + CR_ONE)
        sp.wait_ge(u_out[1], 16 * NB + CR_ONE)
        for h in range(2):
            sp.wait_ge(dd1_out[h], 32 * NB + CR_ONE)
        end_phase(sp, 2)

        def unit_load(b, et):
            sp.wait_ge(st_free[1], 8 * b + 2 * (et - 2) + 2 + CR_ST)
            sp.dma_start(pt[:, et % 2], d["prep1"][bass.ds(b, 1), :, et].rearrange("o a p t -> p (o a) t")).then_inc(pt_in[1][et % 2], 16)

        def bc_load(b, c):
            sp.wait_ge(p_ready[c % 2], 8 * (b - 1) + 2 * (ET - 1) + c // 2 + 1 + CR_TWO)
            for a in range(2):
                src = d["bc1"][bass.ds(b, 1), DS * a + CH * c:DS * a + CH * c + CH, :].rearrange("o n t -> o (n t)")
                sp.dma_start(flat(bc[:, a, CH * c:CH * c + CH, :]), src.to_broadcast([P, CH * L])).then_inc(bc_in[c], 16)

        def up_weights(e, w, k):
            sp.wait_ge(w2_lo, w + CR_ONE)
            sp.dma_start(stage, d["w1"][bass.ds(e, 1), :, k * FG:k * FG + FG].rearrange("o (k p) f -> p (o k) f", p=P)).then_inc(w1_in, 16)

        for hf in range(2):
            sp.wait_ge(xT_ready, HTILES * hf + HTILES)
            for a in range(2):
                sp.dma_start(d["xT"][hf, a].rearrange("(k p) t -> p k t", p=P), xTh[hf][:, a]).then_inc(xT_out, 16)
        sp.wait_ge(sel_ready, 1)
        sp.dma_start(d["sel"], topi[0:1, :]).then_inc(sel_out, 16)
        sp.wait_ge(sel_out, 16)
        up_weights(sp.value_load(d["sel"][0:1, 0:1], min_val=0, max_val=E - 1), 0, 0)
        sp.wait_ge(xT_out, 64)
        end_phase(sp, 3)

        with sp.Fori(0, 2) as hf:
            sp.wait_ge(up_done, 64 * hf + CR_UP)
            for a in range(2):
                sp.dma_start(xT[:, a], d["xT"][bass.ds(hf, 1), a].rearrange("o (k p) t -> p (o k) t", p=P)).then_inc(xT_in, 16)
            with sp.Fori(0, 2) as i:
                e = sp.value_load(d["sel"][0:1, bass.ds(i, 1)], min_val=0, max_val=E - 1)
                other = sp.value_load(d["sel"][0:1, bass.ds(1 - i, 1)], min_val=0, max_val=E - 1)
                j = 2 * hf + i
                sp.wait_ge(hid_lo, 32 * j + CR_TWO)
                sp.dma_start(b1s[:, :], d["b1"][bass.ds(e, 1)].rearrange("o p f -> p (o f)")).then_inc(b1_in, 16)
                sp.dma_start(b2b, d["b2"][bass.ds(e, 1)].to_broadcast([P, DM])).then_inc(b2_in, 16)
                for k in range(NG):
                    w = 4 * j + k
                    unit_load(j, k)
                    if k == 0:
                        bc_load(j, 0)
                    sp.wait_ge(w1_lo, w + 1 + CR_ONE)
                    sp.dma_start(stage, d["w2"][bass.ds(e, 1), k * FG:k * FG + FG].rearrange("o (k p) f -> p (o k) f", p=P)).then_inc(w2_in, 16)
                    if k == 0:
                        for c in range(1, NC):
                            bc_load(j, c)
                    sp.wait_ge(st_free[1], 2 * w + CR_ST)
                    sp.dma_start(one(d["y1"][bass.ds(w, 1)].rearrange("o p t -> p o t")), yt[:, (k - 1) % 2, :]).then_inc(y1_out[(k - 1) % 2], 16)
                    up_weights(other if k == NG - 1 else e, w + 1, (k + 1) % NG)
        sp.wait_ge(st_free[1], 2 * NB * ET + CR_ST)
        sp.dma_start(d["y1"][NB * ET], yt[:, 1, :]).then_inc(y1_out[1], 16)
        sp.wait_ge(y1_out[0], 16 * 8 + CR_ONE)
        sp.wait_ge(y1_out[1], 16 * 9 + CR_ONE)
        end_phase(sp, 4)

        def y1_load(b):
            sp.wait_ge(g_gated, b + CR_ONE)
            sp.dma_start(y1b, d["y1"][bass.ds(ET * b + 1, ET)].rearrange("e p t -> p e t")).then_inc(y1_in, 16)

        def in_weights(w, g):
            sp.wait_ge(cw_lo, w + CR_ONE)
            sp.dma_start(stage, d["W1T"][:, bass.ds(g * FG, FG)].rearrange("(k p) f -> p k f", p=P)).then_inc(cw_in, 16)
            sp.dma_start(stage3, d["W3T"][:, bass.ds(g * FG, FG)].rearrange("(k p) f -> p k f", p=P)).then_inc(cw_in, 16)

        y1_load(0)
        in_weights(0, 0)
        y1_load(1)
        end_phase(sp, 5)

        for hf in range(2):
            with sp.Fori(0, NG // 2) as q:
                for s in range(2):
                    w, g = NG * hf + 2 * q + s, 2 * q + s
                    sp.wait_ge(c_down, 8 * w + CR_DOWN)
                    for a in range(2):
                        sp.dma_start(w2g[:, a], d["w2h"][a, bass.ds(g * FG, FG)].rearrange("(k p) f -> p k f", p=P)).then_inc(cw2_in, 16)
                    in_weights(w + 1, (g + 1) % NG)
                    if hf == 0 and s == 0:
                        y1_load(HB + q)
            if hf == 0:
                sp.wait_ge(c_evac, 8 * NG + CR_EV)
                sp.dma_start(d["out"][0:HTOK].rearrange("(t p) d -> p t d", p=P), x_sb[:, 0:HTILES, :]).then_inc(out_sem, 16)
        for t in range(0, HTILES, 2):
            sp.wait_ge(c_evac, 8 * (2 * NG - 1) + t + 2 + CR_EV)
            o = HTOK + t * P
            sp.dma_start(d["out"][o:o + 2 * P].rearrange("(t p) d -> p t d", p=P), x_sb[:, HTILES + t:HTILES + t + 2, :]).then_inc(out_sem, 16)
        sp.wait_ge(cw_in, 32 * (2 * NG + 1))
        sp.wait_ge(out_sem, 16 * (1 + HTILES // 2))

    @block.tensor
    def _(pe):
        mm = nc.tensor.matmul
        pe.wait_ge(dma_ctx, 16)

        def in_proj(b):
            for et in range(ET):
                pe.wait_ge(conv[0], ET * b + et + 1)
                for k in range(KC):
                    last = mm(bank[et][:, :], inw[:, k, et * P:et * P + P], ctxT[:, k, bass.ds(b * L, L)],
                              start=(k == 0), stop=(k == KC - 1))
                last.then_inc(xin[0], 1)

        def x_proj(b):
            pe.wait_ge(soft[0], b + CR_ONE)
            for k in range(ET):
                pe.wait_ge(u_ready[0], ET * b + k + 1)
                last = mm(bank[4][0:48, :], xpw[:, k, :], u_of(b, k), start=(k == 0), stop=(k == ET - 1))
            last.then_inc(xdbl[0], 1)

        def dt_proj(b):
            pe.wait_ge(xd_ready[0], b + 1)
            for et in range(ET):
                mm(bank[4 + et][:, :], dtw[32:48, et * P:et * P + P], xd[32:48, :], start=True, stop=True).then_inc(dtraw[0], 1)

        pe.wait_ge(dma_w[0], 48)
        in_proj(0)
        pe.wait_ge(dma_ctx_rest, 16)
        with pe.Fori(0, NB - 1) as b:
            x_proj(b)
            in_proj(b + 1)
            dt_proj(b)
        x_proj(NB - 1)

        def hadamard(tiles):
            for h in tiles:
                if h >= 4:
                    pe.wait_ge(had_lo, h - 3)
                mm(bank[h % 4][:, :], hd, wv[:, h, :], start=True, stop=True).then_inc(had_mm, 1)

        pe.wait_ge(dma_had, 32)
        pe.wait_ge(butterfly, 1)
        pe.wait_ge(conv[0], ET * NB + CR_BANK)
        hadamard(range(HAD_FIRST))
        dt_proj(NB - 1)
        hadamard(range(HAD_FIRST, HAD_TILES))
        end_phase(pe, 1)

        def turn(bk, src, done):
            for k in range(4):
                last = nc.tensor.transpose(bk[:, k * P:k * P + P], src[:, k * P:k * P + P], ident[:, :])
            last.then_inc(done, 1)

        def reduce_chunk(b, et, c):
            pe.wait_ge(a_p, NC * (ET * b + et) + c + 1 + CR_RING)
            for n in range(CH):
                last = mm(bank[et % 2][:, :], ident[:, :], stA(c)[:, n, :], start=(c == 0 and n == 0), stop=(c == NC - 1 and n == CH - 1))
            last.then_inc(a_summed, 1)

        def turn_unit(b, et):
            pe.wait_ge(y_gated, ET * b + et + 1 + CR_TWO)
            pe.wait_ge(y_added, ET * b + et - 2 + 1 + CR_TWO)
            turn(bank[2 + et % 2], yt[:, et % 2, :], y_turned)

        def in_proj1(b):
            pe.wait_ge(ctx_in, 16 * b + 16)
            for et in range(ET):
                pe.wait_ge(soft[1], 2 * (b - 1) + et // 2 + 1 + CR_TWO)
                for k in range(KC):
                    last = mm(bank[4 + et][:, :], inw[:, k, et * P:et * P + P], ctxb[:, k, :], start=(k == 0), stop=(k == KC - 1))
                last.then_inc(xin[1], 1)

        def x_proj1(b):
            pe.wait_ge(conv[1], ET * b + 1 + CR_BANK)
            for k in range(ET):
                pe.wait_ge(u_ready[1], ET * b + k + 1)
                last = mm(bank[4][0:48, :], xpw[:, k, :], u1[:, k, :], start=(k == 0), stop=(k == ET - 1))
            last.then_inc(xdbl[1], 1)

        def dt_proj1(b):
            pe.wait_ge(xd_ready[1], b + 1)
            for et in range(ET):
                mm(bank[4 + et][:, :], dtw[32:48, et * P:et * P + P], xd[32:48, :], start=True, stop=True).then_inc(dtraw[1], 1)

        def scan_sums(b, first):
            for et in range(ET):
                pe.wait_ge(unit_done, ET * b + et - 2 + 1 + CR_TWO)
                if et == 0:
                    in_proj1(b)
                reduce_chunk(b, et, 0)
                reduce_chunk(b, et, 1)
                if et:
                    turn_unit(b, et - 1)
                elif not first:
                    turn_unit(b - 1, ET - 1)
                if et == 1:
                    x_proj1(b)
                reduce_chunk(b, et, 2)
                reduce_chunk(b, et, 3)
                if et == 1:
                    dt_proj1(b)

        pe.wait_ge(dma_w[1], 48)
        scan_sums(0, True)
        with pe.Fori(0, NB - 1) as b:
            scan_sums(b + 1, False)
        turn_unit(NB - 1, ET - 1)
        end_phase(pe, 2)

        def logits(t):
            pe.wait_ge(xT_f32, t + 1)
            for k in range(KD):
                last = mm(bank[6][:, t * E:t * E + E], xTf[:, t % 4, k, :], gwT[:, k, :], start=(k == 0), stop=(k == KD - 1))
            last.then_inc(logit_mm, 1)

        for t in range(TILES):
            pe.wait_ge(ln_done, 4 + t // TT + 1)
            if t >= 4:
                pe.wait_ge(xT_ready, t - 3)
            turn(bank[2 + t % 4], st[:, (t // TT) % 2, t % TT, :], xn_turned)
            if t:
                logits(t - 1)
        logits(TILES - 1)
        pe.wait_ge(lsum_in, 1)
        mm(bank[7][:, 0:E], ones, lsum[:, :], start=True, stop=True).then_inc(lsum_mm, 1)
        end_phase(pe, 3)

        def mm3(out, wt, tok, first, last_k):
            for m, (a, b) in enumerate(((0, 0), (0, 1), (1, 0))):
                ins = mm(out, wt[a], tok[b], start=(first and m == 0), stop=(last_k and m == 2))
            return ins

        with pe.Fori(0, 2) as hf:
            pe.wait_ge(xT_in, 32 * hf + 32)
            hold(pe)
            with pe.Fori(0, 2) as i:
                for k in range(NG):
                    w = 4 * (2 * hf + i) + k
                    pe.wait_ge(w1_lo, w + 1 + CR_ONE)
                    for g in range(2):
                        for f in range(FT):
                            pe.wait_ge(h_full, 8 * w + 4 * g + f - 4 + 1 + CR_HID)
                            for kd in range(KD):
                                last = mm3(bank[f][:, :], [w1g[:, a, kd, f * P:f * P + P] for a in range(2)],
                                           [xT[:, a, kd, g * L:g * L + L] for a in range(2)], kd == 0, kd == KD - 1)
                            last.then_inc(up_done, 1)
                    pe.wait_ge(w2_lo, w + 1 + CR_ONE)
                    for g in range(2):
                        pe.wait_ge(hid_lo, 8 * w + 4 * g + FT + CR_TWO)
                        for t in range(TT):
                            pe.wait_ge(evac_done, 8 * w + 4 * g + t - 4 + 1 + CR_EV)
                            for f in range(FT):
                                last = mm3(bank[4 + t][:, :], [hT[:, a, g, f, t * P:t * P + P] for a in range(2)],
                                           [w2g[:, a, f, :] for a in range(2)], f == 0, f == FT - 1)
                            last.then_inc(down_done, 1)
        end_phase(pe, 4)

        def turn_y(b, et, bk, back):
            pe.wait_ge(g_gated, b + 1 + CR_ONE)
            pe.wait_ge(g_added, ET * b + et - back + 1 + CR_BANK)
            turn(bank[bk], st[:, 1, et, :], g_turned)

        def turn_x(b, t, bk, back):
            pe.wait_ge(g_norm, 2 * b + 2)
            pe.wait_ge(g_xT, TT * b + t - back + 1 + CR_BANK)
            turn(bank[bk], st[:, 0, t, :], g_xturned)

        with pe.Fori(0, HB) as b:
            for et in range(ET):
                turn_y(b, et, et, 4)
            for t in range(TT):
                turn_x(b, t, 4 + t, 4)
        end_phase(pe, 5)

        for hf in range(2):
            pe.wait_ge(g_xT, HTILES * (hf + 1) + CR_BANK)
            with pe.Fori(0, NG // 2) as q:
                for s in range(2):
                    w = NG * hf + 2 * q + s
                    pe.wait_ge(cw_lo, w + 1 + CR_ONE)
                    for g in range(2):
                        for f in range(FT):
                            n = FT * g + f
                            pe.wait_ge(c_full, 8 * w + n - 2 + 1 + CR_TWO)
                            for m, wt in enumerate((w1g, w3g)):
                                for kd in range(KD):
                                    o = hf * HTOK + g * L
                                    last = mm3(bank[2 * m + f % 2][:, :], [wt[:, a, kd, f * P:f * P + P] for a in range(2)],
                                               [xT1[:, a, kd, o:o + L] for a in range(2)], kd == 0, kd == KD - 1)
                            last.then_inc(c_up, 1)
                            if hf == 0 and s == 0 and n >= G_Y:
                                turn_y(HB + q, n - G_Y, G_BANK, 1)
                            if hf == 0 and s == 1 and n >= G_X:
                                turn_x(HB + q, n - G_X, G_BANK, 1)
                    pe.wait_ge(cw2_in, 32 * w + 32)
                    for g in range(2):
                        pe.wait_ge(c_lo, 8 * w + 4 * g + FT + CR_TWO)
                        for t in range(TT):
                            n = TT * g + t
                            pe.wait_ge(c_evac, 8 * w + n - (3 if n >= 2 else 2) + 1 + CR_EV)
                            for f in range(FT):
                                last = mm3(bank[4 + n % 3][:, :], [hT[:, a, g, f, t * P:t * P + P] for a in range(2)],
                                           [w2g[:, a, f, :] for a in range(2)], f == 0, f == FT - 1)
                            last.then_inc(c_down, 1)

    @block.scalar
    def _(act):
        A = nc.scalar.activation
        own = Chain(act, act_own)
        act.wait_ge(dma_par, 16 * 6)
        A(gates[:, :], gates[:, :], ACT.Tanh).then_inc(gates_ready, 1)
        for l in range(2):
            own.link(A(negA[l][:, :, :], par[l][:, :, P_AL:], ACT.Exp))
            own.step(A(negA[l][:, :, :], negA[l][:, :, :], ACT.Copy, scale=-1.0))
        act.wait_ge(consts_ready, 1)

        def std(stats, done, n):
            act.wait_ge(stats, n)
            A(rstd[:, :], mv[:, :, 1], ACT.Sqrt, bias=epsc[:, 0:1]).then_inc(done, 1)

        def last_taps(b):
            for et in range(ET):
                act.wait_ge(xin[0], ET * b + et + 1)
                A(u_of(b, et), bank[et][:, :], ACT.Identity, bias=par[0][:, et, P_CB:P_CB + 1],
                  scale=par[0][:, et, P_W + TAPS - 1:P_W + TAPS]).then_inc(tap_last[0], 1)

        def silu_u(b):
            for et in range(ET):
                act.wait_ge(conv[0], ET * b + et + 1 + CR_BANK)
                hold(act)
                A(u_of(b, et), u_of(b, et), ACT.Silu).then_inc(u_ready[0], 1)

        def silu_z(b):
            act.wait_ge(ln_done, b + 1)
            A(flat(zg), flat(zg), ACT.Silu).then_inc(z_ready, 1)

        def copy_xd(b):
            act.wait_ge(xdbl[0], b + 1)
            act.wait_ge(xd_out[0], 16 * b + CR_ONE)
            A(xd[0:48, :], bank[4][0:48, :], ACT.Copy).then_inc(xd_ready[0], 1)

        def softplus(b):
            act.wait_ge(prep_ready[0], b + CR_ONE)
            for et in range(ET):
                act.wait_ge(dtraw[0], ET * b + et + 1)
                A(r4[:, et, :], bank[4 + et][:, :], ACT.Relu, bias=par[0][:, et, P_DB:P_DB + 1])
                ab = A(e4[:, et, :], bank[4 + et][:, :], ACT.Abs, bias=par[0][:, et, P_DB:P_DB + 1])
            own.link(ab)
            own.link(A(e4, e4, ACT.Exp, scale=-1.0))
            act.wait_ge(dd_out, 32 * b + CR_ONE)
            A(l4, e4, ACT.Ln, bias=onec[:, 0:1]).then_inc(soft[0], 1)

        last_taps(0)
        silu_u(0)
        with act.Fori(0, NB - 1) as b:
            own.enter(b, 2)
            copy_xd(b)
            std(ln_stats, ln_std, b + 1)
            act.wait_ge(u_out[0], 16 * b + CR_ONE)
            act.wait_ge(prep_ready[0], b + CR_ONE)
            last_taps(b + 1)
            softplus(b)
            silu_u(b + 1)
            silu_z(b)
            own.leave(2, NB - 1)

        def hadamard_hi(tiles):
            for h in tiles:
                act.wait_ge(had_mm, h + 1)
                A(w2s[h // 4][:, h % 4, 0], bank[h % 4][:, :], ACT.Copy, scale=N_SCALE).then_inc(had_hi, 1)

        copy_xd(NB - 1)
        std(ln_stats, ln_std, NB)
        hadamard_hi(range(HAD_FIRST))
        softplus(NB - 1)
        silu_z(NB - 1)
        hadamard_hi(range(HAD_FIRST, HAD_TILES))
        end_phase(act, 1)

        def exp_chunk(slot, delta, l, et, c):
            for n in range(CH):
                last = A(dA[:, slot, n, 1:], delta, ACT.Exp, scale=negA[l][:, et, CH * c + n:CH * c + n + 1])
            return last

        def exps0(b, et, c):
            if c == 0:
                act.wait_ge(pt_in[0][et % 2], 16 * (2 * b + et // 2) + 16)
            act.wait_ge(a_scan, NC * (ET * b + et) + c - 2 + 1 + CR_TWO)
            exp_chunk(c % 2, pt[:, et % 2, 1, 1:], 0, et, c).then_inc(a_exp, 1)

        def exps(b, et, c):
            s, m = c % 2, 8 * b + 2 * et + c // 2
            if c == 0:
                act.wait_ge(pt_in[1][et % 2], 16 * (2 * b + et // 2) + 16)
            act.wait_ge(dA_free[s], m + CR_ONE)
            exp_chunk(s, pt[:, et % 2, 1, 1:], 1, et, c).then_inc(dA_ready[s], 1)

        def last_taps1(b):
            act.wait_ge(u_out[1], 16 * b + CR_ONE)
            act.wait_ge(prep_ready[1], 2 * b + CR_TWO)
            for et in range(ET):
                act.wait_ge(xin[1], ET * b + et + 1)
                A(u1[:, et, :], bank[4 + et][:, :], ACT.Identity, bias=par[1][:, et, P_CB:P_CB + 1],
                  scale=par[1][:, et, P_W + TAPS - 1:P_W + TAPS]).then_inc(tap_last[1], 1)

        def silu1(b):
            for et in range(ET):
                act.wait_ge(conv[1], ET * b + et + 1 + CR_BANK)
                A(u1[:, et, :], u1[:, et, :], ACT.Silu).then_inc(u_ready[1], 1)

        def soft1(b, h):
            act.wait_ge(prep_ready[1], 2 * b + h + CR_TWO)
            act.wait_ge(dd1_out[h], 32 * b + CR_ONE)
            for s in range(2):
                et = 2 * h + s
                act.wait_ge(dtraw[1], ET * b + et + 1)
                A(r1[:, s, :], bank[4 + et][:, :], ACT.Relu, bias=par[1][:, et, P_DB:P_DB + 1])
                ab = A(e1[:, h, s, :], bank[4 + et][:, :], ACT.Abs, bias=par[1][:, et, P_DB:P_DB + 1])
            own.link(ab)
            own.link(A(flat(e1[:, h]), flat(e1[:, h]), ACT.Exp, scale=-1.0))
            A(flat(l1[:, h]), flat(e1[:, h]), ACT.Ln, bias=onec[:, 0:1]).then_inc(soft[1], 1)

        act.wait_ge(dA_zero, 1)
        with act.Fori(0, NB) as b:
            own.enter(b, 4)
            for et in range(ET):
                exps0(b, et, 0)
                if et == 1:
                    silu1(b)
                if et == 2:
                    act.wait_ge(xdbl[1], b + 1)
                    act.wait_ge(xd_out[1], 16 * b + CR_ONE)
                    A(xd[0:48, :], bank[4][0:48, :], ACT.Copy).then_inc(xd_ready[1], 1)
                exps0(b, et, 1)
                if et == 3:
                    soft1(b, 1)
                exps0(b, et, 2)
                if et == 0:
                    last_taps1(b)
                if et == 2:
                    soft1(b, 0)
                exps0(b, et, 3)
            act.wait_ge(prep_ready[1], 2 * b + 2 + CR_TWO)
            for a, part in enumerate((l1[:, 1], e1[:, 1])):
                act.dma_start(d["prep1"][bass.ds(b, 1), 1 + a, 2:4].rearrange("o e p t -> p (o e) t"), part).then_inc(dd1_out[1], 16)
            own.leave(4, NB)
        end_phase(act, 2)

        std(ln_stats, ln_std, NB + 1)
        for g in range(NB):
            if g < NB - 1:
                std(ln_stats, ln_std, NB + g + 2)
            for t in range(TT * g, TT * g + TT):
                act.wait_ge(xn_turned, t + 1)
                o = (t % HTILES) * P
                turned = bank[2 + t % 4][:, :].rearrange("p (k t) -> p k t", k=KD)
                A(xTh[t // HTILES][:, 0, :, o:o + P], turned, ACT.Copy).then_inc(xT_hi, 1)
                if t >= 4:
                    act.wait_ge(logit_mm, t - 3)
                A(xTf[:, t % 4], turned, ACT.Copy).then_inc(xT_f32, 1)
        act.wait_ge(rt_in, 1)
        A(lexp[:, :, :], lsel[:, :, :], ACT.Exp).then_inc(rt_exp, 1)
        end_phase(act, 3)

        def gelu(w, k, g, f):
            n = 8 * w + 4 * g + f
            act.wait_ge(up_done, n + 1 + CR_UP)
            act.wait_ge(hid_lo, n - 2 + 1 + CR_TWO)
            A(h32[:, f % 2], bank[f][:, :], ACT.Gelu_apprx_tanh, bias=b1s[:, k * FT + f:k * FT + f + 1], scale=1 / (S_X * S_W)).then_inc(h_full, 1)
            if f == 0:
                act.wait_ge(down_done, 8 * w + 4 * g + 4 - 8 + CR_DOWN)
            act.wait_ge(h_full, n + 1 + CR_HID)
            A(hT[:, 0, g, f, :], h32[:, f % 2], ACT.Copy, scale=S_H).then_inc(hid_hi, 1)

        def split_hi(arrived, n, dst, src, used, n_used, done):
            act.wait_ge(arrived, n)
            act.wait_ge(used, n_used)
            A(dst.rearrange("p k f -> p (k f)"), src.rearrange("p k f -> p (k f)"), ACT.Copy, scale=S_W).then_inc(done, 1)

        split_hi(w1_in, 16, w1g[:, 0], stage, up_done, CR_UP, w1_hi)
        with act.Fori(0, 2) as hf:
            with act.Fori(0, 2) as i:
                j = 2 * hf + i
                for k in range(NG):
                    w = 4 * j + k
                    exps(j, k, 0)
                    exps(j, k, 1)
                    split_hi(w2_in, 16 * w + 16, w2g[:, 0], stage, down_done, 8 * w + CR_DOWN, w2_hi)
                    if k == 0:
                        act.wait_ge(b1_in, 16 * j + 16)
                        act.wait_ge(b2_used, j + 1 + CR_ONE)
                    for g in range(2):
                        for f in range(FT):
                            gelu(w, k, g, f)
                    split_hi(w1_in, 16 * w + 32, w1g[:, 0], stage, up_done, 8 * w + 8 + CR_UP, w1_hi)
                    exps(j, k, 2)
                    exps(j, k, 3)
        end_phase(act, 4)

        def gate_silu(b):
            std(g_stats, g_std, 2 * b + 1)
            act.wait_ge(g_norm, 2 * b + 1)
            A(flat(st[:, 1]), flat(st[:, 1]), ACT.Silu).then_inc(g_z, 1)

        def hi_x(b, t, bk):
            act.wait_ge(g_xturned, TT * b + t + 1)
            A(xT1[:, 0, :, bass.ds(b * L + t * P, P)], bank[bk][:, :].rearrange("p (k t) -> p k t", k=KD), ACT.Copy).then_inc(g_xhi, 1)

        def hi_weights(w):
            act.wait_ge(cw_in, 32 * w + 32)
            act.wait_ge(c_up, 8 * w + CR_UP)
            A(w1g[:, 0].rearrange("p k f -> p (k f)"), stage.rearrange("p k f -> p (k f)"), ACT.Copy, scale=S_W)
            A(w3g[:, 0].rearrange("p k f -> p (k f)"), stage3.rearrange("p k f -> p (k f)"), ACT.Copy, scale=S_W).then_inc(cw_hi, 1)

        for b in range(HB):
            gate_silu(b)
            std(g_stats, g_std, 2 * b + 2)
            for t in range(TT):
                hi_x(b, t, 4 + t)
            if b == 0:
                hi_weights(0)
        end_phase(act, 5)

        for hf in range(2):
            with act.Fori(0, NG // 2) as q:
                for s in range(2):
                    w = NG * hf + 2 * q + s
                    for g in range(2):
                        for f in range(FT):
                            k = FT * g + f
                            n = 8 * w + k
                            act.wait_ge(c_up, n + 1 + CR_UP)
                            act.wait_ge(c_full, n - 2 + 1 + CR_TWO)
                            A(sg[:, f % 2, :], bank[f % 2][:, :], ACT.Silu, scale=1 / (S_X * S_W)).then_inc(c_sg, 1)
                            if f == 0:
                                act.wait_ge(c_down, 8 * w + 4 * g + 4 - 8 + CR_DOWN)
                            act.wait_ge(c_full, n + 1 + CR_TWO)
                            A(hT[:, 0, g, f, :], h32[:, f % 2], ACT.Copy).then_inc(c_hi, 1)
                            if hf == 0 and s == 0 and k == 1:
                                gate_silu(HB + q)
                            if hf == 0 and s == 1 and k == 1:
                                std(g_stats, g_std, 2 * (HB + q) + 2)
                            if hf == 0 and s == 1 and k >= G_X:
                                hi_x(HB + q, k - G_X, G_BANK)
                    hi_weights(w + 1)

    @block.vector
    def _(dve):
        V = nc.vector
        own = Chain(dve, dve_own)
        V.memset(yt[:, :, :], 0.0)
        V.memset(onec[:, :], 1.0)
        V.memset(epsc[:, :], EPS).then_inc(consts_ready, 1)
        dve.wait_ge(dma_par, 16 * 6)

        def norm(tile_ap, dst, stats, std_done, done, n, scale=1.0):
            for t in range(TT):
                ins = V.bn_stats(bnst[:, t, :], tile_ap(t))
            own.link(ins)
            hold(dve)
            for t in range(TT):
                ins = V.bn_aggr(mv[:, t, :], bnst[:, t, :])
            ins.then_inc(stats, 1)
            dve.wait_ge(std_done, n)
            own.link(V.reciprocal(rstd[:, :], rstd[:, :]))
            if scale != 1.0:
                own.link(V.tensor_scalar(rstd[:, :], rstd[:, :], scale, None, ALU.mult))
            for t in range(TT):
                ins = V.tensor_scalar(dst(t), tile_ap(t), mv[:, t, 0:1], rstd[:, t:t + 1], ALU.subtract, ALU.mult)
            ins.then_inc(done, 1)

        def taps(u, l, first, done):
            for tap in range(1, TAPS):
                for et in range(ET):
                    if tap == 1:
                        dve.wait_ge(tap_last[l], first + et + 1)
                    o = u(et, tap)
                    ins = V.scalar_tensor_tensor(out=o, in0=bank[4 * l + et][:, 0:L - tap], scalar=par[l][:, et, P_W + TAPS - 1 - tap:P_W + TAPS - tap],
                                                 in1=o, op0=ALU.mult, op1=ALU.add)
                    if tap == TAPS - 1:
                        ins.then_inc(done, 1)
                if tap < TAPS - 1:
                    own.link(ins)

        def convolve(b):
            taps(lambda et, tap: u4[:, bass.ds(b % 2, 1), et, tap:].rearrange("p o t -> p (o t)"), 0, ET * b, conv[0])

        def delta(ef, rf, lf, qf, u, done):
            own.link(V.tensor_tensor(lf, lf, rf, ALU.add))
            own.link(V.tensor_scalar(rf, ef, 1.0, 1.0, ALU.add, ALU.subtract))
            own.link(V.tensor_tensor(rf, ef, rf, ALU.subtract))
            own.link(V.tensor_tensor(lf, lf, rf, ALU.add))
            V.tensor_tensor(qf, lf, u, ALU.mult).then_inc(done, 1)

        def delta0(b):
            dve.wait_ge(soft[0], b + 1 + CR_ONE)
            delta(flat(e4), flat(r4), flat(l4), flat(q4), u4[:, bass.ds(b % 2, 1)].rearrange("p o e t -> p (o e t)"), prep_ready[0])

        def delta1(b, h):
            dve.wait_ge(soft[1], 2 * b + h + 1 + CR_TWO)
            delta(*(flat(x) for x in (e1[:, h], r1, l1[:, h], e1[:, h])), flat(u1[:, 2 * h:2 * h + 2, :]), prep_ready[1])

        def norm_z(b):
            dve.wait_ge(z_out, 16 * b + CR_ONE)
            hold(dve)
            norm(lambda t: tile_of(TT * b + t), lambda t: zg[:, t, :], ln_stats, ln_std, ln_done, b + 1)

        convolve(0)
        dve.wait_ge(dma_x, 16)
        with dve.Fori(0, NB - 1) as b:
            own.enter(b, 8)
            norm_z(b)
            convolve(b + 1)
            delta0(b)
            own.leave(8, NB - 1)

        def hadamard_lo(tiles):
            for h in tiles:
                dve.wait_ge(had_hi, h + 1)
                V.scalar_tensor_tensor(out=w2s[h // 4][:, h % 4, 1], in0=bank[h % 4][:, :], scalar=N_SCALE, in1=w2s[h // 4][:, h % 4, 0],
                                       op0=ALU.mult, op1=ALU.subtract).then_inc(had_lo, 1)

        norm_z(NB - 1)
        hadamard_lo(range(HAD_FIRST))
        delta0(NB - 1)
        hadamard_lo(range(HAD_FIRST, HAD_TILES))
        end_phase(dve, 1)

        def scan0(b, et, c):
            n = NC * (ET * b + et) + c
            dve.wait_ge(a_exp, n + 1 + CR_RING)
            dve.wait_ge(a_bx, n + 1 + CR_RING)
            V.tensor_tensor_scan(flat(stA(c)), flat(dA[:, c % 2]), flat(stA(c)), 0.0, ALU.mult, ALU.add).then_inc(a_scan, 1)
            if et == 0:
                dve.wait_ge(a_c_in[c], 16 * b + 16)
            dve.wait_ge(a_scan, n + 1 + CR_TWO)
            V.tensor_tensor(stA(c), stA(c), bc[:, 1, CH * c:CH * c + CH, :], ALU.mult).then_inc(a_p, 1)

        def scan(b, et, c):
            s, m = c % 2, 8 * b + 2 * et + c // 2
            dve.wait_ge(dA_ready[s], m + 1)
            dve.wait_ge(bx_ready[s], m + 1)
            V.tensor_tensor_scan(flat(st[:, s]), flat(dA[:, s]), flat(st[:, s]), 0.0, ALU.mult, ALU.add).then_inc(dA_free[s], 1)

        def times_c(b, et, c):
            s, m = c % 2, 8 * b + 2 * et + c // 2
            dve.wait_ge(dA_free[s], m + 1 + CR_ONE)
            V.tensor_tensor(st[:, s], st[:, s], bc[:, 1, CH * c:CH * c + CH, :], ALU.mult).then_inc(p_ready[s], 1)

        dve.wait_ge(gates_ready, 1)

        def gate_unit(b, et):
            s, u = et % 2, ET * b + et
            dve.wait_ge(uz_in[s], 32 * (2 * b + et // 2) + 32)
            dve.wait_ge(a_summed, NC * u + NC + CR_RING)
            V.scalar_tensor_tensor(out=yt[:, s, :], in0=pt[:, s, 0, :], scalar=par[0][:, et, P_D:P_D + 1], in1=bank[s][:, :],
                                   op0=ALU.mult, op1=ALU.add).then_inc(unit_done, 1)
            dve.wait_ge(unit_done, u + 1 + CR_TWO)
            V.tensor_tensor(yt[:, s, :], yt[:, s, :], zt[:, s, :], ALU.mult).then_inc(y_gated, 1)

        def add_unit(b, et):
            dve.wait_ge(y_turned, ET * b + et + 1)
            xs = x_sb[:, bass.ds(TT * b, TT), et * P:et * P + P]
            V.scalar_tensor_tensor(out=xs, in0=bank[2 + et % 2][:, :].rearrange("p (t e) -> p t e", t=TT), scalar=gates[:, 0:1],
                                   in1=xs, op0=ALU.mult, op1=ALU.add).then_inc(y_added, 1)

        def scan_batch(b, first):
            for et in range(ET):
                before = (b, et - 1) if et else (b - 1, ET - 1)
                scan0(b, et, 0)
                scan0(b, et, 1)
                if et or not first:
                    gate_unit(*before)
                if et == 3:
                    delta1(b, 1)
                scan0(b, et, 2)
                if et == 0:
                    taps(lambda et, tap: u1[:, et, tap:], 1, ET * b, conv[1])
                if et or not first:
                    add_unit(*before)
                scan0(b, et, 3)
                if et == 2:
                    delta1(b, 0)

        own.enter(0, 2 + 2 * 4)
        scan_batch(0, True)
        own.leave(2 + 2 * 4, 1)
        with dve.Fori(0, NB - 1) as b:
            own.enter(b, 2 + 2 * 4)
            scan_batch(b + 1, False)
            own.leave(2 + 2 * 4, NB - 1)
        gate_unit(NB - 1, ET - 1)
        add_unit(NB - 1, ET - 1)
        end_phase(dve, 2)
        V.memset(ones, 1.0)

        def norm_turn(g):
            if g >= 2:
                dve.wait_ge(xn_turned, TT * (g - 1))
            norm(lambda t: x_sb[:, TT * g + t, :], lambda t: st[:, g % 2, t, :], ln_stats, ln_std, ln_done, NB + g + 1, S_X)

        norm_turn(0)
        for g in range(NB):
            if g < NB - 1:
                norm_turn(g + 1)
            for t in range(TT * g, TT * g + TT):
                o = (t % HTILES) * P
                dve.wait_ge(xT_hi, t + 1)
                dve.wait_ge(xT_f32, t + 1)
                half_of = xTh[t // HTILES]
                V.tensor_tensor(half_of[:, 1, :, o:o + P], bank[2 + t % 4][:, :].rearrange("p (k t) -> p k t", k=KD), half_of[:, 0, :, o:o + P],
                                ALU.subtract).then_inc(xT_ready, 1)
        dve.wait_ge(logit_mm, TILES)
        own.link(V.tensor_scalar(logit[:, :, :], bank[6][:, 0:TILES * E].rearrange("p (t e) -> p t e", e=E), 1 / S_X, None, ALU.mult))
        V.tensor_reduce(out=lsum[:, :], in_=logit[:, :, :].rearrange("p t e -> p e t"), axis=AX.X, op=ALU.add).then_inc(lsum_in, 1)
        dve.wait_ge(lsum_mm, 1)
        own.link(V.tensor_copy(lsum[:, :], bank[7][:, 0:E]))
        own.link(V.max(top[:, :], lsum[:, :]))
        V.max_index(topi[:, :], top[:, :], lsum[:, :]).then_inc(sel_ready, 1)
        dve.wait_ge(sel_ready, 1)
        own.link(V.tensor_copy(topf[:, :], topi[:, :]))
        for k in range(2):
            ins = V.tensor_scalar(hot[:, k, :], iota[:, :], topf[:, k:k + 1], None, ALU.is_equal)
        own.link(ins)
        for k in range(2):
            own.link(V.tensor_tensor(lwork[:, :, :], logit[:, :, :], hot[:, k:k + 1, :].to_broadcast([P, TILES, E]), ALU.mult))
            own.link(V.tensor_reduce(out=lsel[:, k, :], in_=lwork[:, :, :], axis=AX.X, op=ALU.add))
        own.link(V.tensor_tensor(lmax[:, :], lsel[:, 0, :], lsel[:, 1, :], ALU.max))
        for k in range(2):
            ins = V.tensor_tensor(lsel[:, k, :], lsel[:, k, :], lmax[:, :], ALU.subtract)
        ins.then_inc(rt_in, 1)
        dve.wait_ge(rt_exp, 1)
        own.link(V.tensor_tensor(lmax[:, :], lexp[:, 0, :], lexp[:, 1, :], ALU.add))
        own.link(V.reciprocal(lmax[:, :], lmax[:, :]))
        for k in range(2):
            ins = V.tensor_tensor(lexp[:, k, :], lexp[:, k, :], lmax[:, :], ALU.mult)
        own.link(ins)
        for k in range(2):
            own.link(V.tensor_scalar(cbias[:, :, k, :], lexp[:, k, :].rearrange("p (h t) -> p h t", h=2), gates[:, 2:3], None, ALU.mult))
            ins = V.tensor_scalar(coef[:, :, k, :], cbias[:, :, k, :], 1 / (S_H * S_W), None, ALU.mult)
        V.tensor_scalar(down1[:, :], gates[:, 3:4], 1 / (S_H * S_W), None, ALU.mult)
        end_phase(dve, 3)

        def b_times(b, et, c):
            s, m = c % 2, 8 * b + 2 * et + c // 2
            if c == 0:
                dve.wait_ge(pt_in[1][et % 2], 16 * (2 * b + et // 2) + 16)
            if et == 0:
                dve.wait_ge(bc_in[c], 32 * b + 32)
            dve.wait_ge(st_free[s], m + CR_ST)
            V.tensor_tensor(st[:, s], pt[:, et % 2, 2:3, :].to_broadcast([P, CH, L]), bc[:, 0, CH * c:CH * c + CH, :],
                            ALU.mult).then_inc(bx_ready[s], 1)

        def lo_weights(hi, n, dst, done):
            dve.wait_ge(hi, n)
            f2 = lambda ap: ap.rearrange("p k f -> p (k f)")
            V.scalar_tensor_tensor(out=f2(dst[:, 1]), in0=f2(stage), scalar=S_W, in1=f2(dst[:, 0]),
                                   op0=ALU.mult, op1=ALU.subtract).then_inc(done, 1)

        lo_weights(w1_hi, 1, w1g, w1_lo)
        with dve.Fori(0, 2) as hf:
            with dve.Fori(0, 2) as i:
                j = 2 * hf + i

                def cf(t, src=coef):
                    return src[:, bass.ds(hf, 1), bass.ds(i, 1), t].rearrange("p a b -> p (a b)")

                def lo_hidden(w, g, f):
                    dve.wait_ge(hid_hi, 8 * w + 4 * g + f + 1)
                    V.scalar_tensor_tensor(out=hT[:, 1, g, f, :], in0=h32[:, f % 2], scalar=S_H, in1=hT[:, 0, g, f, :],
                                           op0=ALU.mult, op1=ALU.subtract).then_inc(hid_lo, 1)

                def evac(w, t):
                    dve.wait_ge(down_done, 8 * w + t + 1 + CR_DOWN)
                    dve.wait_ge(evac_done, 8 * w + t + 1 - 8 + CR_EV)
                    xt = tile_of(HTILES * hf + t)
                    V.scalar_tensor_tensor(out=xt, in0=bank[4 + t % 4][:, :], scalar=cf(t), in1=xt, op0=ALU.mult, op1=ALU.add).then_inc(evac_done, 1)

                dve.wait_ge(b2_in, 16 * j + 16)
                dve.wait_ge(evac_done, 32 * j + CR_EV)
                for t in range(HTILES):
                    xt = tile_of(HTILES * hf + t)
                    ins = V.scalar_tensor_tensor(out=xt, in0=b2b, scalar=cf(t, cbias), in1=xt, op0=ALU.mult, op1=ALU.add)
                ins.then_inc(b2_used, 1)
                dve.wait_ge(b2_used, j + 1 + CR_ONE)
                for k in range(NG):
                    w = 4 * j + k
                    b_times(j, k, 0)
                    scan(j, k, 0)
                    lo_hidden(w, 0, 0)
                    times_c(j, k, 0)
                    lo_hidden(w, 0, 1)
                    lo_weights(w2_hi, w + 1, w2g, w2_lo)
                    lo_hidden(w, 0, 2)
                    b_times(j, k, 1)
                    lo_hidden(w, 0, 3)
                    scan(j, k, 1)
                    lo_hidden(w, 1, 0)
                    times_c(j, k, 1)
                    lo_hidden(w, 1, 1)
                    lo_hidden(w, 1, 2)
                    lo_hidden(w, 1, 3)
                    evac(w, 0)
                    lo_weights(w1_hi, w + 2, w1g, w1_lo)
                    evac(w, 1)
                    b_times(j, k, 2)
                    evac(w, 2)
                    scan(j, k, 2)
                    evac(w, 3)
                    times_c(j, k, 2)
                    evac(w, 4)
                    b_times(j, k, 3)
                    evac(w, 5)
                    scan(j, k, 3)
                    evac(w, 6)
                    times_c(j, k, 3)
                    evac(w, 7)
        end_phase(dve, 4)

        def gate_norm(b):
            norm(lambda t: tile_of(TT * b + t), lambda t: st[:, 1, t, :], g_stats, g_std, g_norm, 2 * b + 1)

        def gate_y(b):
            dve.wait_ge(g_z, b + 1)
            dve.wait_ge(y1_in, 16 * b + 16)
            V.tensor_tensor(flat(st[:, 1]), flat(st[:, 1]), y1b.rearrange("p e t -> p (e t)"), ALU.mult).then_inc(g_gated, 1)

        def add_y(b, et, bk):
            dve.wait_ge(g_turned, ET * b + et + 1)
            xs = x_sb[:, bass.ds(TT * b, TT), et * P:et * P + P]
            V.scalar_tensor_tensor(out=xs, in0=bank[bk][:, :].rearrange("p (t e) -> p t e", t=TT), scalar=gates[:, 1:2],
                                   in1=xs, op0=ALU.mult, op1=ALU.add).then_inc(g_added, 1)

        def x_norm(b):
            dve.wait_ge(g_added, ET * b + ET + CR_BANK)
            dve.wait_ge(g_xT, TT * b + CR_BANK)
            hold(dve)
            norm(lambda t: tile_of(TT * b + t), lambda t: st[:, 0, t, :], g_stats, g_std, g_norm, 2 * b + 2, S_X)

        def lo_x(b, t, bk):
            dve.wait_ge(g_xhi, TT * b + t + 1)
            o = bass.ds(b * L + t * P, P)
            V.tensor_tensor(xT1[:, 1, :, o], bank[bk][:, :].rearrange("p (k t) -> p k t", k=KD), xT1[:, 0, :, o],
                            ALU.subtract).then_inc(g_xT, 1)

        def lo_in_weights(w):
            f2 = lambda ap: ap.rearrange("p k f -> p (k f)")
            dve.wait_ge(cw_hi, w + 1)
            for part, src in ((w1g, stage), (w3g, stage3)):
                ins = V.scalar_tensor_tensor(out=f2(part[:, 1]), in0=f2(src), scalar=S_W, in1=f2(part[:, 0]),
                                             op0=ALU.mult, op1=ALU.subtract)
            ins.then_inc(cw_lo, 1)

        for b in range(HB):
            gate_norm(b)
            if b:
                lo_in_weights(0)
            gate_y(b)
            for et in range(ET):
                add_y(b, et, et)
            x_norm(b)
            for t in range(TT):
                lo_x(b, t, 4 + t)
        end_phase(dve, 5)

        for hf in range(2):
            with dve.Fori(0, NG // 2) as q:
                if hf == 0:
                    own.enter(q, 5)
                for s in range(2):
                    w = NG * hf + 2 * q + s
                    for g in range(2):
                        for f in range(FT):
                            k = FT * g + f
                            n = 8 * w + k
                            dve.wait_ge(c_sg, n + 1)
                            dve.wait_ge(c_lo, n - 2 + 1 + CR_TWO)
                            V.scalar_tensor_tensor(out=h32[:, f % 2], in0=bank[2 + f % 2][:, :], scalar=S_H / (S_X * S_W), in1=sg[:, f % 2, :],
                                                   op0=ALU.mult, op1=ALU.mult).then_inc(c_full, 1)
                            dve.wait_ge(c_hi, n + 1)
                            V.tensor_tensor(hT[:, 1, g, f, :], h32[:, f % 2], hT[:, 0, g, f, :], ALU.subtract).then_inc(c_lo, 1)
                            if hf == 0 and s == 0:
                                if k == 1:
                                    gate_norm(HB + q)
                                if k == 2:
                                    gate_y(HB + q)
                                if k >= G_Y:
                                    add_y(HB + q, k - G_Y, G_BANK)
                            if hf == 0 and s == 1:
                                if k == 1:
                                    x_norm(HB + q)
                                if k >= G_X:
                                    lo_x(HB + q, k - G_X, G_BANK)
                    for t in range(HTILES):
                        if t == 2:
                            lo_in_weights(w + 1)
                        dve.wait_ge(c_down, 8 * w + t + 1 + CR_DOWN)
                        dve.wait_ge(c_evac, 8 * w + t + 1 - 8 + CR_EV)
                        xt = x_sb[:, HTILES * hf + t, :]
                        V.scalar_tensor_tensor(out=xt, in0=bank[4 + t % 3][:, :], scalar=down1[:, 0:1], in1=xt, op0=ALU.mult, op1=ALU.add).then_inc(c_evac, 1)
                if hf == 0:
                    own.leave(5, NG // 2)

    @block.gpsimd
    def _(gp):
        G = nc.gpsimd
        own = Chain(gp, pool_own)
        gp.wait_ge(dma_had, 32)
        src, dst = wv, wz
        for s in range(4):
            a = src.rearrange("p (h two l) d -> p two h (l d)", two=2, l=2 ** s)
            o = dst.rearrange("p (h two l) d -> p two h (l d)", two=2, l=2 ** s)
            G.tensor_tensor(o[:, 0], a[:, 0], a[:, 1], ALU.add)
            last = G.tensor_tensor(o[:, 1], a[:, 0], a[:, 1], ALU.subtract)
            if s < 3:
                own.link(last)
            src, dst = dst, src
        last.then_inc(butterfly, 1)
        end_phase(gp, 1)

        G.memset(dA[:, :, :, 0:1], 0.0).then_inc(dA_zero, 1)
        with gp.Fori(0, NB) as b:
            for et in range(ET):
                gp.wait_ge(pt_in[0][et % 2], 16 * (2 * b + et // 2) + 16)
                for c in range(NC):
                    if et == 0:
                        gp.wait_ge(a_b_in[c], 16 * b + 16)
                    gp.wait_ge(a_summed, NC * (ET * b + et) + c - NC + 1 + CR_RING)
                    G.tensor_tensor(stA(c), pt[:, et % 2, 2:3, :].to_broadcast([P, CH, L]), bc[:, 0, CH * c:CH * c + CH, :],
                                    ALU.mult).then_inc(a_bx, 1)
        end_phase(gp, 2)
        end_phase(gp, 3)

        with gp.Fori(0, 2) as hf:
            with gp.Fori(0, 2) as i:
                j = 2 * hf + i
                own.enter(j, ET * (1 + 2 * NC))
                for et in range(ET):
                    s2 = et % 2
                    gp.wait_ge(pt_in[1][s2], 16 * (2 * j + et // 2) + 16)
                    gp.wait_ge(y1_out[s2], 16 * (2 * j + et // 2 + s2) + CR_ONE)
                    hold(gp)
                    own.link(G.tensor_scalar(yt[:, s2, :], pt[:, s2, 0, :], par[1][:, et, P_D:P_D + 1], None, ALU.mult))
                    for c in range(NC):
                        s, m = c % 2, 8 * j + 2 * et + c // 2
                        gp.wait_ge(p_ready[s], m + 1 + CR_TWO)
                        own.link(G.tensor_tensor(st[:, s, 0:2], st[:, s, 0:2], st[:, s, 2:4], ALU.add))
                        own.link(G.tensor_tensor(st[:, s, 0], st[:, s, 0], st[:, s, 1], ALU.add))
                        G.tensor_tensor(yt[:, s2, :], yt[:, s2, :], st[:, s, 0], ALU.add).then_inc(st_free[s], 1)
                        gp.wait_ge(st_free[s], m + 1 + CR_ST)
                own.leave(ET * (1 + 2 * NC), 4)
        end_phase(gp, 4)
        end_phase(gp, 5)

    ctx.close()


def kernel(**a):
    import concourse.bacc as bacc
    from concourse.bass_utils import run_bass_kernel_spmd

    n = lambda name: np.asarray(a[name])
    had = np.array([[1.0]], np.float32)
    while had.shape[0] < P:
        had = np.block([[had, had], [had, -had]]).astype(np.float32)
    host = {
        "x": n("x").reshape(NB * L, DM),
        "ctxT": n("ctx_1024").reshape(NB * L, DC).T,
        "gates": np.concatenate([n("g_xattn"), n("g_ffn")])[None, :],
        "ident": np.eye(P, dtype=np.float32),
        "had": had,
        "iota": np.arange(E, dtype=np.float32)[None, :],
        "gwT": n("L0_ffn_gate_w").T,
        "w1": n("L0_ffn_w1"),
        "b1": n("L0_ffn_b1").reshape(E, F // P, P).transpose(0, 2, 1),
        "w2": n("L0_ffn_w2"),
        "b2": n("L0_ffn_b2"),
        "W1T": n("L1_ffn_W1").T,
        "W2T": n("L1_ffn_W2").T,
        "W3T": n("L1_ffn_W3").T,
    }
    for l in range(2):
        g = lambda name: n(f"L{l}_xattn_{name}")
        host[f"inw{l}"] = g("in_proj_w").T
        host[f"xpw{l}"] = np.concatenate([g("x_proj_w")[DR:], g("x_proj_w")[:DR]]).T
        host[f"dtw{l}"] = g("dt_proj_w").T
        cols = [g("conv_w").reshape(DI, TAPS), g("conv_b")[:, None], g("dt_proj_b")[:, None], g("D")[:, None], g("A_log")]
        host[f"par{l}"] = np.concatenate(cols, axis=1).reshape(ET, P, NPAR).transpose(1, 0, 2).reshape(P, ET * NPAR)
    nc = bacc.Bacc("TRN2", target_bir_lowering=False, num_devices=1)
    arrays = {f"in_{k}": np.ascontiguousarray(v) for k, v in host.items()}
    d = {k: nc.dram_tensor(f"in_{k}", v.shape, mybir.dt.from_np(v.dtype), kind="ExternalInput").ap() for k, v in host.items()}
    scratch = {"bc0": [NB, 2 * DS, L], "bc1": [NB, 2 * DS, L], "prep0": [NB, 3, ET, P, L], "prep1": [NB, 3, ET, P, L],
               "z": [NB, TT, P, L], "y1": [1 + NB * ET, P, L], "xT": [2, 2, DM, HTOK], "w2h": [2, F, DM]}
    for k, shape in scratch.items():
        d[k] = nc.dram_tensor(k, shape, F16 if k in ("xT", "w2h") else F32, kind="Internal").ap()
    d["sel"] = nc.dram_tensor("sel", [1, 8], U32, kind="Internal").ap()
    d["out"] = nc.dram_tensor("out_0", [NB * L, DM], F32, kind="ExternalOutput").ap()
    build(nc, d)
    r = run_bass_kernel_spmd(nc, [arrays], core_ids=[0])
    return r.results[0]["out_0"].reshape(NB, L, DM)
```
